# Optimizing a Trainium2 kernel written in Bass

```python
import numpy as np
import jax
import jax.numpy as jnp

def _softmax(x, axis=-1):
    return jax.nn.softmax(x, axis=axis)

def _gelu(x):
    return jax.nn.gelu(x, approximate=True)

def _silu(x):
    return jax.nn.silu(x)

def _sigmoid(x):
    return jax.nn.sigmoid(x)

def _layernorm(x, axis=-1, eps=1e-05):
    m = jnp.mean(x, axis=axis, keepdims=True)
    v = jnp.var(x, axis=axis, keepdims=True)
    return (x - m) / jnp.sqrt(v + eps)

def _scatter_add(tgt, idx, src, axis=0):
    return tgt.at[idx].add(src)

def _segment_sum(src, seg, n):
    return jax.ops.segment_sum(src, seg, n)
kernel_name = 'mk_decoder_postln_d2_seqx_r2_704f3f'

def setup_inputs(seed: int=0):
    np.random.seed(seed)
    _w = jnp.asarray

    def _rec_inputs():
        import jax
        import jax.numpy as jnp
        _rk = jax.random.key(seed)
        x = 7.22e-05 + 1 * jax.random.normal(jax.random.fold_in(_rk, 1), (8, 100, 512), jnp.float32)
        _lenS = 100 - jax.random.randint(jax.random.fold_in(_rk, 7), (8,), 0, max(1, 100 // 4) + 1, jnp.int32)
        _lenS2 = 722 - jax.random.randint(jax.random.fold_in(_rk, 8), (8,), 0, max(1, 722 // 4) + 1, jnp.int32)
        _ctx_768P = jax.random.normal(jax.random.fold_in(_rk, 11), (8, 16, 384), jnp.float32)
        _ctx_768c = jax.random.dirichlet(jax.random.fold_in(_rk, 511), 0.3 * jnp.ones((16,), jnp.float32), (8, 722))
        _ctx_768t = jnp.einsum('bsk,bkd->bsd', _ctx_768c, _ctx_768P)
        _ctx_768t = _ctx_768t * jax.lax.rsqrt(jnp.mean(jnp.square(_ctx_768t)) + 1e-12) * 0.953939
        ctx_768 = -0.000191848 + 0.999787 * (_ctx_768t + 0.3 * jax.random.normal(jax.random.fold_in(_rk, 611), (8, 722, 384), jnp.float32))
        return (x, ctx_768)
    x, ctx_768 = _rec_inputs()

    def _L0_attn_setup():
        import jax, jax.numpy as jnp
        import numpy as np
        B, L, D, N = (2, 1024, 512, 16)
        DT = 0.1
        key = jax.random.key(seed)
        ks = jax.random.split(key, 10)

        def w(k, shape, scale=0.02):
            return jax.random.normal(k, shape, jnp.float32) * scale
        log_min, log_max = (float(np.log(0.001)), float(np.log(0.1)))
        dt_bias = jax.random.uniform(ks[1], (D,), jnp.float32) * (log_max - log_min) + log_min
        return {'x': jax.random.normal(ks[0], (B, L, D), jnp.float32), 'delta_W': w(ks[2], (D, D)), 'delta_b': jnp.zeros((D,), jnp.float32), 'B_W': w(ks[3], (N, D)), 'B_b': jnp.zeros((N,), jnp.float32), 'C_W': w(ks[4], (N, D)), 'C_b': jnp.zeros((N,), jnp.float32), 'A_log': jnp.zeros((D, N), jnp.float32), 'dt_bias': dt_bias, 'tau': jnp.ones((N,), jnp.float32), 'Wi_W': w(ks[5], (N, D)), 'Wi_b': jnp.zeros((N,), jnp.float32), 'Wr_W': w(ks[6], (N, N)), 'sel_W': w(ks[7], (D, N)), 'sel_b': jnp.zeros((D,), jnp.float32), 'h0': jnp.zeros((1, N), jnp.float32)}
    _L0_attn_all = _L0_attn_setup()
    _L0_attn_in = {k: v for k, v in _L0_attn_all.items() if k in ('delta_W', 'delta_b', 'B_W', 'B_b', 'C_W', 'C_b', 'A_log', 'dt_bias', 'tau', 'Wi_W', 'Wi_b', 'Wr_W', 'sel_W', 'sel_b', 'h0')}
    del _L0_attn_all

    def _L0_xattn_setup():
        import jax, jax.numpy as jnp
        import numpy as np
        DIM_Q = 512
        DIM_KV = 384
        N_HEADS = 4

        def _split_heads(x):
            b, l, d = x.shape
            return x.reshape(b, l, N_HEADS, d // N_HEADS).transpose(0, 2, 1, 3)
        key = jax.random.key(seed)
        ks = jax.random.split(key, 7)
        b, lq, lkv = (4, 1024, 1024)
        q = jax.random.normal(ks[0], (b, lq, DIM_Q), dtype=jnp.float32)
        kv = jax.random.normal(ks[1], (b, lkv, DIM_KV), dtype=jnp.float32)
        s_q = 1.0 / np.sqrt(DIM_Q)
        s_kv = 1.0 / np.sqrt(DIM_KV)
        Wq = jax.random.normal(ks[2], (DIM_Q, DIM_Q), dtype=jnp.float32) * s_q
        Wk = jax.random.normal(ks[3], (DIM_Q, DIM_KV), dtype=jnp.float32) * s_kv
        Wv = jax.random.normal(ks[4], (DIM_Q, DIM_KV), dtype=jnp.float32) * s_kv
        Wo = jax.random.normal(ks[5], (DIM_Q, DIM_Q), dtype=jnp.float32) * s_q
        bo = jax.random.normal(ks[6], (DIM_Q,), dtype=jnp.float32) * 0.01
        return {'q': q, 'kv': kv, 'Wq': Wq, 'Wk': Wk, 'Wv': Wv, 'Wo': Wo, 'bo': bo}
    _L0_xattn_all = _L0_xattn_setup()
    _L0_xattn_in = {k: v for k, v in _L0_xattn_all.items() if k in ('Wq', 'Wk', 'Wv', 'Wo', 'bo')}
    del _L0_xattn_all

    def _L0_ffn_setup():
        import jax, jax.numpy as jnp
        import numpy as np
        DIM = 512
        INTER = 1024
        E = 8
        TOPK = 2
        ROUTE_SCALE = 1.0

        def _mlp(x, w1, w2, w3):
            h = jax.nn.silu(x @ w1.T) * (x @ w3.T)
            return h @ w2.T
        key = jax.random.key(seed)
        ks = jax.random.split(key, 10)
        s_in = 0.02
        return {'x': jax.random.normal(ks[0], (4, 1024, DIM), dtype=jnp.float32), 'gate_w': jax.random.normal(ks[1], (E, DIM), dtype=jnp.float32) * s_in, 'gate_bias': jax.random.normal(ks[2], (E,), dtype=jnp.float32) * 0.01, 'w1': jax.random.normal(ks[3], (E, INTER, DIM), dtype=jnp.float32) * s_in, 'w2': jax.random.normal(ks[4], (E, DIM, INTER), dtype=jnp.float32) * s_in, 'w3': jax.random.normal(ks[5], (E, INTER, DIM), dtype=jnp.float32) * s_in, 'sw1': jax.random.normal(ks[6], (INTER, DIM), dtype=jnp.float32) * s_in, 'sw2': jax.random.normal(ks[7], (DIM, INTER), dtype=jnp.float32) * s_in, 'sw3': jax.random.normal(ks[8], (INTER, DIM), dtype=jnp.float32) * s_in}
    _L0_ffn_all = _L0_ffn_setup()
    _L0_ffn_in = {k: v for k, v in _L0_ffn_all.items() if k in ('gate_w', 'gate_bias', 'w1', 'w2', 'w3', 'sw1', 'sw2', 'sw3')}
    del _L0_ffn_all

    def _L1_attn_setup():
        import jax, jax.numpy as jnp
        import numpy as np
        D_MODEL = 512
        N_HEADS = 16
        HEAD_DIM = D_MODEL // N_HEADS
        ROPE_BASE = 10000.0

        def _rope_tables(T, dtype=jnp.float32):
            half = HEAD_DIM // 2
            inv_freq = 1.0 / ROPE_BASE ** (jnp.arange(0, HEAD_DIM, 2, dtype=jnp.float32) / HEAD_DIM)
            t = jnp.arange(T, dtype=jnp.float32)
            freqs = jnp.einsum('i,j->ij', t, inv_freq)
            return (jnp.cos(freqs).astype(dtype), jnp.sin(freqs).astype(dtype))

        def _apply_rotary(x, cos, sin):
            B, T, H, D = x.shape
            xr = x.reshape(B, T, H, D // 2, 2)
            x0, x1 = (xr[..., 0], xr[..., 1])
            c = cos[None, :, None, :]
            s = sin[None, :, None, :]
            out = jnp.stack([x0 * c - x1 * s, x0 * s + x1 * c], axis=-1)
            return out.reshape(B, T, H, D)
        key = jax.random.key(seed)
        ks = jax.random.split(key, 5)
        x = jax.random.normal(ks[0], (4, 512, D_MODEL), dtype=jnp.float32)
        init = 1.0 / np.sqrt(D_MODEL)
        Wq = jax.random.uniform(ks[1], (D_MODEL, D_MODEL), jnp.float32, -init, init)
        Wk = jax.random.uniform(ks[2], (D_MODEL, D_MODEL), jnp.float32, -init, init)
        Wv = jax.random.uniform(ks[3], (D_MODEL, D_MODEL), jnp.float32, -init, init)
        Wo = jax.random.uniform(ks[4], (D_MODEL, D_MODEL), jnp.float32, -init, init)
        return {'x': x, 'Wq': Wq, 'Wk': Wk, 'Wv': Wv, 'Wo': Wo}
    _L1_attn_all = _L1_attn_setup()
    _L1_attn_in = {k: v for k, v in _L1_attn_all.items() if k in ('Wq', 'Wk', 'Wv', 'Wo')}
    del _L1_attn_all

    def _L1_xattn_setup():
        import jax, jax.numpy as jnp
        import numpy as np
        IMAGE_DIM = 512
        TEXT_DIM = 384
        NUM_HEADS = 16
        HEAD_DIM = IMAGE_DIM // NUM_HEADS
        key = jax.random.key(seed)
        ks = jax.random.split(key, 14)
        B, N, M = (4, 2048, 256)
        s_img = 1.0 / np.sqrt(IMAGE_DIM)
        s_txt = 1.0 / np.sqrt(TEXT_DIM)
        s_ff = 1.0 / np.sqrt(2 * IMAGE_DIM)
        return {'x': jax.random.normal(ks[0], (B, N, IMAGE_DIM), jnp.float32), 'y': jax.random.normal(ks[1], (B, M, TEXT_DIM), jnp.float32), 'Wq': jax.random.normal(ks[2], (IMAGE_DIM, IMAGE_DIM), jnp.float32) * s_img, 'bq': jax.random.normal(ks[3], (IMAGE_DIM,), jnp.float32) * s_img, 'Wk': jax.random.normal(ks[4], (TEXT_DIM, IMAGE_DIM), jnp.float32) * s_txt, 'bk': jax.random.normal(ks[5], (IMAGE_DIM,), jnp.float32) * s_txt, 'Wv': jax.random.normal(ks[6], (TEXT_DIM, IMAGE_DIM), jnp.float32) * s_txt, 'bv': jax.random.normal(ks[7], (IMAGE_DIM,), jnp.float32) * s_txt, 'W1': jax.random.normal(ks[8], (IMAGE_DIM, 2 * IMAGE_DIM), jnp.float32) * s_img, 'b1': jax.random.normal(ks[9], (2 * IMAGE_DIM,), jnp.float32) * s_img, 'W2': jax.random.normal(ks[10], (2 * IMAGE_DIM, IMAGE_DIM), jnp.float32) * s_ff, 'b2': jax.random.normal(ks[11], (IMAGE_DIM,), jnp.float32) * s_ff}
    _L1_xattn_all = _L1_xattn_setup()
    _L1_xattn_in = {k: v for k, v in _L1_xattn_all.items() if k in ('Wq', 'bq', 'Wk', 'bk', 'Wv', 'bv', 'W1', 'b1', 'W2', 'b2')}
    del _L1_xattn_all

    def _L1_ffn_setup():
        import jax, jax.numpy as jnp
        import numpy as np
        BLOCK = 16
        _GRID = jnp.array([0.0, 0.5, 1.0, 1.5, 2.0, 3.0, 4.0, 6.0], dtype=jnp.float32)
        _MID = jnp.array([0.25, 0.75, 1.25, 1.75, 2.5, 3.5, 5.0], dtype=jnp.float32)

        def fp4_quant_dequant(x):
            shape = x.shape
            xb = x.reshape(shape[:-1] + (shape[-1] // BLOCK, BLOCK))
            scale = jnp.max(jnp.abs(xb), axis=-1, keepdims=True) / 6.0
            scale = jnp.maximum(scale, jnp.float32(1e-12))
            xn = xb / scale
            idx = jnp.searchsorted(_MID, jnp.abs(xn))
            q = _GRID[idx] * jnp.sign(xn) * scale
            return q.reshape(shape)

        def fp4_linear(x, w):
            xq = fp4_quant_dequant(x)
            wq = fp4_quant_dequant(w)
            return jnp.einsum('bsk,nk->bsn', xq, wq)
        key = jax.random.key(seed)
        k1, k2, k3, k4 = jax.random.split(key, 4)
        H, I = (512, 1408)
        x = jax.random.normal(k1, (4, 2048, H), dtype=jnp.float32)
        w_gate = jax.random.normal(k2, (I, H), dtype=jnp.float32) * 0.02
        w_up = jax.random.normal(k3, (I, H), dtype=jnp.float32) * 0.02
        w_down = jax.random.normal(k4, (H, I), dtype=jnp.float32) * 0.02
        return {'x': x, 'w_gate': w_gate, 'w_up': w_up, 'w_down': w_down}
    _L1_ffn_all = _L1_ffn_setup()
    _L1_ffn_in = {k: v for k, v in _L1_ffn_all.items() if k in ('w_gate', 'w_up', 'w_down')}
    del _L1_ffn_all
    return {'x': x, 'ctx_768': ctx_768, 'L0_attn_delta_W': _L0_attn_in['delta_W'], 'L0_attn_delta_b': _L0_attn_in['delta_b'], 'L0_attn_B_W': _L0_attn_in['B_W'], 'L0_attn_B_b': _L0_attn_in['B_b'], 'L0_attn_C_W': _L0_attn_in['C_W'], 'L0_attn_C_b': _L0_attn_in['C_b'], 'L0_attn_A_log': _L0_attn_in['A_log'], 'L0_attn_dt_bias': _L0_attn_in['dt_bias'], 'L0_attn_tau': _L0_attn_in['tau'], 'L0_attn_Wi_W': _L0_attn_in['Wi_W'], 'L0_attn_Wi_b': _L0_attn_in['Wi_b'], 'L0_attn_Wr_W': _L0_attn_in['Wr_W'], 'L0_attn_sel_W': _L0_attn_in['sel_W'], 'L0_attn_sel_b': _L0_attn_in['sel_b'], 'L0_attn_h0': _L0_attn_in['h0'], 'L0_xattn_Wq': _L0_xattn_in['Wq'], 'L0_xattn_Wk': _L0_xattn_in['Wk'], 'L0_xattn_Wv': _L0_xattn_in['Wv'], 'L0_xattn_Wo': _L0_xattn_in['Wo'], 'L0_xattn_bo': _L0_xattn_in['bo'], 'L0_ffn_gate_w': _L0_ffn_in['gate_w'], 'L0_ffn_gate_bias': _L0_ffn_in['gate_bias'], 'L0_ffn_w1': _L0_ffn_in['w1'], 'L0_ffn_w2': _L0_ffn_in['w2'], 'L0_ffn_w3': _L0_ffn_in['w3'], 'L0_ffn_sw1': _L0_ffn_in['sw1'], 'L0_ffn_sw2': _L0_ffn_in['sw2'], 'L0_ffn_sw3': _L0_ffn_in['sw3'], 'L1_attn_Wq': _L1_attn_in['Wq'], 'L1_attn_Wk': _L1_attn_in['Wk'], 'L1_attn_Wv': _L1_attn_in['Wv'], 'L1_attn_Wo': _L1_attn_in['Wo'], 'L1_xattn_Wq': _L1_xattn_in['Wq'], 'L1_xattn_bq': _L1_xattn_in['bq'], 'L1_xattn_Wk': _L1_xattn_in['Wk'], 'L1_xattn_bk': _L1_xattn_in['bk'], 'L1_xattn_Wv': _L1_xattn_in['Wv'], 'L1_xattn_bv': _L1_xattn_in['bv'], 'L1_xattn_W1': _L1_xattn_in['W1'], 'L1_xattn_b1': _L1_xattn_in['b1'], 'L1_xattn_W2': _L1_xattn_in['W2'], 'L1_xattn_b2': _L1_xattn_in['b2'], 'L1_ffn_w_gate': _L1_ffn_in['w_gate'], 'L1_ffn_w_up': _L1_ffn_in['w_up'], 'L1_ffn_w_down': _L1_ffn_in['w_down']}

def reference(x, ctx_768, L0_attn_delta_W, L0_attn_delta_b, L0_attn_B_W, L0_attn_B_b, L0_attn_C_W, L0_attn_C_b, L0_attn_A_log, L0_attn_dt_bias, L0_attn_tau, L0_attn_Wi_W, L0_attn_Wi_b, L0_attn_Wr_W, L0_attn_sel_W, L0_attn_sel_b, L0_attn_h0, L0_xattn_Wq, L0_xattn_Wk, L0_xattn_Wv, L0_xattn_Wo, L0_xattn_bo, L0_ffn_gate_w, L0_ffn_gate_bias, L0_ffn_w1, L0_ffn_w2, L0_ffn_w3, L0_ffn_sw1, L0_ffn_sw2, L0_ffn_sw3, L1_attn_Wq, L1_attn_Wk, L1_attn_Wv, L1_attn_Wo, L1_xattn_Wq, L1_xattn_bq, L1_xattn_Wk, L1_xattn_bk, L1_xattn_Wv, L1_xattn_bv, L1_xattn_W1, L1_xattn_b1, L1_xattn_W2, L1_xattn_b2, L1_ffn_w_gate, L1_ffn_w_up, L1_ffn_w_down):
    import jax
    import jax.numpy as jnp

    def _L0_attn_ref(x, delta_W, delta_b, B_W, B_b, C_W, C_b, A_log, dt_bias, tau, Wi_W, Wi_b, Wr_W, sel_W, sel_b, h0):
        import jax, jax.numpy as jnp
        import numpy as np
        B, L, D, N = (2, 1024, 512, 16)
        DT = 0.1
        Bsz, Ls, Dm = x.shape
        Ns = A_log.shape[1]
        gc = x.mean(axis=1)
        inp_sig = gc @ Wi_W.T + Wi_b
        cur = jnp.broadcast_to(h0, (Bsz, Ns))
        rec = cur @ Wr_W.T
        tau_c = jnp.clip(tau, 0.1, 10.0)
        dh_dt = (-cur + jnp.tanh(inp_sig + rec)) / tau_c[None, :]
        new_h = cur + DT * dh_dt
        sel = jax.nn.sigmoid(new_h @ sel_W.T + sel_b)
        xs = x * sel[:, None, :]
        delta = jax.nn.softplus(xs @ delta_W.T + delta_b + dt_bias)
        Bm = xs @ B_W.T + B_b
        Cm = xs @ C_W.T + C_b
        A = -jnp.exp(A_log)
        A_d = jnp.exp(A[None, None] * delta[..., None])
        factor = jnp.where(jnp.abs(A)[None, None] < 1e-06, delta[..., None], (A_d - 1.0) / A[None, None])
        B_d = factor * Bm[:, :, None, :]

        def step(h, inputs):
            Ad_t, Bd_t, x_t, C_t = inputs
            h = Ad_t * h + Bd_t * x_t[..., None]
            y = jnp.einsum('bdn,bn->bd', h, C_t)
            return (h, y)
        h_init = jnp.zeros((Bsz, Dm, Ns), x.dtype)
        _, ys = jax.lax.scan(step, h_init, (A_d.transpose(1, 0, 2, 3), B_d.transpose(1, 0, 2, 3), xs.transpose(1, 0, 2), Cm.transpose(1, 0, 2)))
        return ys.transpose(1, 0, 2)

    def _L0_xattn_ref(q, kv, Wq, Wk, Wv, Wo, bo):
        import jax, jax.numpy as jnp
        import numpy as np
        DIM_Q = 512
        DIM_KV = 384
        N_HEADS = 4

        def _split_heads(x):
            b, l, d = x.shape
            return x.reshape(b, l, N_HEADS, d // N_HEADS).transpose(0, 2, 1, 3)
        qp = q @ Wq.T
        kp = kv @ Wk.T
        vp = kv @ Wv.T
        qh, kh, vh = (_split_heads(qp), _split_heads(kp), _split_heads(vp))
        scale = (DIM_Q // N_HEADS) ** (-0.5)
        scores = jnp.einsum('bhqd,bhkd->bhqk', qh, kh) * scale
        attn = jax.nn.softmax(scores, axis=-1)
        ctx = jnp.einsum('bhqk,bhkd->bhqd', attn, vh)
        b, h, lq, hd = ctx.shape
        ctx = ctx.transpose(0, 2, 1, 3).reshape(b, lq, h * hd)
        return ctx @ Wo.T + bo

    def _L0_ffn_ref(x, gate_w, gate_bias, w1, w2, w3, sw1, sw2, sw3):
        import jax, jax.numpy as jnp
        import numpy as np
        DIM = 512
        INTER = 1024
        E = 8
        TOPK = 2
        ROUTE_SCALE = 1.0

        def _mlp(x, w1, w2, w3):
            h = jax.nn.silu(x @ w1.T) * (x @ w3.T)
            return h @ w2.T
        shape = x.shape
        xt = x.reshape(-1, DIM)
        T = xt.shape[0]
        logits = xt @ gate_w.T
        scores = jax.nn.softmax(logits.astype(jnp.float32), axis=-1)
        original_scores = scores
        biased = scores + gate_bias
        _, indices = jax.lax.top_k(biased, TOPK)
        weights = jnp.take_along_axis(original_scores, indices, axis=1)
        weights = (weights * ROUTE_SCALE).astype(x.dtype)
        combine = (jax.nn.one_hot(indices, E, dtype=weights.dtype) * weights[..., None]).sum(axis=1)
        y = jnp.zeros_like(xt)
        for e in range(E):
            y = y + _mlp(xt, w1[e], w2[e], w3[e]) * combine[:, e:e + 1]
        z = _mlp(xt, sw1, sw2, sw3)
        return (y + z).reshape(shape)

    def _L1_attn_ref(x, Wq, Wk, Wv, Wo):
        import jax, jax.numpy as jnp
        import numpy as np
        D_MODEL = 512
        N_HEADS = 16
        HEAD_DIM = D_MODEL // N_HEADS
        ROPE_BASE = 10000.0

        def _rope_tables(T, dtype=jnp.float32):
            half = HEAD_DIM // 2
            inv_freq = 1.0 / ROPE_BASE ** (jnp.arange(0, HEAD_DIM, 2, dtype=jnp.float32) / HEAD_DIM)
            t = jnp.arange(T, dtype=jnp.float32)
            freqs = jnp.einsum('i,j->ij', t, inv_freq)
            return (jnp.cos(freqs).astype(dtype), jnp.sin(freqs).astype(dtype))

        def _apply_rotary(x, cos, sin):
            B, T, H, D = x.shape
            xr = x.reshape(B, T, H, D // 2, 2)
            x0, x1 = (xr[..., 0], xr[..., 1])
            c = cos[None, :, None, :]
            s = sin[None, :, None, :]
            out = jnp.stack([x0 * c - x1 * s, x0 * s + x1 * c], axis=-1)
            return out.reshape(B, T, H, D)
        B, T, C = x.shape
        H, Dh = (N_HEADS, HEAD_DIM)
        scale = Dh ** (-0.5)
        q = (x @ Wq.T).reshape(B, T, H, Dh)
        k = (x @ Wk.T).reshape(B, T, H, Dh)
        v = (x @ Wv.T).reshape(B, T, H, Dh)
        cos, sin = _rope_tables(T, x.dtype)
        q = _apply_rotary(q, cos, sin)
        k = _apply_rotary(k, cos, sin)
        q = q.transpose(0, 2, 1, 3).astype(jnp.float32)
        k = k.transpose(0, 2, 1, 3).astype(jnp.float32)
        v = v.transpose(0, 2, 1, 3)
        scores = jnp.einsum('bhqd,bhkd->bhqk', q, k) * scale
        causal = jnp.triu(jnp.ones((T, T), dtype=bool), k=1)
        scores = jnp.where(causal[None, None], -jnp.inf, scores)
        attn = jax.nn.softmax(scores, axis=-1).astype(v.dtype)
        out = jnp.einsum('bhqk,bhkd->bhqd', attn, v)
        out = out.transpose(0, 2, 1, 3).reshape(B, T, C)
        return out @ Wo.T

    def _L1_xattn_ref(x, y, Wq, bq, Wk, bk, Wv, bv, W1, b1, W2, b2):
        import jax, jax.numpy as jnp
        import numpy as np
        IMAGE_DIM = 512
        TEXT_DIM = 384
        NUM_HEADS = 16
        HEAD_DIM = IMAGE_DIM // NUM_HEADS
        B, N, _ = x.shape
        M = y.shape[1]
        q = (x @ Wq + bq).reshape(B, N, NUM_HEADS, HEAD_DIM)
        k = (y @ Wk + bk).reshape(B, M, NUM_HEADS, HEAD_DIM)
        v = (y @ Wv + bv).reshape(B, M, NUM_HEADS, HEAD_DIM)
        scale = 1.0 / np.sqrt(HEAD_DIM)
        scores = jnp.einsum('bnhd,bmhd->bhnm', q, k) * scale
        attn = jax.nn.softmax(scores, axis=-1)
        out = jnp.einsum('bhnm,bmhd->bnhd', attn, v).reshape(B, N, IMAGE_DIM)
        h = jax.nn.relu(out @ W1 + b1)
        return h @ W2 + b2

    def _L1_ffn_ref(x, w_gate, w_up, w_down):
        import jax, jax.numpy as jnp
        import numpy as np
        BLOCK = 16
        _GRID = jnp.array([0.0, 0.5, 1.0, 1.5, 2.0, 3.0, 4.0, 6.0], dtype=jnp.float32)
        _MID = jnp.array([0.25, 0.75, 1.25, 1.75, 2.5, 3.5, 5.0], dtype=jnp.float32)

        def fp4_quant_dequant(x):
            shape = x.shape
            xb = x.reshape(shape[:-1] + (shape[-1] // BLOCK, BLOCK))
            scale = jnp.max(jnp.abs(xb), axis=-1, keepdims=True) / 6.0
            scale = jnp.maximum(scale, jnp.float32(1e-12))
            xn = xb / scale
            idx = jnp.searchsorted(_MID, jnp.abs(xn))
            q = _GRID[idx] * jnp.sign(xn) * scale
            return q.reshape(shape)

        def fp4_linear(x, w):
            xq = fp4_quant_dequant(x)
            wq = fp4_quant_dequant(w)
            return jnp.einsum('bsk,nk->bsn', xq, wq)
        gate = fp4_linear(x, w_gate)
        y = fp4_linear(x, w_up)
        h = jax.nn.silu(gate) * y
        return fp4_linear(h, w_down)
    x = _layernorm(x + _L0_attn_ref(x, L0_attn_delta_W, L0_attn_delta_b, L0_attn_B_W, L0_attn_B_b, L0_attn_C_W, L0_attn_C_b, L0_attn_A_log, L0_attn_dt_bias, L0_attn_tau, L0_attn_Wi_W, L0_attn_Wi_b, L0_attn_Wr_W, L0_attn_sel_W, L0_attn_sel_b, L0_attn_h0), axis=-1)
    x = _layernorm(x + _L0_xattn_ref(x, ctx_768, L0_xattn_Wq, L0_xattn_Wk, L0_xattn_Wv, L0_xattn_Wo, L0_xattn_bo), axis=-1)
    x = _layernorm(x + _L0_ffn_ref(x, L0_ffn_gate_w, L0_ffn_gate_bias, L0_ffn_w1, L0_ffn_w2, L0_ffn_w3, L0_ffn_sw1, L0_ffn_sw2, L0_ffn_sw3), axis=-1)
    x = _layernorm(x + _L1_attn_ref(x, L1_attn_Wq, L1_attn_Wk, L1_attn_Wv, L1_attn_Wo), axis=-1)
    x = _layernorm(x + _L1_xattn_ref(x, ctx_768, L1_xattn_Wq, L1_xattn_bq, L1_xattn_Wk, L1_xattn_bk, L1_xattn_Wv, L1_xattn_bv, L1_xattn_W1, L1_xattn_b1, L1_xattn_W2, L1_xattn_b2), axis=-1)
    x = _layernorm(x + _L1_ffn_ref(x, L1_ffn_w_gate, L1_ffn_w_up, L1_ffn_w_down), axis=-1)
    return x

_drawn_inputs = setup_inputs


def setup_inputs(seed=0):
    import zlib

    import numpy as np

    out = dict(_drawn_inputs(seed))
    spreads = {'L0_attn_delta_b': (0.0, 2.0),
     'L0_attn_B_b': (0.0, 2.0),
     'L0_attn_C_b': (0.0, 2.0),
     'L0_attn_A_log': (0.0, 2.0),
     'L0_attn_tau': (1.0, 0.6),
     'L0_attn_Wi_b': (0.0, 2.0),
     'L0_attn_sel_b': (0.0, 2.0),
     'L0_attn_h0': (0.0, 2.0)}
    factors = {'L0_attn_delta_W': 64.0,
     'L0_attn_B_W': 38.92,
     'L0_attn_C_W': 37.52,
     'L0_attn_dt_bias': 45.208,
     'L0_attn_Wi_W': 64.0,
     'L0_attn_Wr_W': 64.0,
     'L0_attn_sel_W': 64.0,
     'L0_xattn_bo': 4.687,
     'L0_ffn_gate_w': 2.994,
     'L0_ffn_gate_bias': 44.398,
     'L1_attn_Wq': 2.731,
     'L1_xattn_bq': 6.245,
     'L1_xattn_bk': 64.0}
    for name, (base, spread) in spreads.items():
        noise = np.random.default_rng([zlib.crc32(name.encode()), seed]).standard_normal(out[name].shape)
        drawn = base * np.exp(spread * noise) if base else spread * noise
        out[name] = jnp.asarray(drawn.astype(out[name].dtype))
    for name, factor in factors.items():
        out[name] = (out[name] * factor).astype(out[name].dtype)
    return out
```

```python
import math
from contextlib import ExitStack

import numpy as np

import concourse.bass as bass
from concourse import mybir

F32 = mybir.dt.float32
I32 = mybir.dt.int32
ALU = mybir.AluOpType
ACT = mybir.ActivationFunctionType
AX = mybir.AxisListType.X

P = 128
B, L, D = 8, 100, 512
T = B * L
KD = D // P
HALF = T // 2
N = 16
S, DC = 722, 384
KC = DC // P
SH = S // 2
SJ = -(-S // P)
H0 = 4
H1 = 16
DH = D // H1
E, FF = 8, 1024
FM = FF // P
I4 = 1408
I4M = I4 // P
LN_EPS = 1e-5
TINY_A = 1e-6
NEG = -1e30

VEC = {}
for _name, _n in (("delta_b", KD), ("dt_bias", KD), ("sel_b", KD), ("bo", KD), ("bq", KD), ("bk", KD),
                  ("b1", FM), ("b2", KD)):
    VEC[_name] = (sum(n for _, n in VEC.values()), _n)
NVEC = sum(n for _, n in VEC.values())


class Count:

    def __init__(self, sem):
        self.sem, self.n, self.base = sem, 0, 0

    def inc(self, ins):
        ins.then_inc(self.sem, 1)
        self.n = self.n + 1

    def enter(self, done):
        self.base = self.n
        self.n = self.base + done

    def leave(self, total):
        self.n = self.base + total


def program(nc, xT, vecs, small16, bcb, alog, ident_d, ones_d, rope_d, perm_d, mask_d, wiT, wrT, selT, bcT, dwT,
            ctxT, ctxN, wq0T, wk0, wv0T, wo0T, gateT, gate_bias, w1T, w3T, w2T,
            wq1T, wk1T, wv1T, wo1T, xq1, xk1, xv1, bv1, xw1, xw2, wf, out):
    ctx = ExitStack()
    with ctx:
        def sb(name, shape, dt=F32):
            return ctx.enter_context(nc.sbuf_tensor(name, shape, dt))

        def sem(name):
            return ctx.enter_context(nc.semaphore(name))

        PS = ctx.enter_context(nc.psum_tensor("PS", [P, 8, 512], F32))
        XT = sb("XT", [P, KD, T])
        R = sb("R", [P, KD, T])
        SQ = sb("SQ", [P, KD, T])
        RS = sb("RS", [P, T])
        vec = sb("vec", [P, NVEC])
        ident = sb("ident", [P, P])
        mean_w = sb("mean_w", [P, P])
        eps_c = sb("eps_c", [P, 1])
        ARENA = sb("ARENA", [P, 42000])

        def at(off, *dims, rows=P):
            n = math.prod(dims)
            v = ARENA[0:rows, off:off + n]
            assert off + n <= 42000, (off, n)
            if len(dims) == 2:
                return v.rearrange("p (a b) -> p a b", a=dims[0])
            if len(dims) == 3:
                return v.rearrange("p (a b c) -> p a b c", a=dims[0], b=dims[1])
            return v

        def col(name, k):
            return vec[:, VEC[name][0] + k:VEC[name][0] + k + 1]

        def halves(bank):
            return PS[:, bank:bank + 2, 0:HALF]

        def ln_tensor(pe, q):
            for h in range(2):
                pe.wait_ge(ln_in, 2 * q + h + 1)
                for k in range(KD):
                    last = pe.matmul(PS[:, h, 0:HALF], mean_w[:, :], R[:, k, h * HALF:(h + 1) * HALF],
                                     start=(k == 0), stop=(k == KD - 1))
                last.then_inc(ln_mean, 1)
            for h in range(2):
                pe.wait_ge(ln_sq, 2 * q + h + 1)
                for k in range(KD):
                    last = pe.matmul(PS[:, 2 + h, 0:HALF], mean_w[:, :], SQ[:, k, h * HALF:(h + 1) * HALF],
                                     start=(k == 0), stop=(k == KD - 1))
                last.then_inc(ln_var, 1)

        def ln_scalar(act, q):
            for h in range(2):
                act.wait_ge(ln_cen, 2 * q + h + 1)
                act.activation(SQ[:, :, h * HALF:(h + 1) * HALF], R[:, :, h * HALF:(h + 1) * HALF],
                               ACT.Square).then_inc(ln_sq, 1)
            for h in range(2):
                act.wait_ge(ln_var, 2 * q + h + 1)
                act.activation(RS[:, h * HALF:(h + 1) * HALF], PS[:, 2 + h, 0:HALF], ACT.Sqrt,
                               bias=eps_c[:, 0:1]).then_inc(ln_std, 1)

        def ln_vector(v, q):
            for h in range(2):
                v.wait_ge(ln_mean, 2 * q + h + 1)
                rows = R[:, :, h * HALF:(h + 1) * HALF]
                v.tensor_tensor(rows, rows, PS[:, h, 0:HALF].unsqueeze(1).to_broadcast([P, KD, HALF]),
                                ALU.subtract).then_inc(ln_cen, 1)
            for h in range(2):
                v.wait_ge(ln_std, 2 * q + h + 1)
                part = slice(h * HALF, (h + 1) * HALF)
                v.reciprocal(RS[:, part], RS[:, part]).then_inc(ln_inv, 1)
                v.wait_ge(ln_inv, 2 * q + h + 1)
                v.tensor_tensor(XT[:, :, part], R[:, :, part],
                                RS[:, part].unsqueeze(1).to_broadcast([P, KD, HALF]), ALU.mult).then_inc(ln_out, 1)

        XS = at(0, KD, T)
        DL = at(3200, KD, T)
        SP1, SP2, SP3 = at(6400, KD, T), at(9600, KD, T), at(12800, KD, T)
        BC = at(6400, 2, 2, T)
        AD = at(9600, 2, T)
        U, W, HS, V = at(11200, 2, T), at(12800, 2, T), at(14400, 2, T), at(16000, 2, T)
        dw = at(17600, KD, D)
        BCS = at(19648, T, rows=2 * N)
        ALOG, AA, KEEP, INV, TINY = (at(20448 + 64 * j, KD, N) for j in range(5))
        sm = at(20800, 8, rows=N)
        wi = at(20816, KD, N)
        wr = at(20880, N, rows=N)
        selw = at(20896, D, rows=N)
        bcw = at(21408, KD, 2 * N)
        SEL = at(21536, KD, B)
        GC = at(21568, KD, B)
        H8, TH, CUR8 = (at(21600 + 8 * j, B, rows=N) for j in range(3))
        TAU = at(21624, 2, rows=N)
        DB = at(21628, KD)
        bcbias = at(21632, 1, rows=2 * N)
        CNT = at(21636, 4)
        FLAG = sb("FLAG", [P, 1], I32)
        ZERO = at(21640, HALF)
        bc_dram = nc.dram_tensor("bc_rows", [2 * N, T], F32).ap()

        s_x, s_consts, s_wa, s_dw = sem("x_loaded"), sem("consts_loaded"), sem("gate_weights_loaded"), sem("delta_w_loaded")
        s_rows_out, s_bc = sem("bc_rows_stored"), [sem(f"bc_loaded_{e}") for e in range(2)]
        gate_pe, gate_act = sem("gate_product"), sem("gate_act")
        dve = Count(sem("dve_done"))
        xs_ready, gc_ready, newh_ready = sem("xs_ready"), sem("means_ready"), sem("new_h_ready")
        proj, proj_ev = sem("projected"), sem("projection_read")
        sp_dve, sp_act = sem("softplus_dve"), sem("softplus_act")
        a_ready, inv_ready, tiny_sum = sem("a_ready"), sem("inv_ready"), sem("tiny_counted")
        own_act = Count(sem("act_own"))
        ad_ready, ad_free = sem("decay_ready"), sem("decay_read")
        u_ready, w_done = sem("input_ready"), sem("input_read")
        rz, v_ready, v_used = sem("restart_set"), sem("output_ready"), sem("output_summed")
        y_ready = sem("y_ready")
        tiny_s = sem("tiny_path")
        ln_in, ln_mean, ln_cen, ln_sq, ln_var, ln_std, ln_inv, ln_out = (
            sem("ln_" + n) for n in ("in", "mean", "centred", "squared", "variance", "std", "inverse", "out"))
        s_out = sem("out_stored")
        zero_ready, flag_read = sem("zero_ready"), sem("tiny_flag_read")

        wq0, wk0w, wv0, wo0 = at(22100, KD, D), at(24148, H0, DC), at(25684, KC, D), at(27220, KD, D)
        CT = [at(29268 + 2166 * e, KC, S) for e in range(2)]
        CN = [at(33600 + 2304 * e, SJ, DC) for e in range(2)]
        QT = at(0, KD, T)
        QP = [at(3200 + 1200 * e, KC, H0 * L) for e in range(2)]
        PR = [at(5600 + 2888 * e, H0, S, rows=L) for e in range(2)]
        PT = at(11376, SJ, H0 * L)
        TT = at(13776, KC, H0 * L)
        CO = at(14976, KD, T)
        ST = [at(18176 + 16 * e, 4, H0, rows=L) for e in range(2)]
        s_wb = sem("xattn0_weights_loaded")
        s_ct, s_cn = [sem(f"ctxT_loaded_{e}") for e in range(2)], [sem(f"ctxN_loaded_{e}") for e in range(2)]
        q0_full, q0_read = sem("q0_projected"), sem("q0_read")
        s_full, s_free = sem("score_banks_full"), sem("score_banks_free")
        pt_full, pt_free = sem("pt_bank_full"), sem("pt_bank_free")
        tv_full, tv_free = sem("tv_bank_full"), sem("tv_bank_free")
        nm_ready, rs_ready, pr_ready, o0_full = sem("neg_max_ready"), sem("rsum_ready"), sem("probs_ready"), sem("o0_full")

        def width(j):
            return min(P, S - j * P)

        def batches(eng, turn):
            turn(0, None, 0)
            with eng.Fori(0, B // 2 - 1) as two:
                turn(two * 2 + 1, two * 2, 1)
                turn(two * 2 + 2, two * 2 + 1, 0)
            turn(B - 1, B - 2, 1)
            turn(None, B - 1, 0)

        def ctx_loads(b, per, e):
            return b * (per // 2) + (per - e * (per // 2))

        WE = [[at(12288 * e, KD, FF), at(12288 * e + 4096, KD, FF), at(12288 * e + 8192, FM, D)] for e in range(2)]
        HH = [at(24576 + 3200 * h, FM, HALF) for h in range(2)]
        SIL = at(30976, 2, HALF)
        CB = [at(31776 + T * e, T) for e in range(2)]
        TMP = at(33376, 4, HALF)
        gw, gb, rank = at(41900, KD, E), at(41932, E), at(41940, E)
        SC, BI, KEY, OH, CM = (at(34976 + 64 * j, B, E, rows=L) for j in range(5))
        GS = at(35296, 4, B, rows=L)
        CBT = at(35328, T, rows=E)
        ONE = at(36128, T, rows=1)
        comb_dram = nc.dram_tensor("combine_rows", [E + 1, T], F32).ap()
        s_gw, s_we, s_cb = sem("router_loaded"), [sem(f"expert_loaded_{e}") for e in range(2)], [sem(f"combine_loaded_{e}") for e in range(2)]
        s_comb, one_ready, r_copied = sem("combine_stored"), sem("ones_ready"), sem("stream_copied")
        lg_full, rt_dve, rt_exp = sem("logits_ready"), sem("router_dve"), sem("router_exp")
        cm_full, cm_read = sem("combine_transposed"), sem("combine_read")
        up_full, sil_ready, up_free = sem("up_banks_full"), sem("silu_ready"), sem("up_banks_free")
        dn_full, dn_free, acc = sem("down_bank_full"), sem("down_bank_free"), sem("accumulated")

        NU = 3 * KD * I4 // D
        RAW = [at(36928 + 512 * e, D) for e in range(2)]
        WTS = [at(37952 + 512 * e, D) for e in range(2)]
        UA, US, UG, UH = (at(38976 + 512 * j, D) for j in range(4))
        UM, UC, UR = (at(41024 + 32 * j, D // 16) for j in range(3))
        wt_dram = nc.dram_tensor("quantised_weights", [P, NU * D], F32).ap()
        q_scale, q_scaled, q_steps, q_done = sem("quant_scales"), sem("quant_scaled"), sem("quant_steps"), sem("quant_done")
        q_abs, q_sign, q_ss = sem("quant_abs"), sem("quant_sign"), sem("quant_signed_scale")
        s_raw, s_wst = ([sem(f"unit_loaded_{e}") for e in range(2)], [sem(f"unit_stored_{e}") for e in range(2)])
        wt_full, wt_copied = sem("unit_transposed"), sem("unit_copied")

        def units(e):
            if isinstance(e, int) and e == 0:
                return [(0, 0, 0)]
            return [(i, e * 4 + (i - 3), (i + 1) % 2) for i in range(4)]

        def experts(eng, turn):
            turn(0, 0)
            with eng.Fori(0, E // 2) as two:
                turn(two * 2 + 1, 1)
                turn(two * 2 + 2, 0)

        QR, KR, QS = at(0, KD, T), at(3200, KD, T), at(6400, KD, T)
        wq1, wk1, wv1, wo1 = (at(12800 + 2048 * j, KD, D) for j in range(4))
        rope, perm, causal = at(20992, 2 * L), at(21192, P), at(21320, L, rows=L)
        VV = at(24576, B, D, rows=L)
        AO = at(28672, KD, T)
        QB = [at(31872 + 400 * e, KD, L) for e in range(2)]
        KB = [at(32672 + 400 * e, KD, L) for e in range(2)]
        SM = [at(33472 + 1600 * e, H1, L, rows=L) for e in range(2)]
        PT1 = at(36672, H1, L, rows=L)
        ON = at(38400, D, rows=L)
        S1 = [at(38912 + 48 * e, 3, H1, rows=L) for e in range(2)]
        s_wd = sem("attn1_weights_loaded")
        qk_full, qk_read, pm_full, rot = sem("qk_projected"), sem("qk_read"), sem("pairs_swapped"), sem("rotated")
        v1_full, v1_read, qkb = sem("v1_projected"), sem("v1_read"), sem("qk_copied")
        sc_full, sc_read, sc_dve, sc_exp = sem("scores1_full"), sem("scores1_read"), sem("scores1_dve"), sem("probs1_ready")
        p1_full, p1_free, pv_full, on_ready = sem("probs1_transposed"), sem("probs1_read"), sem("pv1_full"), sem("normed1_ready")
        ot_full, ot_free, ri_ready, o1_full = sem("out1_transposed"), sem("out1_read"), sem("rsum1_ready"), sem("o1_full")

        xkw, xvw, xqw, bvr = at(21420, KC, D), at(22956, KC, D), at(9600, KD, D), at(11648, D)
        CX = [at(39100, KC, S), at(12800, KC, S)]
        KX = [at(2888 * e, KD, S) for e in range(2)]
        QX = at(5776, KD, T)
        QBX = [at(8976, KD, L), at(20902, KD, L)]
        AO2 = at(14966, KD, T)
        PX = [at(18166 + SJ * P * e, SJ * P, rows=L) for e in range(2)]
        PTX = [at(19702 + 600 * e, SJ, L) for e in range(2)]
        VX = [at(24576 + 3072 * e, SJ, D) for e in range(2)]
        w1x, w2x = at(30720, KD, 2 * D), at(34816, 2 * KD, D)
        OX = [at(12160, D, rows=L), at(41266, D, rows=L)]
        SX = [at(41778 + 48 * e, 3, H1, rows=L) for e in range(2)]
        HX = at(0, 2 * KD, T)
        s_wx, s_wm, s_cx = sem("xattn1_weights_loaded"), sem("xattn1_mlp_loaded"), [sem(f"ctx1_loaded_{e}") for e in range(2)]
        kv_full, k_read, v_read = sem("kv_bank_full"), sem("keys_read"), sem("values_read")
        qx_full, qx_read, qbx = sem("qx_projected"), sem("qx_read"), sem("qx_copied")
        x_full, x_free, nmx = sem("xscores_full"), sem("xscores_free"), sem("xneg_max")
        ptx_full, ptx_free, pad_ready = sem("xprobs_transposed"), sem("xprobs_read"), sem("pad_zeroed")
        ox_full, ox_norm, rix = sem("xout_full"), sem("xout_normed"), sem("xrsum")
        otx_full, otx_free = sem("xout_transposed"), sem("xout_read")
        mx_full, mx_free, m2_full = sem("mlp_bank_full"), sem("mlp_bank_free"), sem("mlp_out_full")

        NKV = 2 * KD + SJ
        GROUP_AT = {s: s for s in range(NKV - 2)} | {H1: NKV - 2, H1 + 1: NKV - 1}

        def xbatches(eng, turn):
            turn(0, None, 1, 0)
            with eng.Fori(0, B // 2 - 1) as two:
                turn(two * 2 + 1, two * 2, two * 2 + 2, 1)
                turn(two * 2 + 2, two * 2 + 1, two * 2 + 3, 0)
            turn(B - 1, B - 2, None, 1)
            turn(None, B - 1, None, 0)

        def wait(eng, s, value):
            if not isinstance(value, int) or value > 0:
                eng.wait_ge(s, value)

        NT = -(-T // P)
        PARTS = [(0, D), (D, D), (2 * D, I4 - 2 * D)]
        WT = at(17920, NU * D)
        XK = at(0, NT, D)
        XQ = at(3584, D)
        XQT = [at(4096 + 512 * e, KD, P) for e in range(2)]
        HB = [at(5120 + I4 * e, I4) for e in range(2)]
        HQ, HQT = at(7936, I4), at(9344, I4M, P)
        XN, AB, SG, SS, QG, QH = (at(10752 + 512 * j, D) for j in range(6))
        AM, SCL, RI = (at(13824 + 32 * j, D // 16) for j in range(3))
        LS = [at(13920 + 8 * e, 8) for e in range(2)]
        XP = at(34816, KD, NT * P)
        XB = [at(38400 + 512 * e, KD, P) for e in range(2)]
        YR = [at(39424 + 512 * e, D) for e in range(2)]
        YS = at(40448, D)
        SI = at(40960, 2, D)
        WGv = WT[:, 0:KD * I4].rearrange("p (o k c) -> p k o c", k=KD, c=P)
        WUv = WT[:, KD * I4:2 * KD * I4].rearrange("p (o k c) -> p k o c", k=KD, c=P)
        WDv = WT[:, 2 * KD * I4:3 * KD * I4].rearrange("p (c m q) -> p m c q", m=I4M, q=P)

        s_wt = sem("weights_loaded")
        xp_ready, xb_ready = sem("padded"), sem("tile_copied")
        xk_full, xk_read, xq_full, xq_read = sem("xk_full"), sem("xk_read"), sem("xq_full"), sem("xq_read")
        gu_full, si_ready, gu_free = sem("gate_up_full"), sem("gate_silu"), sem("gate_up_read")
        hq_full, hq_read, y_full = sem("hq_full"), sem("hq_read"), sem("y_full")
        f_sum, f_mean, f_cen, f_var, f_inv, f_out = (sem("f_" + n) for n in ("sum", "mean", "centred", "deviation", "inverse", "out"))
        s_tile = [sem(f"tile_stored_{e}") for e in range(2)]

        def tiles(eng, turn):
            turn(0, None, None, NU, 1)
            turn(1, 0, None, NU + 1, 0)
            with eng.Fori(0, (NT - 3) // 2) as two:
                turn(two * 2 + 2, two * 2 + 1, two * 2, two * 8 + (NU + 2), 1)
                turn(two * 2 + 3, two * 2 + 2, two * 2 + 1, two * 8 + (NU + 6), 0)
            turn(NT - 1, NT - 2, NT - 3, 4 * NT + NU - 10, 1)
            turn(None, NT - 1, NT - 2, 4 * NT + NU - 6, 0)
            turn(None, None, NT - 1, 4 * NT + NU - 3, 1)

        block = ctx.enter_context(nc.Block())

        @block.sync
        def _(sp):
            sp.dma_start(XT[:, :, :], xT.rearrange("(k p) t -> p k t", p=P)).then_inc(s_x, 16)
            for dst, src in ((vec[:, :], vecs), (ident[:, :], ident_d), (mean_w[:, :], ones_d),
                             (ALOG, alog.rearrange("(k p) n -> p k n", p=P))):
                sp.dma_start(dst, src).then_inc(s_consts, 16)
            for dst, src in ((sm[:, 0:5], small16), (bcbias, bcb), (wi, wiT.rearrange("(k p) n -> p k n", p=P)),
                             (wr, wrT), (selw, selT), (bcw, bcT.rearrange("(k p) n -> p k n", p=P))):
                sp.dma_start(dst, src).then_inc(s_wa, 16)
            sp.dma_start(dw, dwT.rearrange("(k p) o -> p k o", p=P)).then_inc(s_dw, 16)
            for dst, src in ((wq0, wq0T.rearrange("(k p) o -> p k o", p=P)), (wk0w, wk0.rearrange("(k p) o -> p k o", p=P)),
                             (wv0, wv0T.rearrange("(k p) o -> p k o", p=P)), (wo0, wo0T.rearrange("(k p) o -> p k o", p=P))):
                sp.dma_start(dst, src).then_inc(s_wb, 16)

            def load_ctxT(b, e):
                sp.dma_start(CT[e], ctxT[bass.ds(b, 1), :, :].rearrange("a (k p) s -> p (a k) s", p=P)).then_inc(s_ct[e], 16)

            def load_ctx(b, e):
                whole = (SJ - 1) * P
                sp.dma_start(CN[e][:, 0:SJ - 1, :], ctxN[bass.ds(b, 1), 0:whole, :].rearrange("a (j p) d -> p (a j) d", p=P))\
                    .then_inc(s_cn[e], 16)
                sp.dma_start(CN[e][0:S - whole, SJ - 1, :], ctxN[bass.ds(b, 1), whole:S, :].rearrange("a p d -> (a p) d"))\
                    .then_inc(s_cn[e], 16)

            for e in range(2):
                load_ctxT(e, e)
                load_ctx(e, e)
            for dst, src in ((gw, gateT.rearrange("(k p) e -> p k e", p=P)),
                             (gb, gate_bias[0:1, 0:E].to_broadcast([P, E])), (rank, gate_bias[0:1, E:2 * E].to_broadcast([P, E]))):
                sp.dma_start(dst, src).then_inc(s_gw, 16)
            sp.wait_ge(proj_ev, 2)
            sp.dma_start(bc_dram, BCS).then_inc(s_rows_out, 16)
            sp.wait_ge(s_rows_out, 16)
            sp.wait_ge(sp_dve, 4)
            for n in range(2):
                for which in range(2):
                    sp.dma_start(BC[:, n, which, :],
                                 bc_dram[which * N + n:which * N + n + 1, :].to_broadcast([P, T])).then_inc(s_bc[n], 16)
            with sp.Fori(1, N // 2) as pair:
                n = pair * 2
                for e in range(2):
                    sp.wait_ge(v_ready, n * KD + KD * (e - 1))
                    for which in range(2):
                        sp.dma_start(BC[:, e, which, :],
                                     bc_dram[bass.ds(n + which * N + e, 1), :].to_broadcast([P, T])).then_inc(s_bc[e], 16)
            with sp.Fori(1, B // 2) as two:
                for e in range(2):
                    sp.wait_ge(s_full, two * 12 + 6 * (e - 1))
                    load_ctxT(two * 2 + e, e)
                    sp.wait_ge(tv_full, two * 8 + (4 * (e - 2) + 3))
                    load_ctx(two * 2 + e, e)
            def load_expert(e, slot):
                for dst, src, rows in ((WE[slot][0], w1T, D), (WE[slot][1], w3T, D), (WE[slot][2], w2T, FF)):
                    sp.dma_start(dst, src[bass.ds(e, 1), :, :].rearrange("a (k p) o -> p (a k) o", p=P)).then_inc(s_we[slot], 16)

            def load_combine(e, slot):
                sp.dma_start(CB[slot], comb_dram[bass.ds(e, 1), :].to_broadcast([P, T])).then_inc(s_cb[slot], 16)

            sp.wait_ge(tv_free, B * 4 + 2)
            load_expert(0, 0)
            sp.wait_ge(o0_full, 2 * KD)
            sp.sem_inc(s_wst[0], 16)
            sp.sem_inc(s_wst[1], 16)

            def load_unit(u, slot):
                sp.dma_start(RAW[slot], wf[:, bass.ds(u * D, D)]).then_inc(s_raw[slot], 16)

            load_unit(0, 0)
            load_unit(1, 1)
            load_expert(1, 1)
            sp.wait_ge(one_ready, 1)
            sp.dma_start(comb_dram[E:E + 1, :], ONE).then_inc(s_comb, 16)
            sp.wait_ge(cm_read, 2)
            sp.dma_start(comb_dram[0:E, :], CBT).then_inc(s_comb, 16)
            sp.wait_ge(s_comb, 32)
            load_combine(0, 0)
            load_combine(1, 1)

            def expert_sync(e, slot):
                for i, u, us in units(e):
                    if not isinstance(e, int) or u + 2 < NU:
                        sp.wait_ge(wt_full, u + 1)
                        load_unit(u + 2, us)
                    sp.wait_ge(wt_copied, u + 1)
                    sp.dma_start(wt_dram[:, bass.ds(u * D, D)], WTS[us]).then_inc(s_wst[us], 16)
                if not isinstance(e, int) or e + 2 <= E:
                    sp.wait_ge(dn_free, e * 8 + 12)
                    load_expert(e + 2, slot)
                    load_combine(e + 2, slot)

            expert_sync(0, 0)
            with sp.Fori(0, E // 2 - 1) as two:
                expert_sync(two * 2 + 1, 1)
                expert_sync(two * 2 + 2, 0)
            expert_sync(E - 1, 1)
            expert_sync(E, 0)
            sp.wait_ge(dn_free, 8 * E + 4)
            for dst, src in ((wq1, wq1T), (wk1, wk1T), (wv1, wv1T), (wo1, wo1T)):
                sp.dma_start(dst, src.rearrange("(k p) o -> p k o", p=P)).then_inc(s_wd, 16)
            for dst, src in ((rope, rope_d), (perm, perm_d), (causal, mask_d)):
                sp.dma_start(dst, src).then_inc(s_wd, 16)
            for dst, src in ((xkw, xk1), (xvw, xv1)):
                sp.dma_start(dst, src.rearrange("(k p) o -> p k o", p=P)).then_inc(s_wx, 16)

            def load_cx(b, e):
                sp.dma_start(CX[e], ctxT[bass.ds(b, 1), :, :].rearrange("a (k p) s -> p (a k) s", p=P)).then_inc(s_cx[e], 16)

            load_cx(0, 0)
            sp.wait_ge(dn_free, 8 * (E + 1) + 4)
            sp.dma_start(xqw, xq1.rearrange("(k p) o -> p k o", p=P)).then_inc(s_wx, 16)
            sp.dma_start(bvr, bv1.to_broadcast([P, D])).then_inc(s_wx, 16)
            sp.wait_ge(v1_full, B)
            load_cx(1, 1)
            sp.wait_ge(o1_full, 2 * KD)
            sp.dma_start(w1x, xw1.rearrange("(k p) o -> p k o", p=P)).then_inc(s_wm, 16)
            sp.dma_start(w2x, xw2.rearrange("(k p) o -> p k o", p=P)).then_inc(s_wm, 16)
            with sp.Fori(1, B // 2) as two:
                for e in range(2):
                    sp.wait_ge(v_read, two * (2 * SJ) + SJ * (e - 1))
                    load_cx(two * 2 + e, e)
            sp.wait_ge(s_wst[0], 16 * ((NU + 1) // 2 + 1))
            sp.wait_ge(s_wst[1], 16 * (NU // 2 + 1))
            sp.wait_ge(mx_full, 4 * KD)
            for w in range(3):
                cols = slice(w * KD * I4, (w + 1) * KD * I4)
                sp.dma_start(WT[:, cols], wt_dram[:, cols]).then_inc(s_wt, 16)

            def store(a, g, d, piece, e):
                if d is not None:
                    rows = min(P, T - d * P) if isinstance(d, int) else P
                    sp.wait_ge(f_out, d + 1)
                    sp.dma_start(out[bass.ds(d * P, rows), :], YR[1 - e][0:rows, :]).then_inc(s_tile[1 - e], 16)

            sp.sem_inc(s_tile[0], 16)
            sp.sem_inc(s_tile[1], 16)
            tiles(sp, store)
            sp.wait_ge(s_tile[0], 16 * ((NT + 1) // 2 + 1))
            sp.wait_ge(s_tile[1], 16 * (NT // 2 + 1))

        @block.tensor
        def _(pe):
            pe.wait_ge(s_wa, 96)
            pe.wait_ge(gc_ready, 1)
            for k in range(KD):
                pe.matmul(PS[0:N, 0, 0:B], wi[:, k, :], GC[:, k, :], start=(k == 0), stop=False)
            pe.matmul(PS[0:N, 0, 0:B], wr, CUR8, start=False, stop=True).then_inc(gate_pe, 1)
            pe.wait_ge(newh_ready, 1)
            for c in range(KD):
                last = pe.matmul(PS[:, 1, c * B:(c + 1) * B], selw[:, c * P:(c + 1) * P], H8, start=True, stop=True)
            last.then_inc(gate_pe, 1)
            pe.wait_ge(s_consts, 64)
            pe.wait_ge(inv_ready, 1)
            pe.matmul(PS[:, 1, 64:65], mean_w[:, :], CNT[:, 0:1], start=True, stop=True).then_inc(tiny_sum, 1)
            pe.wait_ge(xs_ready, 1)
            for h in range(2):
                for k in range(KD):
                    last = pe.matmul(PS[0:2 * N, 2 + h, 0:HALF], bcw[:, k, :], XS[:, k, h * HALF:(h + 1) * HALF],
                                     start=(k == 0), stop=(k == KD - 1))
                last.then_inc(proj, 1)
            pe.wait_ge(s_dw, 16)
            pe.wait_ge(flag_read, 1)
            for g in range(2 * KD):
                m, h = g // 2, g % 2
                if g >= 6:
                    pe.wait_ge(proj_ev, g - 5)
                for k in range(KD):
                    last = pe.matmul(PS[:, (4 + g) % 8, 0:HALF], dw[:, k, m * P:(m + 1) * P],
                                     XS[:, k, h * HALF:(h + 1) * HALF], start=(k == 0), stop=(k == KD - 1))
                last.then_inc(proj, 1)
            pe.wait_ge(proj_ev, 10)
            pe.wait_ge(zero_ready, 1)
            for b in range(8):
                pe.matmul(PS[:, b, 0:HALF], ident[:, :], ZERO, start=True, stop=False)
            pe.sem_inc(v_used, 2)
            with pe.Fori(0, N // 2) as pair:
                n = pair * 2
                for e in range(2):
                    for c in range(KD):
                        pe.wait_ge(v_ready, n * KD + (e * KD + c + 1))
                        for h in range(2):
                            last = pe.matmul(PS[:, 2 * c + h, 0:HALF], ident[:, :], V[:, c % 2, h * HALF:(h + 1) * HALF],
                                             start=False, stop=False)
                        last.then_inc(v_used, 1)
            for b in range(8):
                last = pe.matmul(PS[:, b, 0:HALF], ident[:, :], ZERO, start=False, stop=True)
            last.then_inc(y_ready, 1)
            ln_tensor(pe, 0)
            pe.wait_ge(s_wb, 64)
            for h in range(2):
                pe.wait_ge(ln_out, 1 + h)
                for m in range(KD):
                    for k in range(KD):
                        last = pe.matmul(PS[:, 2 * m + h, 0:HALF], wq0[:, k, m * P:(m + 1) * P],
                                         XT[:, k, h * HALF:(h + 1) * HALF], start=(k == 0), stop=(k == KD - 1))
                    last.then_inc(q0_full, 1)
            pe.wait_ge(q0_read, 2 * KD)

            def qk_tensor(b, prev, e):
                def transposes(j0):
                    for j in range(j0, j0 + 2):
                        pe.wait_ge(pt_free, prev * SJ + (j + 1))
                        for h in range(H0):
                            last = pe.transpose(PS[0:width(j), 4 + j % 2, h * L:(h + 1) * L],
                                                PR[1 - e][:, h, j * P:j * P + width(j)], ident[0:L, 0:L])
                        last.then_inc(pt_full, 1)

                if b is not None:
                    for m in range(KC):
                        slot, bank = m // 2, m % 2
                        if bank == 0:
                            pe.wait_ge(s_free, b * 6 + (slot + 1))
                        for h in range(H0):
                            last = pe.matmul(PS[:, 2 * slot + bank, h * L:(h + 1) * L], wk0w[:, h, m * P:(m + 1) * P],
                                             QT[:, h, bass.ds(b * L, L)], start=True, stop=True)
                        if m in (1, 2):
                            last.then_inc(s_full, 1)
                    pe.wait_ge(s_ct[e], ctx_loads(b, 16, e))
                if prev is not None:
                    pe.wait_ge(pr_ready, prev * H0 + H0)
                for h in range(H0):
                    if b is not None:
                        pe.wait_ge(s_free, b * 6 + max(4, 3 + h))
                        for half in range(2):
                            for k in range(KC):
                                last = pe.matmul(PS[0:L, 2 * (h % 2) + half, 0:SH], QP[e][:, k, h * L:(h + 1) * L],
                                                 CT[e][:, k, half * SH:(half + 1) * SH], start=(k == 0), stop=(k == KC - 1))
                        last.then_inc(s_full, 1)
                    if prev is not None and h < 3:
                        transposes(2 * h)
                if prev is not None:
                    pe.wait_ge(s_cn[1 - e], ctx_loads(prev, 32, 1 - e))
                    pe.wait_ge(pt_free, prev * SJ + (SJ + 2))
                    for m in range(KC):
                        pe.wait_ge(tv_free, prev * 4 + (m + 1))
                        for j in range(SJ):
                            last = pe.matmul(PS[:, 6 + m % 2, 0:H0 * L], CN[1 - e][0:width(j), j, m * P:(m + 1) * P],
                                             PT[0:width(j), j, :], start=(j == 0), stop=(j == SJ - 1))
                        last.then_inc(tv_full, 1)
                    pe.wait_ge(tv_free, prev * 4 + (KC + 2))
                    for h in range(H0):
                        for k in range(KC):
                            last = pe.matmul(PS[:, 7, h * L:(h + 1) * L], wv0[:, k, h * P:(h + 1) * P],
                                             TT[:, k, h * L:(h + 1) * L], start=(k == 0), stop=(k == KC - 1))
                    last.then_inc(tv_full, 1)

            batches(pe, qk_tensor)
            pe.wait_ge(tv_free, B * 4 + 2)
            for h in range(2):
                for m in range(KD):
                    for k in range(KD):
                        last = pe.matmul(PS[:, 2 * m + h, 0:HALF], wo0[:, k, m * P:(m + 1) * P],
                                         CO[:, k, h * HALF:(h + 1) * HALF], start=(k == 0), stop=(k == KD - 1))
                    last.then_inc(o0_full, 1)
            ln_tensor(pe, 1)
            pe.wait_ge(s_gw, 48)
            pe.wait_ge(ln_out, 4)
            for b in range(B):
                for k in range(KD):
                    last = pe.matmul(PS[0:L, 4, b * E:(b + 1) * E], XT[:, k, b * L:(b + 1) * L], gw[:, k, :],
                                     start=(k == 0), stop=(k == KD - 1))
            last.then_inc(lg_full, 1)

            def expert_tensor(e, slot):
                pe.wait_ge(s_we[slot], ctx_loads(e, 48, slot))
                for h in range(2):
                    for m in range(FM):
                        for i, u, us in units(e):
                            if h * FM + m == 3 * i + 4:
                                pe.wait_ge(q_done, u + 1)
                                pe.wait_ge(dn_free, e * 8 + (i + 1))
                                for j in range(4):
                                    last = pe.transpose(PS[:, 4 + i, j * P:(j + 1) * P], RAW[us][:, j * P:(j + 1) * P], ident[:, :])
                                last.then_inc(wt_full, 1)
                        pe.wait_ge(up_free, e * 16 + (h * 8 + m + 1))
                        for w in range(2):
                            for k in range(KD):
                                last = pe.matmul(PS[:, 2 * (m % 2) + w, 0:HALF], WE[slot][w][:, k, m * P:(m + 1) * P],
                                                 XT[:, k, h * HALF:(h + 1) * HALF], start=(k == 0), stop=(k == KD - 1))
                        last.then_inc(up_full, 1)
                    if isinstance(e, int) and h == 0:
                        pe.wait_ge(rt_dve, 2)
                        for b in range(B):
                            last = pe.transpose(PS[0:E, 5 + b // 4, (b % 4) * L:(b % 4 + 1) * L], CM[:, b, :], ident[0:L, 0:L])
                            if b % 4 == 3:
                                last.then_inc(cm_full, 1)
                        pe.wait_ge(cm_read, 2)
                for h in range(2):
                    pe.wait_ge(up_free, e * 16 + (h * 8 + 8 + 2))
                    for m in range(KD):
                        for i, u, us in units(e):
                            if h == 0 and i == m:
                                pe.wait_ge(wt_copied, u + 1)
                        pe.wait_ge(dn_free, e * 8 + (h * 4 + m + 1))
                        for k in range(FM):
                            last = pe.matmul(PS[:, 4 + m, 0:HALF], WE[slot][2][:, k, m * P:(m + 1) * P], HH[h][:, k, :],
                                             start=(k == 0), stop=(k == FM - 1))
                        last.then_inc(dn_full, 1)

            experts(pe, expert_tensor)
            ln_tensor(pe, 2)
            pe.wait_ge(s_wd, 112)
            for which, (w, raw) in enumerate(((wq1, QS), (wk1, R))):
                if which:
                    pe.wait_ge(rot, 2)
                for h in range(2):
                    pe.wait_ge(ln_out, 5 + h)
                    for m in range(KD):
                        for k in range(KD):
                            last = pe.matmul(PS[:, 2 * m + h, 0:HALF], w[:, k, m * P:(m + 1) * P],
                                             XT[:, k, h * HALF:(h + 1) * HALF], start=(k == 0), stop=(k == KD - 1))
                        last.then_inc(qk_full, 1)
                for h in range(2):
                    for m in range(KD):
                        pe.wait_ge(qk_read, 8 * which + h * KD + m + 1)
                        last = pe.matmul(PS[:, 2 * m + h, 0:HALF], perm, raw[:, m, h * HALF:(h + 1) * HALF],
                                         start=True, stop=True)
                last.then_inc(pm_full, 1)
            pe.wait_ge(rot, 5)
            for b in range(B):
                for k in range(KD):
                    last = pe.matmul(PS[0:L, b, :], XT[:, k, b * L:(b + 1) * L], wv1[:, k, :],
                                     start=(k == 0), stop=(k == KD - 1))
                last.then_inc(v1_full, 1)
            pe.wait_ge(v1_read, B)

            def attn1_tensor(b, prev, e):
                if b is not None:
                    pe.wait_ge(qkb, b * 2 + 2)
                    pe.wait_ge(sc_read, b + 2)
                    for c in range(KD):
                        for r in range(4):
                            rows = slice(r * DH, (r + 1) * DH)
                            last = pe.matmul(PS[0:L, r, c * L:(c + 1) * L], QB[e][rows, c, :], KB[e][rows, c, :],
                                             start=True, stop=True)
                    last.then_inc(sc_full, 1)
                if prev is not None:
                    pe.wait_ge(sc_exp, prev + 1)
                    for c in range(KD):
                        pe.wait_ge(p1_free, prev * 4 + (c + 1))
                        for r in range(4):
                            last = pe.transpose(PS[0:L, 4 + c % 2, r * L:(r + 1) * L], SM[1 - e][:, 4 * r + c, :],
                                                ident[0:L, 0:L])
                        last.then_inc(p1_full, 1)
                    pe.wait_ge(p1_free, prev * 4 + 6)
                    for h in range(H1):
                        last = pe.matmul(PS[0:L, 6, h * DH:(h + 1) * DH], PT1[:, h, :],
                                         VV[:, bass.ds(prev, 1), h * DH:(h + 1) * DH], start=True, stop=True)
                    last.then_inc(pv_full, 1)
                    pe.wait_ge(on_ready, prev + 1)
                    pe.wait_ge(ot_free, prev + 1)
                    for c in range(KD):
                        last = pe.transpose(PS[:, 7, c * L:(c + 1) * L], ON[:, c * P:(c + 1) * P], ident[0:L, 0:L])
                    last.then_inc(ot_full, 1)

            batches(pe, attn1_tensor)
            pe.wait_ge(ot_free, B + 1)
            for h in range(2):
                for m in range(KD):
                    for k in range(KD):
                        last = pe.matmul(PS[:, 2 * m + h, 0:HALF], wo1[:, k, m * P:(m + 1) * P],
                                         AO[:, k, h * HALF:(h + 1) * HALF], start=(k == 0), stop=(k == KD - 1))
                    last.then_inc(o1_full, 1)
            ln_tensor(pe, 3)
            def kv_group(b, e, g, bank, first=False):
                if first:
                    wait(pe, k_read, max(0, g - 7))
                elif g == 0:
                    pe.wait_ge(v_read, b * SJ)
                elif g <= 2 * KD:
                    pe.wait_ge(k_read, b * (2 * KD) + g)
                else:
                    pe.wait_ge(v_read, b * SJ + (g - 2 * KD))
                if g == 0:
                    pe.wait_ge(s_cx[e], ctx_loads(b, 16, e))
                if g < 2 * KD:
                    m, half = g // 2, g % 2
                    for k in range(KC):
                        last = pe.matmul(PS[:, bank, 0:SH], xkw[:, k, m * P:(m + 1) * P],
                                         CX[e][:, k, half * SH:(half + 1) * SH], start=(k == 0), stop=(k == KC - 1))
                else:
                    j = g - 2 * KD
                    for k in range(KC):
                        last = pe.matmul(PS[0:width(j), bank, :], CX[e][:, k, j * P:j * P + width(j)], xvw[:, k, :],
                                         start=(k == 0), stop=(k == KC - 1))
                last.then_inc(kv_full, 1)

            pe.wait_ge(s_wx, 64)
            pe.wait_ge(ln_out, 8)
            for g in range(NKV):
                kv_group(0, 0, g, g % 8, first=True)
            pe.wait_ge(k_read, 2 * KD)
            pe.wait_ge(v_read, SJ)
            for h in range(2):
                for m in range(KD):
                    for k in range(KD):
                        last = pe.matmul(PS[:, 2 * m + h, 0:HALF], xqw[:, k, m * P:(m + 1) * P],
                                         XT[:, k, h * HALF:(h + 1) * HALF], start=(k == 0), stop=(k == KD - 1))
                    last.then_inc(qx_full, 1)
            pe.wait_ge(qx_read, 2 * KD)
            pe.wait_ge(pad_ready, 2)

            def xattn_tensor(b, prev, nxt, e):
                for s in range(H1 + 2):
                    if b is not None and s < H1:
                        if s == 0:
                            pe.wait_ge(qbx, b + 1)
                        pe.wait_ge(x_free, b * H1 + (s + 1))
                        rows = slice((s % 4) * DH, (s % 4 + 1) * DH)
                        for half in range(2):
                            last = pe.matmul(PS[0:L, 2 * (s % 2) + half, 0:SH], QBX[e][rows, s // 4, :],
                                             KX[e][rows, s // 4, half * SH:(half + 1) * SH], start=True, stop=True)
                        last.then_inc(x_full, 1)
                    if prev is not None and s == 2:
                        pe.wait_ge(ox_norm, prev + 1)
                        if nxt is not None:
                            pe.wait_ge(k_read, nxt * (2 * KD) + 2)
                        else:
                            pe.wait_ge(v_read, B * SJ)
                            pe.wait_ge(otx_free, prev)
                        for c in range(KD):
                            last = pe.transpose(PS[:, 7, c * L:(c + 1) * L], OX[1 - e][:, c * P:(c + 1) * P], ident[0:L, 0:L])
                        last.then_inc(otx_full, 1)
                    if nxt is not None and s in GROUP_AT:
                        if prev is not None and s == 2:
                            pe.wait_ge(otx_free, prev + 1)
                        kv_group(nxt, 1 - e, GROUP_AT[s], 7)
                    if b is not None and 1 <= s <= H1:
                        h = s - 1
                        pe.wait_ge(x_free, b * H1 + (h + 3))
                        for p in range(2):
                            pe.wait_ge(ptx_free, b * (2 * H1) + (2 * h + p + 1))
                            for j in range(3):
                                last = pe.transpose(PS[:, 4 + p, j * L:(j + 1) * L],
                                                    PX[h % 2][:, (3 * p + j) * P:(3 * p + j + 1) * P], ident[0:L, 0:L])
                            last.then_inc(ptx_full, 1)
                    if b is not None and s >= 2:
                        h = s - 2
                        if h == 0:
                            wait(pe, ox_norm, b)
                        pe.wait_ge(ptx_free, b * (2 * H1) + (2 * h + 4))
                        for j in range(SJ):
                            last = pe.matmul(PS[0:L, 6, h * DH:(h + 1) * DH], PTX[h % 2][0:width(j), j, :],
                                             VX[e][0:width(j), j, h * DH:(h + 1) * DH], start=(j == 0), stop=(j == SJ - 1))
                        if h == H1 - 1:
                            last.then_inc(ox_full, 1)

            xbatches(pe, xattn_tensor)
            pe.wait_ge(s_wm, 32)
            pe.wait_ge(otx_free, B)
            for h in range(2):
                for m in range(2 * KD):
                    g = h * 2 * KD + m
                    wait(pe, mx_free, max(0, g - 7))
                    for k in range(KD):
                        last = pe.matmul(PS[:, g % 8, 0:HALF], w1x[:, k, m * P:(m + 1) * P],
                                         AO2[:, k, h * HALF:(h + 1) * HALF], start=(k == 0), stop=(k == KD - 1))
                    last.then_inc(mx_full, 1)
            pe.wait_ge(mx_free, 4 * KD)
            for h in range(2):
                for m in range(KD):
                    for k in range(2 * KD):
                        last = pe.matmul(PS[:, 2 * m + h, 0:HALF], w2x[:, k, m * P:(m + 1) * P],
                                         HX[:, k, h * HALF:(h + 1) * HALF], start=(k == 0), stop=(k == 2 * KD - 1))
                    last.then_inc(m2_full, 1)
            ln_tensor(pe, 4)
            pe.wait_ge(s_wt, 48)

            def ffn_tensor(a, g, d, piece, e):
                if a is not None:
                    pe.wait_ge(xb_ready, a + 1)
                    if g is not None:
                        pe.wait_ge(xq_read, g + 1)
                    pe.wait_ge(hq_read, piece_of_hq(a, g) + 1)
                    for k in range(KD):
                        last = pe.transpose(PS[:, 6, k * P:(k + 1) * P], XB[1 - e][:, k, :], ident[:, :])
                    last.then_inc(xk_full, 1)
                if g is not None:
                    pe.wait_ge(xq_read, g + 1)
                    for p, (c0, n) in enumerate(PARTS):
                        wait(pe, gu_free, g * 3 + p - 2 if not isinstance(g, int) or g else 0)
                        for w, view in enumerate((WGv, WUv)):
                            for k in range(KD):
                                last = pe.matmul(PS[:, 2 * p + w, 0:n], XQT[e][:, k, :], view[:, k, c0 // P:(c0 + n) // P, :],
                                                 start=(k == 0), stop=(k == KD - 1))
                        last.then_inc(gu_full, 1)
                if d is not None:
                    for p, (c0, n) in enumerate(PARTS):
                        pe.wait_ge(q_done, piece + (p + 1))
                        if p == 0:
                            if a is not None:
                                pe.wait_ge(xk_read, a + 1)
                        else:
                            pe.wait_ge(hq_read, d * 3 + p + 1)
                        for i in range(n // P):
                            last = pe.transpose(PS[:, 6, i * P:(i + 1) * P], HQ[:, c0 + i * P:c0 + (i + 1) * P], ident[:, :])
                        last.then_inc(hq_full, 1)
                    pe.wait_ge(hq_read, d * 3 + 4)
                    pe.wait_ge(f_sum, d + 1)
                    for m in range(I4M):
                        last = pe.matmul(PS[:, 7, :], HQT[:, m, :], WDv[:, m, :, :], start=(m == 0), stop=(m == I4M - 1))
                    last.then_inc(y_full, 1)
                if a is not None:
                    pe.wait_ge(q_done, piece + (1 if d is None else 4))
                    pe.wait_ge(xk_read, a + 1)
                    for k in range(KD):
                        last = pe.transpose(PS[:, 6, k * P:(k + 1) * P], XQ[:, k * P:(k + 1) * P], ident[:, :])
                    last.then_inc(xq_full, 1)

            def piece_of_hq(a, g):
                return 0 if g is None or isinstance(g, int) and g < 2 else g * 3 - 3

            tiles(pe, ffn_tensor)

        @block.scalar
        def _(act):
            act.wait_ge(s_wa, 96)
            act.wait_ge(gate_pe, 1)
            act.activation(TH, PS[0:N, 0, 0:B], ACT.Tanh, bias=sm[:, 2:3]).then_inc(gate_act, 1)
            act.wait_ge(gate_pe, 2)
            act.wait_ge(s_consts, 64)
            for c in range(KD):
                act.activation(SEL[:, c, :], PS[:, 1, c * B:(c + 1) * B], ACT.Sigmoid,
                               bias=col("sel_b", c)).then_inc(gate_act, 1)
            act.activation(AA, ALOG, ACT.Exp).then_inc(a_ready, 1)
            for h in range(2):
                act.wait_ge(proj, 1 + h)
                act.activation(BCS[:, h * HALF:(h + 1) * HALF], PS[0:2 * N, 2 + h, 0:HALF], ACT.Identity,
                               bias=bcbias).then_inc(proj_ev, 1)
            act.wait_ge(inv_ready, 1)
            for g in range(2 * KD):
                m, h = g // 2, g % 2
                act.wait_ge(proj, 3 + g)
                act.activation(DL[:, m, h * HALF:(h + 1) * HALF], PS[:, (4 + g) % 8, 0:HALF], ACT.Identity,
                               bias=DB[:, m:m + 1]).then_inc(proj_ev, 1)
            act.wait_ge(sp_dve, 1)
            act.activation(SP1, SP1, ACT.Exp).then_inc(sp_act, 1)
            act.wait_ge(sp_dve, 2)
            act.activation(SP3, SP2, ACT.Ln).then_inc(sp_act, 1)
            act.wait_ge(sp_dve, 4)
            with act.Fori(0, N // 2) as pair:
                n = pair * 2
                for e in range(2):
                    for c in range(KD):
                        act.wait_ge(ad_free, n * KD + (e * KD + c + 1))
                        act.nop()
                        act.activation(AD[:, c % 2, :], DL[:, c, :], ACT.Exp,
                                       scale=AA[:, c, bass.ds(n + e, 1)]).then_inc(ad_ready, 1)
            ln_scalar(act, 0)
            for h in range(2):
                for m in range(KD):
                    act.wait_ge(q0_full, h * KD + m + 1)
                    act.activation(QT[:, m, h * HALF:(h + 1) * HALF], PS[:, 2 * m + h, 0:HALF], ACT.Copy,
                                   scale=float(D // H0) ** -0.5).then_inc(q0_read, 1)
            act.sem_inc(s_free, 2)
            act.sem_inc(tv_free, 2)

            def qk_scalar(b, prev, e):
                if b is not None:
                    act.wait_ge(s_full, b * 6 + 1)
                    act.activation(QP[e][:, 0:2, :], PS[:, 0:2, 0:H0 * L], ACT.Copy).then_inc(s_free, 1)
                    act.wait_ge(s_full, b * 6 + 2)
                    act.activation(QP[e][:, 2, :], PS[:, 2, 0:H0 * L], ACT.Copy).then_inc(s_free, 1)
                    for h in range(H0):
                        act.wait_ge(nm_ready, b * H0 + (h + 1))
                        act.activation(PR[e][:, h, :].rearrange("p (a s) -> p a s", a=2),
                                       PS[0:L, 2 * (h % 2):2 * (h % 2) + 2, 0:SH], ACT.Exp, bias=ST[e][:, 0, h:h + 1],
                                       accum_out=ST[e][:, 1, h:h + 1]).then_inc(s_free, 1)
                if prev is not None:
                    for m in range(KC):
                        act.wait_ge(tv_full, prev * 4 + (m + 1))
                        act.activation(TT[:, m, :], PS[:, 6 + m % 2, 0:H0 * L], ACT.Copy).then_inc(tv_free, 1)
                    act.wait_ge(tv_full, prev * 4 + (KC + 1))
                    act.activation(CO[:, :, bass.ds(prev * L, L)], PS[:, 7, 0:H0 * L].rearrange("p (h q) -> p h q", h=H0),
                                   ACT.Copy).then_inc(tv_free, 1)

            batches(act, qk_scalar)
            ln_scalar(act, 1)
            act.wait_ge(rt_dve, 1)
            act.activation(SC, SC, ACT.Exp).then_inc(rt_exp, 1)

            def quant_scalar(piece, scaled, magnitude, sign):
                act.wait_ge(q_scaled, piece + 1)
                act.activation(magnitude, scaled, ACT.Abs).then_inc(q_abs, 1)
                act.activation(sign, scaled, ACT.Sign).then_inc(q_sign, 1)

            def expert_scalar(e, slot):
                for h in range(2):
                    for m in range(FM):
                        for i, u, us in units(e):
                            if h * FM + m == 3 * i + 4:
                                act.wait_ge(wt_full, u + 1)
                                act.wait_ge(s_wst[us], ctx_loads(u, 16, us))
                                act.activation(WTS[us], PS[:, 4 + i, :], ACT.Copy).then_inc(wt_copied, 1)
                        act.wait_ge(up_full, e * 16 + (h * 8 + m + 1))
                        act.activation(SIL[:, m % 2, :], PS[:, 2 * (m % 2), 0:HALF], ACT.Silu).then_inc(sil_ready, 1)
                        for i, u, us in units(e):
                            if h * FM + m == 3 * i + 1:
                                quant_scalar(u, RAW[us], UA, US)
                    if isinstance(e, int) and h == 0:
                        for half in range(2):
                            act.wait_ge(cm_full, half + 1)
                            act.activation(CBT[:, half * HALF:(half + 1) * HALF], PS[0:E, 5 + half, 0:HALF],
                                           ACT.Copy).then_inc(cm_read, 1)

            experts(act, expert_scalar)
            ln_scalar(act, 2)
            for which, raw in enumerate((QS, R)):
                for h in range(2):
                    for m in range(KD):
                        act.wait_ge(qk_full, 8 * which + h * KD + m + 1)
                        act.activation(raw[:, m, h * HALF:(h + 1) * HALF], PS[:, 2 * m + h, 0:HALF],
                                       ACT.Copy).then_inc(qk_read, 1)
            for b in range(B):
                act.wait_ge(v1_full, b + 1)
                act.activation(VV[:, b, :], PS[0:L, b, :], ACT.Copy).then_inc(v1_read, 1)
            act.sem_inc(p1_free, 2)
            act.sem_inc(ot_free, 1)

            def attn1_scalar(b, prev, e):
                if prev is not None:
                    for c in range(KD):
                        act.wait_ge(p1_full, prev * 4 + (c + 1))
                        act.activation(PT1[:, 4 * c:4 * c + 4, :], PS[0:L, 4 + c % 2, 0:4 * L].rearrange(
                            "p (r q) -> p r q", r=4), ACT.Copy).then_inc(p1_free, 1)
                if b is not None:
                    act.wait_ge(sc_dve, b * 2 + 2)
                    act.activation(SM[e], SM[e], ACT.Exp, scale=float(DH) ** -0.5).then_inc(sc_exp, 1)
                if prev is not None:
                    act.wait_ge(ot_full, prev + 1)
                    act.activation(AO[:, :, bass.ds(prev * L, L)], PS[:, 7, 0:KD * L].rearrange("p (c q) -> p c q", c=KD),
                                   ACT.Copy).then_inc(ot_free, 1)

            batches(act, attn1_scalar)
            ln_scalar(act, 3)
            def keys_scalar(b, e, g, bank):
                if g < 2 * KD:
                    m, half = g // 2, g % 2
                    act.wait_ge(kv_full, b * NKV + (g + 1))
                    act.activation(KX[e][:, m, half * SH:(half + 1) * SH], PS[:, bank, 0:SH], ACT.Identity,
                                   bias=col("bk", m)).then_inc(k_read, 1)

            for g in range(NKV):
                keys_scalar(0, 0, g, g % 8)
            act.sem_inc(x_free, 2)

            def xattn_scalar(b, prev, nxt, e):
                for s in range(H1 + 2):
                    if b is not None and s < H1:
                        act.wait_ge(nmx, b * H1 + (s + 1))
                        wait(act, ptx_free, b * (2 * H1) + 2 * s)
                        act.activation(PX[s % 2][:, 0:S].rearrange("p (a s) -> p a s", a=2),
                                       PS[0:L, 2 * (s % 2):2 * (s % 2) + 2, 0:SH], ACT.Exp, bias=SX[e][:, 0, s:s + 1],
                                       accum_out=SX[e][:, 1, s:s + 1]).then_inc(x_free, 1)
                    if prev is not None and s == 2:
                        act.wait_ge(otx_full, prev + 1)
                        act.activation(AO2[:, :, bass.ds(prev * L, L)], PS[:, 7, 0:KD * L].rearrange(
                            "p (c q) -> p c q", c=KD), ACT.Copy).then_inc(otx_free, 1)
                    if nxt is not None and s in GROUP_AT:
                        keys_scalar(nxt, 1 - e, GROUP_AT[s], 7)

            xbatches(act, xattn_scalar)
            for h in range(2):
                for m in range(2 * KD):
                    g = h * 2 * KD + m
                    act.wait_ge(mx_full, g + 1)
                    act.activation(HX[:, m, h * HALF:(h + 1) * HALF], PS[:, g % 8, 0:HALF], ACT.Relu,
                                   bias=col("b1", m)).then_inc(mx_free, 1)
            ln_scalar(act, 4)
            act.sem_inc(hq_read, 1)

            def ffn_scalar(a, g, d, piece, e):
                if a is not None:
                    act.wait_ge(xk_full, a + 1)
                    act.activation(XK[:, bass.ds(a, 1), :], PS[:, 6:7, :], ACT.Copy).then_inc(xk_read, 1)
                for p, (c0, n) in enumerate(PARTS):
                    if d is not None:
                        quant_scalar(piece + p, XN[:, 0:n], AB[:, 0:n], SG[:, 0:n])
                    if g is not None:
                        act.wait_ge(gu_full, g * 3 + (p + 1))
                        wait(act, gu_free, g * 3 + p - 1 if not isinstance(g, int) or 3 * g + p > 1 else 0)
                        act.activation(SI[:, p % 2, 0:n], PS[:, 2 * p, 0:n], ACT.Silu).then_inc(si_ready, 1)
                if a is not None:
                    quant_scalar(piece + (0 if d is None else 3), XN, AB, SG)
                if d is not None:
                    for p, (c0, n) in enumerate(PARTS):
                        act.wait_ge(hq_full, d * 3 + (p + 1))
                        act.activation(HQT[:, c0 // P:(c0 + n) // P, :], PS[:, 6, 0:n].rearrange("p (i q) -> p i q", q=P),
                                       ACT.Copy).then_inc(hq_read, 1)
                if a is not None:
                    act.wait_ge(xq_full, a + 1)
                    act.activation(XQT[1 - e], PS[:, 6, :].rearrange("p (k q) -> p k q", k=KD), ACT.Copy).then_inc(xq_read, 1)
                if d is not None:
                    act.wait_ge(f_cen, d + 1)
                    act.activation(YS, YR[1 - e], ACT.Square, accum_out=LS[1 - e][:, 2:3]).then_inc(f_var, 1)
                    act.wait_ge(f_var, d * 2 + 1)
                    act.activation(LS[1 - e][:, 3:4], LS[1 - e][:, 2:3], ACT.Sqrt, scale=1.0 / D,
                                   bias=eps_c[:, 0:1]).then_inc(f_var, 1)

            tiles(act, ffn_scalar)

        @block.gpsimd
        def _(pool):
            pool.memset(eps_c[:, :], LN_EPS)
            pool.memset(ZERO, 0.0).then_inc(zero_ready, 1)
            pool.wait_ge(sp_dve, 4)
            with pool.Fori(0, N // 2) as pair:
                n = pair * 2
                for e in range(2):
                    pool.wait_ge(s_bc[e], n * 16 + 32)
                    for c in range(KD):
                        pool.wait_ge(w_done, n * KD + (e * KD + c + 1))
                        pool.tensor_tensor(U[:, c % 2, :], XS[:, c, :], BC[:, e, 0, :], ALU.mult).then_inc(u_ready, 1)
            pool.wait_ge(tv_free, B * 4 + 2)
            pool.wait_ge(ln_out, 4)
            pool.memset(ONE, 1.0).then_inc(one_ready, 1)
            pool.tensor_copy(R[:, :, :], XT[:, :, :]).then_inc(r_copied, 1)
            pool.wait_ge(r_copied, 1)
            pool.sem_inc(acc, 4)

            def quant_pool(piece, n, sign, scale, signed):
                pool.wait_ge(q_sign, piece + 1)
                pool.tensor_tensor(signed[:, 0:n].rearrange("p (b i) -> p b i", i=16), sign[:, 0:n].rearrange("p (b i) -> p b i", i=16),
                                   scale[:, 0:n // 16].unsqueeze(2).to_broadcast([P, n // 16, 16]), ALU.mult).then_inc(q_ss, 1)

            def expert_pool(e, slot):
                for i, u, us in units(e):
                    quant_pool(u, D, US, UC, US)
                for h in range(2):
                    for m in range(KD):
                        rows = R[:, m, h * HALF:(h + 1) * HALF]
                        pool.wait_ge(dn_free, e * 8 + (h * 4 + m + 5))
                        pool.tensor_tensor(rows, rows, TMP[:, m, :], ALU.add).then_inc(acc, 1)

            experts(pool, expert_pool)
            pool.wait_ge(acc, 8 * (E + 1) + 4)
            pool.sem_inc(ln_in, 2)
            pool.wait_ge(rot, 6)

            def attn1_pool(b, prev, e):
                if b is not None:
                    pool.wait_ge(sc_read, b + 1)
                    pool.tensor_copy(QB[e], QR[:, :, bass.ds(b * L, L)]).then_inc(qkb, 1)
                    pool.tensor_copy(KB[e], KR[:, :, bass.ds(b * L, L)]).then_inc(qkb, 1)

            batches(pool, attn1_pool)
            pool.wait_ge(o1_full, 2 * KD)
            for e in range(2):
                pool.memset(PX[e][:, S:SJ * P], 0.0).then_inc(pad_ready, 1)
            pool.wait_ge(qx_read, 2 * KD)

            def xattn_pool(b, prev, nxt, e):
                if b is not None:
                    if not isinstance(b, int) or b:
                        pool.wait_ge(x_free, b * H1 - (H1 - 2))
                    pool.tensor_copy(QBX[e], QX[:, :, bass.ds(b * L, L)]).then_inc(qbx, 1)

            xbatches(pool, xattn_pool)
            pool.wait_ge(ln_out, 10)
            pool.memset(XP[:, :, T:NT * P], 0.0).then_inc(xp_ready, 1)
            pool.tensor_copy(XP[:, :, 0:T], XT[:, :, :]).then_inc(xp_ready, 1)
            pool.wait_ge(xp_ready, 2)

            def ffn_pool(a, g, d, piece, e):
                if a is not None:
                    if g is not None:
                        pool.wait_ge(xk_full, g + 1)
                    pool.tensor_copy(XB[1 - e], XP[:, :, bass.ds(a * P, P)]).then_inc(xb_ready, 1)
                if d is not None:
                    for p, (c0, n) in enumerate(PARTS):
                        quant_pool(piece + p, n, SG, SCL, SS)
                if a is not None:
                    quant_pool(piece + (0 if d is None else 3), D, SG, SCL, SS)

            tiles(pool, ffn_pool)

        @block.vector
        def _(v):
            def link(ins):
                dve.inc(ins)
                v.wait_ge(dve.sem, dve.n)

            v.wait_ge(s_x, 16)
            v.wait_ge(s_wa, 96)
            link(v.reduce_sum(GC, XT[:, :, :].rearrange("p k (b t) -> p (k b) t", b=B), AX))
            link(v.tensor_copy(CUR8, sm[:, 4:5].to_broadcast([N, B])))
            v.tensor_scalar(GC, GC, 1.0 / L, None, ALU.mult).then_inc(gc_ready, 1)
            link(v.tensor_scalar(TAU[:, 0:1], sm[:, 3:4], 0.1, 10.0, ALU.max, ALU.min))
            link(v.reciprocal(TAU[:, 1:2], TAU[:, 0:1]))
            v.wait_ge(gate_act, 1)
            link(v.tensor_tensor(TH, TH, CUR8, ALU.subtract))
            link(v.tensor_scalar(TH, TH, TAU[:, 1:2], 0.1, ALU.mult, ALU.mult))
            v.tensor_tensor(H8, TH, CUR8, ALU.add).then_inc(newh_ready, 1)
            v.wait_ge(gate_act, 1 + KD)
            for c in range(KD):
                last = v.tensor_tensor(XS[:, c, :].rearrange("p (b t) -> p b t", b=B),
                                       XT[:, c, :].rearrange("p (b t) -> p b t", b=B),
                                       SEL[:, c, :].unsqueeze(2).to_broadcast([P, B, L]), ALU.mult)
            last.then_inc(xs_ready, 1)
            v.wait_ge(s_consts, 64)
            v.wait_ge(a_ready, 1)
            link(v.tensor_scalar(KEEP, AA, TINY_A, None, ALU.is_ge))
            link(v.tensor_scalar(TINY, KEEP, -1.0, 1.0, ALU.mult, ALU.add))
            link(v.tensor_scalar(AA, AA, -1.0, None, ALU.mult))
            link(v.tensor_tensor(INV, AA, KEEP, ALU.mult))
            link(v.tensor_tensor(INV, INV, TINY, ALU.add))
            link(v.reciprocal(INV, INV))
            link(v.tensor_tensor(DB, vec[:, VEC["delta_b"][0]:VEC["delta_b"][0] + KD],
                                 vec[:, VEC["dt_bias"][0]:VEC["dt_bias"][0] + KD], ALU.add))
            v.reduce_sum(CNT[:, 0:1], TINY.rearrange("p k n -> p (k n)"), AX).then_inc(inv_ready, 1)
            v.wait_ge(tiny_sum, 1)
            v.tensor_scalar(FLAG[:, :], PS[:, 1, 64:65], 0.0, None, ALU.is_gt).then_inc(flag_read, 1)
            v.wait_ge(flag_read, 1)
            any_tiny = v.value_load(FLAG[0:1, 0:1])
            v.wait_ge(proj_ev, 10)
            v.scalar_tensor_tensor(SP1, DL, -1.0, DL, ALU.mult, ALU.min).then_inc(sp_dve, 1)
            v.wait_ge(sp_act, 1)
            v.tensor_scalar(SP2, SP1, 1.0, None, ALU.add).then_inc(sp_dve, 1)
            v.wait_ge(sp_dve, 2)
            link(v.scalar_tensor_tensor(SP1, SP2, -1.0, SP1, ALU.add, ALU.subtract))
            v.wait_ge(sp_act, 2)
            link(v.reciprocal(SP2, SP2))
            v.tensor_tensor(SP1, SP1, SP2, ALU.mult).then_inc(sp_dve, 1)
            v.wait_ge(sp_dve, 3)
            link(v.scalar_tensor_tensor(DL, DL, 0.0, SP1, ALU.max, ALU.subtract))
            v.tensor_tensor(DL, DL, SP3, ALU.add).then_inc(sp_dve, 1)
            v.wait_ge(sp_dve, 4)
            v.sem_inc(ad_free, 2)
            v.sem_inc(w_done, 2)
            with v.Fori(0, N // 2) as pair:
                n = pair * 2
                for e in range(2):
                    for c in range(KD):
                        t = n * KD + (e * KD + c + 1)
                        r = c % 2
                        with v.If(any_tiny > 0):
                            v.wait_ge(ad_ready, t)
                            v.wait_ge(u_ready, t)
                            v.wait_ge(v_used, t)
                            v.tensor_scalar(HS[:, r, :], AD[:, r, :], -1.0, KEEP[:, c, bass.ds(n + e, 1)],
                                            ALU.add, ALU.mult).then_inc(tiny_s, 1)
                            v.wait_ge(tiny_s, 2 * t - 1)
                            v.nop()
                            v.scalar_tensor_tensor(HS[:, r, :], DL[:, c, :], TINY[:, c, bass.ds(n + e, 1)],
                                                   HS[:, r, :], ALU.mult, ALU.add).then_inc(tiny_s, 1)
                            v.wait_ge(tiny_s, 2 * t)
                            v.tensor_tensor(W[:, r, :], HS[:, r, :], U[:, r, :], ALU.mult).then_inc(w_done, 1)
                        with v.Else():
                            v.wait_ge(ad_ready, t)
                            v.wait_ge(u_ready, t)
                            v.wait_ge(v_used, t)
                            v.scalar_tensor_tensor(W[:, r, :], AD[:, r, :], -1.0, U[:, r, :], ALU.add, ALU.mult)\
                                .then_inc(w_done, 1)
                        v.wait_ge(w_done, t + 2)
                        v.memset(AD[:, r, 0:T:L], 0.0).then_inc(rz, 1)
                        v.wait_ge(rz, t)
                        v.tensor_tensor_scan(HS[:, r, :], AD[:, r, :], W[:, r, :], 0.0, ALU.mult, ALU.add)\
                            .then_inc(ad_free, 1)
                        v.wait_ge(ad_free, t + 2)
                        v.scalar_tensor_tensor(V[:, r, :], HS[:, r, :], INV[:, c, bass.ds(n + e, 1)],
                                               BC[:, e, 1, :], ALU.mult, ALU.mult).then_inc(v_ready, 1)
            v.wait_ge(y_ready, 1)
            for h in range(2):
                part = slice(h * HALF, (h + 1) * HALF)
                v.tensor_tensor(R[:, :, part], XT[:, :, part], PS[:, h:8:2, 0:HALF], ALU.add).then_inc(ln_in, 1)
            ln_vector(v, 0)
            v.sem_inc(pt_free, 2)

            def qk_vector(b, prev, e):
                def norm(h):
                    v.wait_ge(s_free, b * 6 + (h + 5))
                    v.reciprocal(ST[e][:, 2, h:h + 1], ST[e][:, 1, h:h + 1]).then_inc(rs_ready, 1)
                    v.wait_ge(rs_ready, b * H0 + (h + 1))
                    v.tensor_scalar(PR[e][:, h, :], PR[e][:, h, :], ST[e][:, 2, h:h + 1], None, ALU.mult)\
                        .then_inc(pr_ready, 1)

                for h in range(H0):
                    if b is not None:
                        v.wait_ge(s_full, b * 6 + (h + 3))
                        v.tensor_reduce(ST[e][:, 0, h:h + 1], PS[0:L, 2 * (h % 2):2 * (h % 2) + 2, 0:SH],
                                        mybir.AxisListType.XY, ALU.max, negate=True).then_inc(nm_ready, 1)
                        if h:
                            norm(h - 1)
                    if prev is not None and h < 3:
                        for j in range(2 * h, 2 * h + 2):
                            v.wait_ge(pt_full, prev * SJ + (j + 1))
                            v.tensor_copy(PT[0:width(j), j, :], PS[0:width(j), 4 + j % 2, 0:H0 * L]).then_inc(pt_free, 1)
                if b is not None:
                    norm(H0 - 1)

            batches(v, qk_vector)
            for h in range(2):
                part = slice(h * HALF, (h + 1) * HALF)
                for m in range(KD):
                    v.wait_ge(o0_full, h * KD + m + 1)
                    last = v.scalar_tensor_tensor(R[:, m, part], PS[:, 2 * m + h, 0:HALF], col("bo", m), XT[:, m, part],
                                                  ALU.add, ALU.add)
                last.then_inc(ln_in, 1)
            ln_vector(v, 1)
            def spread(x):
                return x.unsqueeze(2).to_broadcast([L, B, E])

            def biases(x):
                return x[0:L, :].unsqueeze(1).to_broadcast([L, B, E])

            v.wait_ge(lg_full, 1)
            v.wait_ge(s_gw, 48)
            logits = PS[0:L, 4, 0:B * E].rearrange("p (b e) -> p b e", b=B)
            link(v.reduce_max(GS[:, 0, :], logits, AX))
            v.tensor_tensor(SC, logits, spread(GS[:, 0, :]), ALU.subtract).then_inc(rt_dve, 1)
            v.wait_ge(rt_exp, 1)
            link(v.reduce_sum(GS[:, 1, :], SC, AX))
            link(v.reciprocal(GS[:, 1, :], GS[:, 1, :]))
            link(v.tensor_tensor(SC, SC, spread(GS[:, 1, :]), ALU.mult))
            link(v.tensor_tensor(BI, SC, biases(gb), ALU.add))
            for best in range(2):
                link(v.reduce_max(GS[:, 2, :], BI, AX))
                link(v.tensor_tensor(KEY, BI, spread(GS[:, 2, :]), ALU.is_equal))
                link(v.tensor_tensor(KEY, KEY, biases(rank), ALU.mult))
                link(v.reduce_max(GS[:, 3, :], KEY, AX))
                link(v.tensor_tensor(OH, KEY, spread(GS[:, 3, :]), ALU.is_equal))
                if best == 0:
                    link(v.tensor_copy(CM, OH))
                    link(v.scalar_tensor_tensor(BI, OH, NEG, BI, ALU.mult, ALU.add))
            link(v.tensor_tensor(CM, CM, OH, ALU.add))
            v.tensor_tensor(CM, CM, SC, ALU.mult).then_inc(rt_dve, 1)
            v.sem_inc(up_free, 2)
            v.sem_inc(dn_free, 4)

            def quant_vector(piece, src, dst, n, places, part):
                scaled, magnitude, signed, low, high, largest, scale, rscale = places

                def blocks(x):
                    return x.rearrange("p (b i) -> p b i", i=16)

                def step(j, ins):
                    ins.then_inc(q_scale if j < 3 else q_steps, 1)

                def after(j):
                    if j < 3:
                        v.wait_ge(q_scale, piece * 3 + (j + 1))
                    else:
                        v.wait_ge(q_steps, piece * 8 + (j - 2))

                nb, ab, qg, qh = n // 16, magnitude[:, 0:n], low[:, 0:n], high[:, 0:n]
                am, sc, ri = largest[:, 0:nb], scale[:, 0:nb], rscale[:, 0:nb]
                if part == 0:
                    if not isinstance(piece, int) or piece:
                        v.wait_ge(q_done, piece)
                    step(0, v.tensor_reduce(am, blocks(src), AX, ALU.max, apply_absolute_value=True))
                    after(0)
                    step(1, v.tensor_scalar(sc, am, 1.0 / 6.0, 1e-12, ALU.mult, ALU.max))
                    after(1)
                    step(2, v.reciprocal(ri, sc))
                    after(2)
                    v.tensor_tensor(blocks(scaled[:, 0:n]), blocks(src), ri.unsqueeze(2).to_broadcast([P, nb, 16]), ALU.mult)\
                        .then_inc(q_scaled, 1)
                elif part == 1:
                    v.wait_ge(q_abs, piece + 1)
                    step(3, v.tensor_scalar(qg, ab, 0.25, None, ALU.is_gt))
                    step(4, v.tensor_scalar(qh, ab, 5.0, 2.0, ALU.is_gt, ALU.mult))
                    after(3)
                    step(5, v.scalar_tensor_tensor(qg, ab, 0.75, qg, ALU.is_gt, ALU.add))
                    after(4)
                    step(6, v.scalar_tensor_tensor(qh, ab, 2.5, qh, ALU.is_gt, ALU.add))
                else:
                    after(5)
                    step(7, v.scalar_tensor_tensor(qg, ab, 1.25, qg, ALU.is_gt, ALU.add))
                    after(6)
                    step(8, v.scalar_tensor_tensor(qh, ab, 3.5, qh, ALU.is_gt, ALU.add))
                    after(7)
                    step(9, v.scalar_tensor_tensor(qg, ab, 1.75, qg, ALU.is_gt, ALU.add))
                    after(9)
                    step(10, v.scalar_tensor_tensor(qg, qh, 2.0, qg, ALU.mult, ALU.add))
                    after(10)
                    v.wait_ge(q_ss, piece + 1)
                    v.scalar_tensor_tensor(dst, qg, 0.5, signed[:, 0:n], ALU.mult, ALU.mult).then_inc(q_done, 1)

            def expert_vector(e, slot):
                for h in range(2):
                    for m in range(FM):
                        v.wait_ge(sil_ready, e * 16 + (h * 8 + m + 1))
                        v.tensor_tensor(HH[h][:, m, :], PS[:, 2 * (m % 2) + 1, 0:HALF], SIL[:, m % 2, :], ALU.mult)\
                            .then_inc(up_free, 1)
                        for i, u, us in units(e):
                            if (h * FM + m) // 3 == i:
                                if (h * FM + m) % 3 == 0:
                                    v.wait_ge(s_raw[us], ctx_loads(u, 16, us))
                                quant_vector(u, RAW[us], RAW[us], D, (RAW[us], UA, US, UG, UH, UM, UC, UR), (h * FM + m) % 3)
                v.wait_ge(s_cb[slot], ctx_loads(e, 16, slot))
                for h in range(2):
                    for m in range(KD):
                        v.wait_ge(dn_full, e * 8 + (h * 4 + m + 1))
                        v.wait_ge(acc, e * 8 + (h * 4 + m + 1))
                        v.tensor_tensor(TMP[:, m, :], PS[:, 4 + m, 0:HALF], CB[slot][:, h * HALF:(h + 1) * HALF], ALU.mult)\
                            .then_inc(dn_free, 1)

            experts(v, expert_vector)
            ln_vector(v, 2)
            v.wait_ge(s_wd, 112)
            for which, (raw, out) in enumerate(((QS, QR), (R[:, :, :], KR))):
                v.wait_ge(qk_read, 8 * which + 8)
                v.tensor_tensor(out.rearrange("p m (b t) -> p (m b) t", t=L), raw.rearrange("p m (b t) -> p (m b) t", t=L),
                                rope[:, 0:L].unsqueeze(1).to_broadcast([P, KD * B, L]), ALU.mult).then_inc(rot, 1)
                v.wait_ge(pm_full, which + 1)
                v.wait_ge(rot, 3 * which + 1)
                v.tensor_tensor(SQ[:, :, :].rearrange("p m (h b t) -> p (m h) b t", h=2, t=L),
                                PS[:, :, 0:HALF].rearrange("p g (b t) -> p g b t", t=L),
                                rope[:, L:2 * L].unsqueeze(1).unsqueeze(1).to_broadcast([P, 2 * KD, B // 2, L]),
                                ALU.mult).then_inc(rot, 1)
                v.wait_ge(rot, 3 * which + 2)
                v.tensor_tensor(out, out, SQ[:, :, :], ALU.add).then_inc(rot, 1)
            v.sem_inc(sc_read, 2)

            def attn1_vector(b, prev, e):
                if b is not None:
                    v.wait_ge(sc_full, b + 1)
                    v.tensor_tensor(SM[e].rearrange("p (r c) k -> p r c k", r=4),
                                    PS[0:L, 0:4, 0:4 * L].rearrange("p r (c k) -> p r c k", c=4),
                                    causal.unsqueeze(1).unsqueeze(1).to_broadcast([L, 4, 4, L]), ALU.add)\
                        .then_inc(sc_read, 1)
                    v.wait_ge(sc_read, b + 3)
                    v.reduce_max(S1[e][:, 0, :], SM[e], AX).then_inc(sc_dve, 1)
                    v.wait_ge(sc_dve, b * 2 + 1)
                    v.tensor_tensor(SM[e], SM[e], S1[e][:, 0, :].unsqueeze(2).to_broadcast([L, H1, L]), ALU.subtract)\
                        .then_inc(sc_dve, 1)
                if prev is not None:
                    v.wait_ge(pv_full, prev + 1)
                    v.tensor_tensor(ON.rearrange("p (c r d) -> p c r d", c=4, r=4),
                                    PS[0:L, 6, :].rearrange("p (c r d) -> p c r d", c=4, r=4),
                                    S1[1 - e][:, 2, :].rearrange("p (r c) -> p c r", r=4).unsqueeze(3).to_broadcast([L, 4, 4, DH]),
                                    ALU.mult).then_inc(on_ready, 1)
                if b is not None:
                    v.wait_ge(sc_exp, b + 1)
                    v.reduce_sum(S1[e][:, 1, :], SM[e], AX).then_inc(ri_ready, 1)
                    v.wait_ge(ri_ready, b * 2 + 1)
                    v.reciprocal(S1[e][:, 2, :], S1[e][:, 1, :]).then_inc(ri_ready, 1)
                    v.wait_ge(ri_ready, b * 2 + 2)

            batches(v, attn1_vector)
            for h in range(2):
                part = slice(h * HALF, (h + 1) * HALF)
                for m in range(KD):
                    v.wait_ge(o1_full, h * KD + m + 1)
                    last = v.tensor_tensor(R[:, m, part], XT[:, m, part], PS[:, 2 * m + h, 0:HALF], ALU.add)
                last.then_inc(ln_in, 1)
            ln_vector(v, 3)
            def values_vector(b, e, g, bank):
                if g >= 2 * KD:
                    j = g - 2 * KD
                    v.wait_ge(kv_full, b * NKV + (g + 1))
                    v.tensor_tensor(VX[e][0:width(j), j, :], PS[0:width(j), bank, :], bvr[0:width(j), :], ALU.add)\
                        .then_inc(v_read, 1)

            v.wait_ge(s_wx, 64)
            for g in range(NKV):
                values_vector(0, 0, g, g % 8)
            for h in range(2):
                for m in range(KD):
                    v.wait_ge(qx_full, h * KD + m + 1)
                    v.tensor_scalar(QX[:, m, h * HALF:(h + 1) * HALF], PS[:, 2 * m + h, 0:HALF], col("bq", m),
                                    float(DH) ** -0.5, ALU.add, ALU.mult).then_inc(qx_read, 1)
            v.sem_inc(ptx_free, 2)

            def xattn_vector(b, prev, nxt, e):
                for s in range(H1 + 2):
                    if b is not None and s < H1:
                        v.wait_ge(x_full, b * H1 + (s + 1))
                        v.tensor_reduce(SX[e][:, 0, s:s + 1], PS[0:L, 2 * (s % 2):2 * (s % 2) + 2, 0:SH],
                                        mybir.AxisListType.XY, ALU.max, negate=True).then_inc(nmx, 1)
                    if nxt is not None and s in GROUP_AT:
                        values_vector(nxt, 1 - e, GROUP_AT[s], 7)
                    if b is not None and 1 <= s <= H1:
                        h = s - 1
                        for p in range(2):
                            v.wait_ge(ptx_full, b * (2 * H1) + (2 * h + p + 1))
                            v.tensor_copy(PTX[h % 2][:, 3 * p:3 * p + 3, :], PS[:, 4 + p, 0:3 * L].rearrange(
                                "p (j q) -> p j q", j=3)).then_inc(ptx_free, 1)
                if b is not None:
                    v.wait_ge(x_free, b * H1 + (H1 + 2))
                    v.reciprocal(SX[e][:, 2, :], SX[e][:, 1, :]).then_inc(rix, 1)
                    v.wait_ge(rix, b + 1)
                    v.wait_ge(ox_full, b + 1)
                    v.tensor_tensor(OX[e].rearrange("p (h d) -> p h d", h=H1),
                                    PS[0:L, 6, :].rearrange("p (h d) -> p h d", h=H1),
                                    SX[e][:, 2, :].unsqueeze(2).to_broadcast([L, H1, DH]), ALU.mult).then_inc(ox_norm, 1)

            xbatches(v, xattn_vector)
            for h in range(2):
                part = slice(h * HALF, (h + 1) * HALF)
                for m in range(KD):
                    v.wait_ge(m2_full, h * KD + m + 1)
                    last = v.scalar_tensor_tensor(R[:, m, part], PS[:, 2 * m + h, 0:HALF], col("b2", m), XT[:, m, part],
                                                  ALU.add, ALU.add)
                last.then_inc(ln_in, 1)
            ln_vector(v, 4)
            tile_places = (XN, AB, SS, QG, QH, AM, SCL, RI)

            def ffn_vector(a, g, d, piece, e):
                for p, (c0, n) in enumerate(PARTS):
                    if d is not None:
                        v.wait_ge(gu_free, d * 3 + 3)
                        v.wait_ge(hq_read, d * 3 + 1)
                        for part in range(3):
                            quant_vector(piece + p, HB[1 - e][:, c0:c0 + n], HQ[:, c0:c0 + n], n, tile_places, part)
                    if g is not None:
                        v.wait_ge(si_ready, g * 3 + (p + 1))
                        v.tensor_tensor(HB[e][:, c0:c0 + n], PS[:, 2 * p + 1, 0:n], SI[:, p % 2, 0:n], ALU.mult)\
                            .then_inc(gu_free, 1)
                if a is not None:
                    v.wait_ge(xk_read, a + 1)
                    if g is not None:
                        v.wait_ge(xq_read, g + 1)
                    for part in range(3):
                        quant_vector(piece + (0 if d is None else 3), XK[:, bass.ds(a, 1), :].rearrange("p a d -> p (a d)"),
                                     XQ, D, tile_places, part)
                if d is not None:
                    y, s = YR[1 - e], LS[1 - e]
                    v.wait_ge(y_full, d + 1)
                    v.wait_ge(s_tile[1 - e], tile_stored(d, 1 - e))
                    v.tensor_tensor(y, PS[:, 7, :], XK[:, bass.ds(d, 1), :].rearrange("p a d -> p (a d)"), ALU.add).then_inc(f_sum, 1)
                    v.wait_ge(f_sum, d + 2)
                    v.reduce_sum(s[:, 0:1], y, AX).then_inc(f_mean, 1)
                    v.wait_ge(f_mean, d * 2 + 1)
                    v.tensor_scalar(s[:, 1:2], s[:, 0:1], 1.0 / D, None, ALU.mult).then_inc(f_mean, 1)
                    v.wait_ge(f_mean, d * 2 + 2)
                    v.tensor_scalar(y, y, s[:, 1:2], None, ALU.subtract).then_inc(f_cen, 1)
                    v.wait_ge(f_var, d * 2 + 2)
                    v.reciprocal(s[:, 4:5], s[:, 3:4]).then_inc(f_inv, 1)
                    v.wait_ge(f_inv, d + 1)
                    v.tensor_scalar(y, y, s[:, 4:5], None, ALU.mult).then_inc(f_out, 1)

            def tile_stored(d, e):
                return d * 8 - 8 * e + 16

            v.sem_inc(f_sum, 1)
            tiles(v, ffn_vector)


def columns(v):
    return np.asarray(v).reshape(-1, P).T


def layouts(x, ctx_768, L0_attn_delta_W, L0_attn_delta_b, L0_attn_B_W, L0_attn_B_b, L0_attn_C_W, L0_attn_C_b,
            L0_attn_A_log, L0_attn_dt_bias, L0_attn_tau, L0_attn_Wi_W, L0_attn_Wi_b, L0_attn_Wr_W, L0_attn_sel_W,
            L0_attn_sel_b, L0_attn_h0, L0_xattn_Wq, L0_xattn_Wk, L0_xattn_Wv, L0_xattn_Wo, L0_xattn_bo,
            L0_ffn_gate_w, L0_ffn_gate_bias, L0_ffn_w1, L0_ffn_w2, L0_ffn_w3, L0_ffn_sw1, L0_ffn_sw2, L0_ffn_sw3,
            L1_attn_Wq, L1_attn_Wk, L1_attn_Wv, L1_attn_Wo, L1_xattn_Wq, L1_xattn_bq, L1_xattn_Wk, L1_xattn_bk,
            L1_xattn_Wv, L1_xattn_bv, L1_xattn_W1, L1_xattn_b1, L1_xattn_W2, L1_xattn_b2, L1_ffn_w_gate,
            L1_ffn_w_up, L1_ffn_w_down):
    inv = (np.float32(1.0) / np.float32(10000.0) ** (np.arange(0, DH, 2, dtype=np.float32) / np.float32(DH))).astype(np.float32)
    freqs = np.arange(L, dtype=np.float32)[:, None] * inv[None, :]
    pair = (np.arange(P) % DH) // 2
    rope = np.concatenate([np.cos(freqs).astype(np.float32).T[pair], np.sin(freqs).astype(np.float32).T[pair]], axis=1)
    perm = np.zeros((P, P), np.float32)
    perm[np.arange(1, P, 2), np.arange(0, P, 2)] = -1.0
    perm[np.arange(0, P, 2), np.arange(1, P, 2)] = 1.0
    mask = np.triu(np.full((L, L), NEG, np.float32), k=1)
    return [
        ("xT", x.reshape(T, D).T),
        ("vecs", np.concatenate([columns(v) for v in (L0_attn_delta_b, L0_attn_dt_bias, L0_attn_sel_b, L0_xattn_bo,
                                                      L1_xattn_bq, L1_xattn_bk, L1_xattn_b1, L1_xattn_b2)], axis=1)),
        ("small16", np.stack([L0_attn_B_b, L0_attn_C_b, L0_attn_Wi_b, L0_attn_tau, L0_attn_h0[0]], axis=1)),
        ("bcb", np.concatenate([L0_attn_B_b, L0_attn_C_b])[:, None]),
        ("alog", L0_attn_A_log),
        ("ident", np.eye(P, dtype=np.float32)),
        ("mean_w", np.full((P, P), 1.0 / D, np.float32)),
        ("rope", rope), ("perm", perm), ("causal", mask),
        ("wiT", L0_attn_Wi_W.T), ("wrT", L0_attn_Wr_W.T), ("selT", L0_attn_sel_W.T),
        ("bcT", np.concatenate([L0_attn_B_W, L0_attn_C_W]).T), ("dwT", L0_attn_delta_W.T),
        ("ctxT", ctx_768.transpose(0, 2, 1)), ("ctxN", ctx_768),
        ("wq0T", L0_xattn_Wq.T), ("wk0", L0_xattn_Wk), ("wv0T", L0_xattn_Wv.T), ("wo0T", L0_xattn_Wo.T),
        ("gateT", L0_ffn_gate_w.T), ("gate_bias", np.concatenate([L0_ffn_gate_bias, np.arange(E, 0, -1, dtype=np.float32)])[None, :]),
        ("w1T", np.concatenate([L0_ffn_w1, L0_ffn_sw1[None]]).transpose(0, 2, 1)),
        ("w3T", np.concatenate([L0_ffn_w3, L0_ffn_sw3[None]]).transpose(0, 2, 1)),
        ("w2T", np.concatenate([L0_ffn_w2, L0_ffn_sw2[None]]).transpose(0, 2, 1)),
        ("wq1T", L1_attn_Wq.T), ("wk1T", L1_attn_Wk.T), ("wv1T", L1_attn_Wv.T), ("wo1T", L1_attn_Wo.T),
        ("xq1", L1_xattn_Wq), ("xk1", L1_xattn_Wk), ("xv1", L1_xattn_Wv), ("bv1", L1_xattn_bv[None, :]),
        ("xw1", L1_xattn_W1), ("xw2", L1_xattn_W2),
        ("wf", np.concatenate([w.reshape(-1, P, w.shape[1]).transpose(1, 0, 2).reshape(P, -1)
                               for w in (L1_ffn_w_gate, L1_ffn_w_up, L1_ffn_w_down)], axis=1)),
    ]


def kernel(**inputs):
    import concourse.bacc as bacc
    from concourse.bass_utils import run_bass_kernel_spmd

    nc = bacc.Bacc("TRN2", target_bir_lowering=False, num_devices=1)
    arrays, args = {}, []
    for name, a in layouts(**{k: np.asarray(v) for k, v in inputs.items()}):
        name = "in_" + name
        arrays[name] = np.ascontiguousarray(a)
        args.append(nc.dram_tensor(name, arrays[name].shape, mybir.dt.from_np(arrays[name].dtype),
                                   kind="ExternalInput").ap())
    args.append(nc.dram_tensor("out", (T, D), F32, kind="ExternalOutput").ap())
    program(nc, *args)
    got = run_bass_kernel_spmd(nc, [arrays], core_ids=[0]).results[0]["out"]
    return np.ascontiguousarray(got).reshape(B, L, D)
```

```python
import math
from contextlib import ExitStack

import numpy as np

import concourse.bass as bass
from concourse import mybir

F32 = mybir.dt.float32
F32R = mybir.dt.float32r
I32 = mybir.dt.int32
ALU = mybir.AluOpType
ACT = mybir.ActivationFunctionType
AX = mybir.AxisListType.X

P = 128
B, L, D = 8, 100, 512
T = B * L
KD = D // P
HALF = T // 2
N = 16
S, DC = 722, 384
KC = DC // P
SH = S // 2
SJ = -(-S // P)
H0 = 4
H1 = 16
DH = D // H1
E, FF = 8, 1024
FM = FF // P
ARENA_WORDS, SPLIT_WORDS = 42000, 23296
CHUNK = 2 * KD * P
I4 = 1408
I4M = I4 // P
LN_EPS = 1e-5
TINY_A = 1e-6
NEG = -1e30

VEC = {}
for _name, _n in (("delta_b", KD), ("dt_bias", KD), ("sel_b", KD), ("bo", KD), ("bq", KD), ("bk", KD),
                  ("b1", FM), ("b2", KD)):
    VEC[_name] = (sum(n for _, n in VEC.values()), _n)
NVEC = sum(n for _, n in VEC.values())


class Count:

    def __init__(self, sem):
        self.sem, self.n = sem, 0

    def inc(self, ins):
        ins.then_inc(self.sem, 1)
        self.n = self.n + 1


def program(nc, xT, vecs, small16, bcb, alog, ident_d, ones_d, rope_d, perm_d, mask_d, wiT, wrT, selT, bcT, dwT,
            ctxT, ctxN, wq0T, wk0, wv0T, wo0T, gateT, gate_bias, wc,
            wq1T, wk1T, wv1T, wo1T, xq1, xk1, xv1, bv1, xw1, xw2, wf, out):
    ctx = ExitStack()
    with ctx:
        def sb(name, shape, dt=F32):
            return ctx.enter_context(nc.sbuf_tensor(name, shape, dt))

        def sem(name):
            return ctx.enter_context(nc.semaphore(name))

        PS = ctx.enter_context(nc.psum_tensor("PS", [P, 8, 512], F32))
        XT = sb("XT", [P, KD, T])
        R = sb("R", [P, KD, T])
        SQ = sb("SQ", [P, KD, T])
        RS = sb("RS", [P, T])
        vec = sb("vec", [P, NVEC])
        ident = sb("ident", [P, P])
        mean_w = sb("mean_w", [P, P])
        eps_c = sb("eps_c", [P, 1])
        warm_c = sb("warm_c", [P, 1])
        with nc.sbuf_tensor("ARENA", [P, ARENA_WORDS], F32) as ARENA:
            pass
        SPLIT = sb("SPLIT", [P, SPLIT_WORDS], F32R)
        REST = sb("REST", [P, ARENA_WORDS - SPLIT_WORDS])

        def beside(off, *dims):
            v = REST[:, off - SPLIT_WORDS:off - SPLIT_WORDS + math.prod(dims)]
            return v.rearrange("p (a b) -> p a b", a=dims[0]) if len(dims) == 2 else v

        def at(off, *dims, rows=P, dt=F32):
            n = math.prod(dims)
            assert off + n <= (SPLIT_WORDS if dt == F32R else ARENA_WORDS), (off, n)
            v = (ARENA if dt == F32 else SPLIT)[0:rows, off:off + n]
            if len(dims) == 2:
                return v.rearrange("p (a b) -> p a b", a=dims[0])
            if len(dims) == 3:
                return v.rearrange("p (a b c) -> p a b c", a=dims[0], b=dims[1])
            return v

        def col(name, k):
            return vec[:, VEC[name][0] + k:VEC[name][0] + k + 1]

        def ln_tensor(pe, q):
            for h in range(2):
                pe.wait_ge(ln_in, 2 * q + h + 1)
                for k in range(KD):
                    last = pe.matmul(PS[:, h, 0:HALF], mean_w[:, :], R[:, k, h * HALF:(h + 1) * HALF],
                                     start=(k == 0), stop=(k == KD - 1))
                last.then_inc(ln_mean, 1)
            for h in range(2):
                for k in range(KD):
                    pe.wait_ge(ln_sq, 2 * KD * q + h * KD + k + 1)
                    last = pe.matmul(PS[:, 2 + h, 0:HALF], mean_w[:, :], SQ[:, k, h * HALF:(h + 1) * HALF],
                                     start=(k == 0), stop=(k == KD - 1))
                last.then_inc(ln_var, 1)

        def ln_scalar(act, q):
            for h in range(2):
                for k in range(KD):
                    act.wait_ge(ln_cen, 2 * KD * q + h * KD + k + 1)
                    act.activation(SQ[:, k, h * HALF:(h + 1) * HALF], R[:, k, h * HALF:(h + 1) * HALF],
                                   ACT.Square).then_inc(ln_sq, 1)
            act.activation(warm_c[:, 0:1], eps_c[:, 0:1], ACT.Sqrt)
            for h in range(2):
                act.wait_ge(ln_var, 2 * q + h + 1)
                act.activation(RS[:, h * HALF:(h + 1) * HALF], PS[:, 2 + h, 0:HALF], ACT.Sqrt,
                               bias=eps_c[:, 0:1]).then_inc(ln_std, 1)

        def ln_vector(v, q):
            for h in range(2):
                v.wait_ge(ln_mean, 2 * q + h + 1)
                for k in range(KD):
                    rows = R[:, k, h * HALF:(h + 1) * HALF]
                    v.tensor_tensor(rows, rows, PS[:, h, 0:HALF], ALU.subtract).then_inc(ln_cen, 1)
            for h in range(2):
                v.wait_ge(ln_std, 2 * q + h + 1)
                part = slice(h * HALF, (h + 1) * HALF)
                v.reciprocal(RS[:, part], RS[:, part]).then_inc(ln_inv, 1)
                v.wait_ge(ln_inv, 2 * q + h + 1)
                v.tensor_tensor(XT[:, :, part], R[:, :, part],
                                RS[:, part].unsqueeze(1).to_broadcast([P, KD, HALF]), ALU.mult).then_inc(ln_out, 1)

        XS = at(0, KD, T)
        DL = at(3200, KD, T)
        SP1, SP2, SP3 = at(6400, KD, T), at(9600, KD, T), at(12800, KD, T)
        BC = at(6400, 2, 2, T)
        AD = at(9600, 2, T)
        U, W, HS, V = at(11200, 2, T), at(12800, 2, T), at(14400, 2, T), at(16000, 2, T)
        dw = at(17600, KD, D)
        BCS = at(19648, T, rows=2 * N)
        ALOG, AA, KEEP, INV, TINY = (at(20448 + 64 * j, KD, N) for j in range(5))
        sm = at(20800, 8, rows=N)
        wi = at(20816, KD, N)
        wr = at(20880, N, rows=N)
        selw = at(20896, D, rows=N)
        bcw = at(21408, KD, 2 * N)
        SEL = at(21536, KD, B)
        GC = at(21568, KD, B)
        H8, TH, CUR8 = (at(21600 + 8 * j, B, rows=N) for j in range(3))
        TAU = at(21624, 2, rows=N)
        DB = at(21628, KD)
        bcbias = at(21632, 1, rows=2 * N)
        CNT = at(21636, 4)
        FLAG = sb("FLAG", [P, 1], I32)
        ZERO = at(21640, HALF)
        bc_dram = nc.dram_tensor("bc_rows", [2 * N, T], F32).ap()

        s_x, s_consts, s_wa, s_dw = sem("x_loaded"), sem("consts_loaded"), sem("gate_weights_loaded"), sem("delta_w_loaded")
        s_rows_out, s_bc = sem("bc_rows_stored"), [sem(f"bc_loaded_{e}") for e in range(2)]
        gate_pe, gate_act = sem("gate_product"), sem("gate_act")
        dve = Count(sem("dve_done"))
        xs_ready, gc_ready, newh_ready = sem("xs_ready"), sem("means_ready"), sem("new_h_ready")
        proj, proj_ev = sem("projected"), sem("projection_read")
        sp_dve, sp_act = sem("softplus_dve"), sem("softplus_act")
        a_ready, inv_ready, tiny_sum = sem("a_ready"), sem("inv_ready"), sem("tiny_counted")
        ad_ready, ad_free = sem("decay_ready"), sem("decay_read")
        u_ready, w_done = sem("input_ready"), sem("input_read")
        rz, v_ready, v_used = sem("restart_set"), sem("output_ready"), sem("output_summed")
        y_ready = sem("y_ready")
        tiny_s = sem("tiny_path")
        ln_in, ln_mean, ln_cen, ln_sq, ln_var, ln_std, ln_inv, ln_out = (
            sem("ln_" + n) for n in ("in", "mean", "centred", "squared", "variance", "std", "inverse", "out"))
        s_out = sem("out_stored")
        zero_ready, flag_read = sem("zero_ready"), sem("tiny_flag_read")

        def sp_step(m):
            return 2 * m + min(m + 2, KD) + 1

        wq0, wk0w, wv0, wo0 = at(22100, KD, D), at(24148, H0, DC), at(25684, KC, D), at(27220, KD, D)
        CT = [at(29268 + 2166 * e, KC, S) for e in range(2)]
        CN = [at(33600 + 2304 * e, SJ, DC) for e in range(2)]
        QT = at(0, KD, T)
        QP = [at(3200 + 1200 * e, KC, H0 * L) for e in range(2)]
        PR = [at(5600 + 2888 * e, H0, S, rows=L) for e in range(2)]
        PT = at(11376, SJ, H0 * L)
        TT = at(13776, KC, H0 * L)
        CO = at(14976, KD, T)
        ST = [at(18176 + 16 * e, 4, H0, rows=L) for e in range(2)]
        s_wb = sem("xattn0_weights_loaded")
        s_ct, s_cn = [sem(f"ctxT_loaded_{e}") for e in range(2)], [sem(f"ctxN_loaded_{e}") for e in range(2)]
        q_full, q0_read = sem("queries_projected"), sem("q0_read")
        s_full, s_free = sem("score_banks_full"), sem("score_banks_free")
        pt_full, pt_free = sem("pt_bank_full"), sem("pt_bank_free")
        tv_full, tv_free = sem("tv_bank_full"), sem("tv_bank_free")
        nm_ready, rs_ready, pr_ready, o_full = sem("neg_max_ready"), sem("rsum_ready"), sem("probs_ready"), sem("branch_projected")

        def width(j):
            return min(P, S - j * P)

        def batches(eng, turn):
            turn(0, None, 0)
            with eng.Fori(0, B // 2 - 1) as two:
                turn(two * 2 + 1, two * 2, 1)
                turn(two * 2 + 2, two * 2 + 1, 0)
            turn(B - 1, B - 2, 1)
            turn(None, B - 1, 0)

        def ctx_loads(b, per, e):
            return b * (per // 2) + (per - e * (per // 2))

        XH, XL = at(0, KD, T, dt=F32R), at(3200, KD, T, dt=F32R)
        HHH = [at(6400 + 3200 * h, FM, HALF, dt=F32R) for h in range(2)]
        HHL = [at(12800 + 3200 * h, FM, HALF, dt=F32R) for h in range(2)]
        CHUNKS, CW = FM + KD, 2 * KD * P
        CR = [beside(23296 + CW * j, CW) for j in range(3)]
        CH, CL = ([at(first + CW * j, 2 * KD, P, dt=F32R) for j in range(2)] for first in (19200, 21248))
        HT, SIL = beside(26368, 2, HALF), beside(27168, 2, HALF)
        CB = [at(27968 + T * e, T) for e in range(2)]
        TMP = at(29568, 4, HALF)
        gw, gb, rank = at(41900, KD, E), at(41932, E), at(41940, E)
        SC, BI, KEY, OH, CM = (at(34976 + 64 * j, B, E, rows=L) for j in range(5))
        GS = at(35296, 4, B, rows=L)
        CBT = at(35328, T, rows=E)
        ONE = at(36128, T, rows=1)
        comb_dram = nc.dram_tensor("combine_rows", [E + 1, T], F32).ap()
        s_gw, s_ck, s_cb = sem("router_loaded"), [sem(f"chunk_loaded_{j}") for j in range(3)], [sem(f"combine_loaded_{e}") for e in range(2)]
        s_comb, one_ready, r_copied = sem("combine_stored"), sem("ones_ready"), sem("stream_copied")
        lg_full, rt_dve, rt_exp = sem("logits_ready"), sem("router_dve"), sem("router_exp")
        cm_full, cm_read = sem("combine_transposed"), sem("combine_read")
        up_full, sil_ready, up_free = sem("up_banks_full"), sem("silu_ready"), sem("up_banks_free")
        x_high, x_low, ck_high, ck_low = sem("stream_high"), sem("stream_low"), sem("chunk_high"), sem("chunk_low")
        hh_high, hh_low = sem("hidden_high"), sem("hidden_low")
        dn_full, dn_free, acc = sem("down_bank_full"), sem("down_bank_free"), sem("accumulated")

        NU = 3 * KD * I4 // D
        RAW = [at(36928 + 512 * e, D) for e in range(2)]
        WTS = [at(37952 + 512 * e, D) for e in range(2)]
        UA, US, UG, UH = (at(38976 + 512 * j, D) for j in range(4))
        UM, UC, UR = (at(41024 + 32 * j, D // 16) for j in range(3))
        wt_dram = nc.dram_tensor("quantised_weights", [P, NU * D], F32).ap()
        q_scale, q_scaled, q_steps, q_done = sem("quant_scales"), sem("quant_scaled"), sem("quant_steps"), sem("quant_done")
        q_abs, q_sign, q_ss = sem("quant_abs"), sem("quant_sign"), sem("quant_signed_scale")
        s_raw, s_wst = ([sem(f"unit_loaded_{e}") for e in range(2)], [sem(f"unit_stored_{e}") for e in range(2)])
        wt_full, wt_copied = sem("unit_transposed"), sem("unit_copied")

        def chunk_loads(e, c):
            return e * (16 * CHUNKS // 3) + 16 * (c // 3 + 1)

        def wait_consumed(eng, e, c):
            if c < 0:
                if not isinstance(e, int) or e:
                    eng.wait_ge(dn_full, e * (2 * KD) + 2 * (c + 1))
            elif c < FM:
                eng.wait_ge(up_full, e * (2 * FM) + 2 * (c + 1))
            else:
                eng.wait_ge(dn_full, e * (2 * KD) + 2 * (c - FM + 1))

        def units(e):
            if isinstance(e, int) and e == 0:
                return [(0, 0, 0)]
            return [(i, e * 4 + (i - 3), (i + 1) % 2) for i in range(4)]

        def experts(eng, turn):
            turn(0, 0)
            with eng.Fori(0, E // 2 - 1) as two:
                turn(two * 2 + 1, 1)
                turn(two * 2 + 2, 0)
            turn(E - 1, 1)
            turn(E, 0)

        QR, KR, QS = at(0, KD, T), at(3200, KD, T), at(6400, KD, T)
        wv1, wo1 = at(12800, KD, D), at(15200, KD, D)
        causal = at(21320, L, rows=L)
        wq1, wk1 = (at(31168 + 2048 * j, KD, D) for j in range(2))
        perm, rope = at(35264, P), at(41280, 2 * L)
        VV = at(24576, B, D, rows=L)
        AO = at(28672, KD, T)
        QB = [at(31872 + 400 * e, KD, L) for e in range(2)]
        KB = [at(32672 + 400 * e, KD, L) for e in range(2)]
        SM = [at(33472 + 1600 * e, H1, L, rows=L) for e in range(2)]
        PT1 = at(36672, H1, L, rows=L)
        ON = at(38400, D, rows=L)
        S1 = [at(38912 + 48 * e, 3, H1, rows=L) for e in range(2)]
        s_wd, s_wd2 = sem("attn1_weights_loaded"), sem("attn1_late_weights_loaded")
        qk_read, pm_full, rot = sem("qk_read"), sem("pairs_swapped"), sem("rotated")
        v1_full, v1_read, qkb = sem("v1_projected"), sem("v1_read"), sem("qk_copied")
        sc_full, sc_read, sc_dve, sc_exp = sem("scores1_full"), sem("scores1_read"), sem("scores1_dve"), sem("probs1_ready")
        p1_full, p1_free, pv_full, on_ready = sem("probs1_transposed"), sem("probs1_read"), sem("pv1_full"), sem("normed1_ready")
        ot_full, ot_free, ri_ready = sem("out1_transposed"), sem("out1_read"), sem("rsum1_ready")

        def batches3(eng, turn):
            turn(0, None, None, 0)
            turn(1, 0, None, 1)
            with eng.Fori(0, B // 2 - 1) as two:
                turn(two * 2 + 2, two * 2 + 1, two * 2, 0)
                turn(two * 2 + 3, two * 2 + 2, two * 2 + 1, 1)
            turn(None, B - 1, B - 2, 0)
            turn(None, None, B - 1, 1)

        xkw, xvw, xqw, bvr = at(21420, KC, D), at(22956, KC, D), at(9600, KD, D), at(11648, D)
        CX = [at(39100, KC, S), at(12800, KC, S)]
        KX = [at(2888 * e, KD, S) for e in range(2)]
        QX = at(5776, KD, T)
        QBX = [at(8976, KD, L), at(20902, KD, L)]
        AO2 = at(14966, KD, T)
        PX = [at(18166 + SJ * P * e, SJ * P, rows=L) for e in range(2)]
        PTX = [at(19702 + 600 * e, SJ, L) for e in range(2)]
        VX = [at(24576 + 3072 * e, SJ, D) for e in range(2)]
        w1x, w2x = at(30720, KD, 2 * D), at(34816, 2 * KD, D)
        OX = [at(12160, D, rows=L), at(41266, D, rows=L)]
        SX = [at(41778 + 48 * e, 3, H1, rows=L) for e in range(2)]
        HX = at(0, 2 * KD, T)
        s_wx, s_wm, s_cx = sem("xattn1_weights_loaded"), sem("xattn1_mlp_loaded"), [sem(f"ctx1_loaded_{e}") for e in range(2)]
        kv_full, k_read, v_read = sem("kv_bank_full"), sem("keys_read"), sem("values_read")
        qx_read, qbx = sem("qx_read"), sem("qx_copied")
        x_full, x_free, nmx = sem("xscores_full"), sem("xscores_free"), sem("xneg_max")
        ptx_full, ptx_free, pad_ready = sem("xprobs_transposed"), sem("xprobs_read"), sem("pad_zeroed")
        ox_full, ox_norm, rix = sem("xout_full"), sem("xout_normed"), sem("xrsum")
        otx_full, otx_free = sem("xout_transposed"), sem("xout_read")
        mx_full, mx_free = sem("mlp_bank_full"), sem("mlp_bank_free")

        NKV = 2 * KD + SJ
        GROUP_AT = {s: s for s in range(NKV - 2)} | {H1: NKV - 2, H1 + 1: NKV - 1}

        def xbatches(eng, turn):
            turn(0, None, 1, 0)
            with eng.Fori(0, B // 2 - 1) as two:
                turn(two * 2 + 1, two * 2, two * 2 + 2, 1)
                turn(two * 2 + 2, two * 2 + 1, two * 2 + 3, 0)
            turn(B - 1, B - 2, None, 1)
            turn(None, B - 1, None, 0)

        def wait(eng, s, value):
            if not isinstance(value, int) or value > 0:
                eng.wait_ge(s, value)

        NT = -(-T // P)
        PARTS = [(0, D), (D, D), (2 * D, I4 - 2 * D)]
        WT = at(17920, NU * D)
        XK = at(0, NT, D)
        XQ = at(3584, D)
        XQT = [at(4096 + 512 * e, KD, P) for e in range(2)]
        HB = [at(5120 + I4 * e, I4) for e in range(2)]
        HQ, HQT = at(7936, I4), at(9344, I4M, P)
        XN, AB, SG, SS, QG, QH = ([at(10752 + 3200 * q + 512 * j, D) for q in range(2)] for j in range(6))
        AM, SCL, RI = ([at(13824 + 3200 * q + 32 * j, D // 16) for q in range(2)] for j in range(3))
        LS = [at(17152 + 8 * e, 8) for e in range(2)]
        XB = [at(38400 + 512 * e, KD, P) for e in range(2)]
        YR = [at(39424 + 512 * e, D) for e in range(2)]
        YS = at(40448, D)
        SI = at(40960, 2, D)
        WGv = WT[:, 0:KD * I4].rearrange("p (o k c) -> p k o c", k=KD, c=P)
        WUv = WT[:, KD * I4:2 * KD * I4].rearrange("p (o k c) -> p k o c", k=KD, c=P)
        WDv = WT[:, 2 * KD * I4:3 * KD * I4].rearrange("p (c m q) -> p m c q", m=I4M, q=P)

        s_wt = sem("weights_loaded")
        xb_ready = sem("tile_copied")
        xk_full, xk_read, xq_full, xq_read = sem("xk_full"), sem("xk_read"), sem("xq_full"), sem("xq_read")
        gu_full, si_ready, gu_free = sem("gate_up_full"), sem("gate_silu"), sem("gate_up_read")
        hq_full, hq_read, y_full = sem("hq_full"), sem("hq_read"), sem("y_full")
        f_sum, f_dve, f_var = sem("f_sum"), sem("f_dve"), sem("f_deviation")
        s_tile = [sem(f"tile_stored_{e}") for e in range(2)]

        def tiles(eng, turn):
            turn(0, None, None, None, NU, 1)
            turn(1, 0, None, None, NU + 1, 0)
            turn(2, 1, 0, None, NU + 2, 1)
            with eng.Fori(0, (NT - 5) // 2) as two:
                turn(two * 2 + 3, two * 2 + 2, two * 2 + 1, two * 2, two * 8 + (NU + 6), 0)
                turn(two * 2 + 4, two * 2 + 3, two * 2 + 2, two * 2 + 1, two * 8 + (NU + 10), 1)
            turn(NT - 2, NT - 3, NT - 4, NT - 5, 4 * NT + NU - 14, 0)
            turn(NT - 1, NT - 2, NT - 3, NT - 4, 4 * NT + NU - 10, 1)
            turn(None, NT - 1, NT - 2, NT - 3, 4 * NT + NU - 6, 0)
            turn(None, None, NT - 1, NT - 2, 4 * NT + NU - 3, 1)
            turn(None, None, None, NT - 1, 4 * NT + NU, 0)

        block = ctx.enter_context(nc.Block())

        @block.sync
        def _(sp):
            sp.dma_start(XT[:, :, :], xT.rearrange("(k p) t -> p k t", p=P)).then_inc(s_x, 16)
            for dst, src in ((vec[:, :], vecs), (ident[:, :], ident_d), (mean_w[:, :], ones_d),
                             (ALOG, alog.rearrange("(k p) n -> p k n", p=P))):
                sp.dma_start(dst, src).then_inc(s_consts, 16)
            for dst, src in ((sm[:, 0:3], small16), (bcbias, bcb), (wi, wiT.rearrange("(k p) n -> p k n", p=P)),
                             (wr, wrT), (selw, selT), (bcw, bcT.rearrange("(k p) n -> p k n", p=P))):
                sp.dma_start(dst, src).then_inc(s_wa, 16)
            sp.dma_start(dw, dwT.rearrange("(k p) o -> p k o", p=P)).then_inc(s_dw, 16)
            for dst, src in ((wq0, wq0T.rearrange("(k p) o -> p k o", p=P)), (wk0w, wk0.rearrange("(k p) o -> p k o", p=P)),
                             (wv0, wv0T.rearrange("(k p) o -> p k o", p=P)), (wo0, wo0T.rearrange("(k p) o -> p k o", p=P))):
                sp.dma_start(dst, src).then_inc(s_wb, 16)

            def load_ctxT(b, e):
                sp.dma_start(CT[e], ctxT[bass.ds(b, 1), :, :].rearrange("a (k p) s -> p (a k) s", p=P)).then_inc(s_ct[e], 16)

            def load_ctx(b, e):
                whole = (SJ - 1) * P
                sp.dma_start(CN[e][:, 0:SJ - 1, :], ctxN[bass.ds(b, 1), 0:whole, :].rearrange("a (j p) d -> p (a j) d", p=P))\
                    .then_inc(s_cn[e], 16)
                sp.dma_start(CN[e][0:S - whole, SJ - 1, :], ctxN[bass.ds(b, 1), whole:S, :].rearrange("a p d -> (a p) d"))\
                    .then_inc(s_cn[e], 16)

            for e in range(2):
                load_ctxT(e, e)
                load_ctx(e, e)
            for dst, src in ((gw, gateT.rearrange("(k p) e -> p k e", p=P)),
                             (gb, gate_bias[0:1, 0:E].to_broadcast([P, E])), (rank, gate_bias[0:1, E:2 * E].to_broadcast([P, E]))):
                sp.dma_start(dst, src).then_inc(s_gw, 16)
            sp.wait_ge(proj_ev, 2)
            sp.dma_start(bc_dram, BCS).then_inc(s_rows_out, 16)
            sp.wait_ge(s_rows_out, 16)
            sp.wait_ge(sp_dve, 3 * KD + 2)
            for n in range(2):
                for which in range(2):
                    sp.dma_start(BC[:, n, which, :],
                                 bc_dram[which * N + n:which * N + n + 1, :].to_broadcast([P, T])).then_inc(s_bc[n], 16)
            with sp.Fori(1, N // 2) as pair:
                n = pair * 2
                for e in range(2):
                    sp.wait_ge(v_ready, n * KD + KD * (e - 1))
                    for which in range(2):
                        sp.dma_start(BC[:, e, which, :],
                                     bc_dram[bass.ds(n + which * N + e, 1), :].to_broadcast([P, T])).then_inc(s_bc[e], 16)
            with sp.Fori(1, B // 2) as two:
                for e in range(2):
                    sp.wait_ge(s_full, two * 12 + 6 * (e - 1))
                    load_ctxT(two * 2 + e, e)
                    sp.wait_ge(tv_full, two * 8 + (4 * (e - 2) + 3))
                    load_ctx(two * 2 + e, e)
            def load_chunk(e, c):
                sp.dma_start(CR[c % 3], wc[bass.ds(e, 1), c, :, :].rearrange("a p w -> (a p) w")).then_inc(s_ck[c % 3], 16)

            def load_attn1():
                for dst, src in ((wq1, wq1T), (wk1, wk1T)):
                    sp.dma_start(dst, src.rearrange("(k p) o -> p k o", p=P)).then_inc(s_wd, 16)
                for dst, src in ((rope, rope_d), (perm, perm_d)):
                    sp.dma_start(dst, src).then_inc(s_wd, 16)

            def load_combine(e, slot):
                sp.dma_start(CB[slot], comb_dram[bass.ds(e, 1), :].to_broadcast([P, T])).then_inc(s_cb[slot], 16)

            sp.wait_ge(tv_free, B * 4 + 2)
            for c in range(3):
                load_chunk(0, c)
            sp.wait_ge(o_full, 2 * KD)
            sp.sem_inc(s_wst[0], 16)
            sp.sem_inc(s_wst[1], 16)

            def load_unit(u, slot):
                sp.dma_start(RAW[slot], wf[:, bass.ds(u * D, D)]).then_inc(s_raw[slot], 16)

            load_unit(0, 0)
            load_unit(1, 1)
            sp.wait_ge(one_ready, 1)
            sp.dma_start(comb_dram[E:E + 1, :], ONE).then_inc(s_comb, 16)

            def expert_sync(e, slot):
                for c in range(CHUNKS):
                    last = isinstance(e, int) and e == E
                    if not (last and c + 3 >= CHUNKS):
                        sp.wait_ge(ck_low, e * CHUNKS + (c + 1))
                        load_chunk(e + (c + 3) // CHUNKS, (c + 3) % CHUNKS)
                    if c == 3 and not last and not (isinstance(e, int) and e == 0):
                        sp.wait_ge(dn_free, e * 8 + 4)
                        load_combine(e + 1, 1 - slot)
                    if isinstance(e, int) and e == 0 and c == FM // 2 + 2:
                        sp.wait_ge(cm_read, 2)
                        sp.dma_start(comb_dram[0:E, :], CBT).then_inc(s_comb, 16)
                        sp.wait_ge(s_comb, 32)
                        load_combine(0, 0)
                        load_combine(1, 1)
                        load_attn1()
                    for i, u, us in units(e):
                        if c == (3 * i + 4) // 2 + 1:
                            if not isinstance(e, int) or u + 2 < NU:
                                sp.wait_ge(wt_full, u + 1)
                                load_unit(u + 2, us)
                            sp.wait_ge(wt_copied, u + 1)
                            sp.dma_start(wt_dram[:, bass.ds(u * D, D)], WTS[us]).then_inc(s_wst[us], 16)

            experts(sp, expert_sync)
            sp.wait_ge(dn_full, 8 * (E + 1))
            for dst, src in ((wv1, wv1T), (wo1, wo1T)):
                sp.dma_start(dst, src.rearrange("(k p) o -> p k o", p=P)).then_inc(s_wd2, 16)
            sp.dma_start(causal, mask_d).then_inc(s_wd2, 16)
            for dst, src in ((xkw, xk1), (xvw, xv1)):
                sp.dma_start(dst, src.rearrange("(k p) o -> p k o", p=P)).then_inc(s_wx, 16)

            def load_cx(b, e):
                sp.dma_start(CX[e], ctxT[bass.ds(b, 1), :, :].rearrange("a (k p) s -> p (a k) s", p=P)).then_inc(s_cx[e], 16)

            load_cx(0, 0)
            sp.dma_start(xqw, xq1.rearrange("(k p) o -> p k o", p=P)).then_inc(s_wx, 16)
            sp.dma_start(bvr, bv1.to_broadcast([P, D])).then_inc(s_wx, 16)
            sp.wait_ge(v1_full, B)
            load_cx(1, 1)
            sp.wait_ge(o_full, 2 * KD + 2 * KD)
            sp.dma_start(w1x, xw1.rearrange("(k p) o -> p k o", p=P)).then_inc(s_wm, 16)
            sp.dma_start(w2x, xw2.rearrange("(k p) o -> p k o", p=P)).then_inc(s_wm, 16)
            with sp.Fori(1, B // 2) as two:
                for e in range(2):
                    sp.wait_ge(v_read, two * (2 * SJ) + SJ * (e - 1))
                    load_cx(two * 2 + e, e)
            sp.wait_ge(s_wst[0], 16 * ((NU + 1) // 2 + 1))
            sp.wait_ge(s_wst[1], 16 * (NU // 2 + 1))
            sp.wait_ge(mx_full, 4 * KD)
            for w in range(3):
                cols = slice(w * KD * I4, (w + 1) * KD * I4)
                sp.dma_start(WT[:, cols], wt_dram[:, cols]).then_inc(s_wt, 16)

            def store(a, g, d, l, piece, e):
                if l is not None:
                    rows = min(P, T - l * P) if isinstance(l, int) else P
                    sp.wait_ge(f_dve, l * 5 + 5)
                    sp.dma_start(out[bass.ds(l * P, rows), :], YR[e][0:rows, :]).then_inc(s_tile[e], 16)

            sp.sem_inc(s_tile[0], 16)
            sp.sem_inc(s_tile[1], 16)
            tiles(sp, store)
            sp.wait_ge(s_tile[0], 16 * ((NT + 1) // 2 + 1))
            sp.wait_ge(s_tile[1], 16 * (NT // 2 + 1))

        @block.tensor
        def _(pe):
            pe.wait_ge(s_wa, 96)
            pe.wait_ge(gc_ready, 1)
            for k in range(KD):
                pe.matmul(PS[0:N, 0, 0:B], wi[:, k, :], GC[:, k, :], start=(k == 0), stop=False)
            pe.matmul(PS[0:N, 0, 0:B], wr, CUR8, start=False, stop=True).then_inc(gate_pe, 1)
            pe.wait_ge(newh_ready, 1)
            for c in range(KD):
                last = pe.matmul(PS[:, 1, c * B:(c + 1) * B], selw[:, c * P:(c + 1) * P], H8, start=True, stop=True)
            last.then_inc(gate_pe, 1)
            pe.wait_ge(s_consts, 64)
            pe.wait_ge(inv_ready, 1)
            pe.matmul(PS[:, 1, 64:65], mean_w[:, :], CNT[:, 0:1], start=True, stop=True).then_inc(tiny_sum, 1)
            pe.wait_ge(xs_ready, 1)
            for h in range(2):
                for k in range(KD):
                    last = pe.matmul(PS[0:2 * N, 2 + h, 0:HALF], bcw[:, k, :], XS[:, k, h * HALF:(h + 1) * HALF],
                                     start=(k == 0), stop=(k == KD - 1))
                last.then_inc(proj, 1)
            pe.wait_ge(s_dw, 16)
            pe.wait_ge(flag_read, 1)
            for g in range(2 * KD):
                m, h = g // 2, g % 2
                if g >= 6:
                    pe.wait_ge(proj_ev, g - 5)
                for k in range(KD):
                    last = pe.matmul(PS[:, (4 + g) % 8, 0:HALF], dw[:, k, m * P:(m + 1) * P],
                                     XS[:, k, h * HALF:(h + 1) * HALF], start=(k == 0), stop=(k == KD - 1))
                last.then_inc(proj, 1)
            pe.wait_ge(proj_ev, 10)
            pe.wait_ge(zero_ready, 1)
            for b in range(8):
                pe.matmul(PS[:, b, 0:HALF], ident[:, :], ZERO, start=True, stop=False)
            pe.sem_inc(v_used, 2)
            with pe.Fori(0, N // 2) as pair:
                n = pair * 2
                for e in range(2):
                    for c in range(KD):
                        pe.wait_ge(v_ready, n * KD + (e * KD + c + 1))
                        for h in range(2):
                            last = pe.matmul(PS[:, 2 * c + h, 0:HALF], ident[:, :], V[:, c % 2, h * HALF:(h + 1) * HALF],
                                             start=False, stop=False)
                        last.then_inc(v_used, 1)
            for b in range(8):
                last = pe.matmul(PS[:, b, 0:HALF], ident[:, :], ZERO, start=False, stop=True)
            last.then_inc(y_ready, 1)
            ln_tensor(pe, 0)
            pe.wait_ge(s_wb, 64)
            for h in range(2):
                pe.wait_ge(ln_out, 1 + h)
                for m in range(KD):
                    for k in range(KD):
                        last = pe.matmul(PS[:, 2 * m + h, 0:HALF], wq0[:, k, m * P:(m + 1) * P],
                                         XT[:, k, h * HALF:(h + 1) * HALF], start=(k == 0), stop=(k == KD - 1))
                    last.then_inc(q_full, 1)
            pe.wait_ge(q0_read, 2 * KD)

            def qk_tensor(b, prev, e):
                def transposes(j0):
                    for j in range(j0, j0 + 2):
                        pe.wait_ge(pt_free, prev * SJ + (j + 1))
                        for h in range(H0):
                            last = pe.transpose(PS[0:width(j), 4 + j % 2, h * L:(h + 1) * L],
                                                PR[1 - e][:, h, j * P:j * P + width(j)], ident[0:L, 0:L])
                        last.then_inc(pt_full, 1)

                if b is not None:
                    for m in range(KC):
                        slot, bank = m // 2, m % 2
                        if bank == 0:
                            pe.wait_ge(s_free, b * 6 + (slot + 1))
                        for h in range(H0):
                            last = pe.matmul(PS[:, 2 * slot + bank, h * L:(h + 1) * L], wk0w[:, h, m * P:(m + 1) * P],
                                             QT[:, h, bass.ds(b * L, L)], start=True, stop=True)
                        if m in (1, 2):
                            last.then_inc(s_full, 1)
                    pe.wait_ge(s_ct[e], ctx_loads(b, 16, e))
                if prev is not None:
                    pe.wait_ge(pr_ready, prev * H0 + H0)
                for h in range(H0):
                    if b is not None:
                        pe.wait_ge(s_free, b * 6 + max(4, 3 + h))
                        for half in range(2):
                            for k in range(KC):
                                last = pe.matmul(PS[0:L, 2 * (h % 2) + half, 0:SH], QP[e][:, k, h * L:(h + 1) * L],
                                                 CT[e][:, k, half * SH:(half + 1) * SH], start=(k == 0), stop=(k == KC - 1))
                        last.then_inc(s_full, 1)
                    if prev is not None and h < 3:
                        transposes(2 * h)
                if prev is not None:
                    pe.wait_ge(s_cn[1 - e], ctx_loads(prev, 32, 1 - e))
                    pe.wait_ge(pt_free, prev * SJ + (SJ + 2))
                    for m in range(KC):
                        pe.wait_ge(tv_free, prev * 4 + (m + 1))
                        for j in range(SJ):
                            last = pe.matmul(PS[:, 6 + m % 2, 0:H0 * L], CN[1 - e][0:width(j), j, m * P:(m + 1) * P],
                                             PT[0:width(j), j, :], start=(j == 0), stop=(j == SJ - 1))
                        last.then_inc(tv_full, 1)
                    pe.wait_ge(tv_free, prev * 4 + (KC + 2))
                    for h in range(H0):
                        for k in range(KC):
                            last = pe.matmul(PS[:, 7, h * L:(h + 1) * L], wv0[:, k, h * P:(h + 1) * P],
                                             TT[:, k, h * L:(h + 1) * L], start=(k == 0), stop=(k == KC - 1))
                    last.then_inc(tv_full, 1)

            batches(pe, qk_tensor)
            pe.wait_ge(tv_free, B * 4 + 2)
            for h in range(2):
                for m in range(KD):
                    for k in range(KD):
                        last = pe.matmul(PS[:, 2 * m + h, 0:HALF], wo0[:, k, m * P:(m + 1) * P],
                                         CO[:, k, h * HALF:(h + 1) * HALF], start=(k == 0), stop=(k == KD - 1))
                    last.then_inc(o_full, 1)
            ln_tensor(pe, 1)
            pe.wait_ge(s_gw, 48)
            pe.wait_ge(ln_out, 4)
            for b in range(B):
                for k in range(KD):
                    last = pe.matmul(PS[0:L, 4, b * E:(b + 1) * E], XT[:, k, b * L:(b + 1) * L], gw[:, k, :],
                                     start=(k == 0), stop=(k == KD - 1))
            last.then_inc(lg_full, 1)

            def split_product(dst, w_high, w_low, x_high, x_low, n):
                for k in range(n):
                    pe.matmul(dst, w_high(k), x_high(k), start=(k == 0), stop=False)
                    pe.matmul(dst, w_high(k), x_low(k), start=False, stop=False)
                    last = pe.matmul(dst, w_low(k), x_high(k), start=False, stop=(k == n - 1))
                return last

            def expert_tensor(e, slot):
                for m in range(FM):
                    pe.wait_ge(ck_low, e * CHUNKS + (m + 1))
                    for h in range(2):
                        s, part = 2 * m + h, slice(h * HALF, (h + 1) * HALF)
                        for i, u, us in units(e):
                            if s == 3 * i + 4:
                                pe.wait_ge(q_done, u + 1)
                                pe.wait_ge(dn_free, e * 8 + (i + 1))
                                for j in range(4):
                                    last = pe.transpose(PS[:, 4 + i, j * P:(j + 1) * P], RAW[us][:, j * P:(j + 1) * P], ident[:, :])
                                last.then_inc(wt_full, 1)
                        pe.wait_ge(up_free, e * 16 + (s + 1))
                        for w in range(2):
                            last = split_product(PS[:, 2 * h + w, 0:HALF], lambda k: CH[m % 2][:, w * KD + k, :],
                                                 lambda k: CL[m % 2][:, w * KD + k, :], lambda k: XH[:, k, part],
                                                 lambda k: XL[:, k, part], KD)
                        last.then_inc(up_full, 1)
                    if isinstance(e, int) and e == 0 and m == FM // 2:
                        pe.wait_ge(rt_dve, 2)
                        for b in range(B):
                            last = pe.transpose(PS[0:E, 5 + b // 4, (b % 4) * L:(b % 4 + 1) * L], CM[:, b, :], ident[0:L, 0:L])
                            if b % 4 == 3:
                                last.then_inc(cm_full, 1)
                        pe.wait_ge(cm_read, 2)
                for m in range(KD):
                    pe.wait_ge(ck_low, e * CHUNKS + (FM + m + 1))
                    for h in range(2):
                        t = 2 * m + h
                        for i, u, us in units(e):
                            if i == t:
                                pe.wait_ge(wt_copied, u + 1)
                        pe.wait_ge(dn_free, e * 8 + (t + 1))
                        if m == 0:
                            pe.wait_ge(hh_low, e * 16 + (2 * FM - 1 + h))
                        split_product(PS[:, 4 + t % 4, 0:HALF], lambda k: CH[m % 2][:, k, :], lambda k: CL[m % 2][:, k, :],
                                      lambda k: HHH[h][:, k, :], lambda k: HHL[h][:, k, :], FM).then_inc(dn_full, 1)

            pe.wait_ge(x_low, 2)
            experts(pe, expert_tensor)
            ln_tensor(pe, 2)
            pe.wait_ge(s_wd, 64)
            for which, (w, raw) in enumerate(((wq1, QS), (wk1, R))):
                if which:
                    pe.wait_ge(rot, 2)
                for h in range(2):
                    pe.wait_ge(ln_out, 5 + h)
                    for m in range(KD):
                        for k in range(KD):
                            last = pe.matmul(PS[:, 2 * m + h, 0:HALF], w[:, k, m * P:(m + 1) * P],
                                             XT[:, k, h * HALF:(h + 1) * HALF], start=(k == 0), stop=(k == KD - 1))
                        last.then_inc(q_full, 1)
                for h in range(2):
                    for m in range(KD):
                        pe.wait_ge(qk_read, 8 * which + h * KD + m + 1)
                        last = pe.matmul(PS[:, 2 * m + h, 0:HALF], perm, raw[:, m, h * HALF:(h + 1) * HALF],
                                         start=True, stop=True)
                last.then_inc(pm_full, 1)
            pe.wait_ge(rot, 5)
            pe.wait_ge(s_wd2, 48)
            for b in range(B):
                for k in range(KD):
                    last = pe.matmul(PS[0:L, b, :], XT[:, k, b * L:(b + 1) * L], wv1[:, k, :],
                                     start=(k == 0), stop=(k == KD - 1))
                last.then_inc(v1_full, 1)
            pe.wait_ge(v1_read, B)

            def attn1_tensor(b, prev, old, e):
                if b is not None:
                    pe.wait_ge(qkb, b * 2 + 2)
                    pe.wait_ge(sc_read, b + 2)
                    for c in range(KD):
                        for r in range(4):
                            rows = slice(r * DH, (r + 1) * DH)
                            last = pe.matmul(PS[0:L, r, c * L:(c + 1) * L], QB[e][rows, c, :], KB[e][rows, c, :],
                                             start=True, stop=True)
                    last.then_inc(sc_full, 1)
                if old is not None:
                    pe.wait_ge(on_ready, old + 1)
                    pe.wait_ge(ot_free, old + 1)
                    for c in range(KD):
                        last = pe.transpose(PS[:, 7, c * L:(c + 1) * L], ON[:, c * P:(c + 1) * P], ident[0:L, 0:L])
                    last.then_inc(ot_full, 1)
                if prev is not None:
                    pe.wait_ge(sc_exp, prev + 1)
                    for c in range(KD):
                        pe.wait_ge(p1_free, prev * 4 + (c + 1))
                        for r in range(4):
                            last = pe.transpose(PS[0:L, 4 + c % 2, r * L:(r + 1) * L], SM[1 - e][:, 4 * r + c, :],
                                                ident[0:L, 0:L])
                        last.then_inc(p1_full, 1)
                    pe.wait_ge(p1_free, prev * 4 + 6)
                    for h in range(H1):
                        last = pe.matmul(PS[0:L, 6, h * DH:(h + 1) * DH], PT1[:, h, :],
                                         VV[:, bass.ds(prev, 1), h * DH:(h + 1) * DH], start=True, stop=True)
                    last.then_inc(pv_full, 1)

            batches3(pe, attn1_tensor)
            pe.wait_ge(ot_free, B + 1)
            for h in range(2):
                for m in range(KD):
                    for k in range(KD):
                        last = pe.matmul(PS[:, 2 * m + h, 0:HALF], wo1[:, k, m * P:(m + 1) * P],
                                         AO[:, k, h * HALF:(h + 1) * HALF], start=(k == 0), stop=(k == KD - 1))
                    last.then_inc(o_full, 1)
            ln_tensor(pe, 3)
            def kv_group(b, e, g, bank, first=False):
                if first:
                    wait(pe, k_read, max(0, g - 7))
                elif g == 0:
                    pe.wait_ge(v_read, b * SJ)
                elif g <= 2 * KD:
                    pe.wait_ge(k_read, b * (2 * KD) + g)
                else:
                    pe.wait_ge(v_read, b * SJ + (g - 2 * KD))
                if g == 0:
                    pe.wait_ge(s_cx[e], ctx_loads(b, 16, e))
                if g < 2 * KD:
                    m, half = g // 2, g % 2
                    for k in range(KC):
                        last = pe.matmul(PS[:, bank, 0:SH], xkw[:, k, m * P:(m + 1) * P],
                                         CX[e][:, k, half * SH:(half + 1) * SH], start=(k == 0), stop=(k == KC - 1))
                else:
                    j = g - 2 * KD
                    for k in range(KC):
                        last = pe.matmul(PS[0:width(j), bank, :], CX[e][:, k, j * P:j * P + width(j)], xvw[:, k, :],
                                         start=(k == 0), stop=(k == KC - 1))
                last.then_inc(kv_full, 1)

            pe.wait_ge(s_wx, 64)
            pe.wait_ge(ln_out, 8)
            for g in range(NKV):
                kv_group(0, 0, g, g % 8, first=True)
            pe.wait_ge(k_read, 2 * KD)
            pe.wait_ge(v_read, SJ)
            for h in range(2):
                for m in range(KD):
                    for k in range(KD):
                        last = pe.matmul(PS[:, 2 * m + h, 0:HALF], xqw[:, k, m * P:(m + 1) * P],
                                         XT[:, k, h * HALF:(h + 1) * HALF], start=(k == 0), stop=(k == KD - 1))
                    last.then_inc(q_full, 1)
            pe.wait_ge(qx_read, 2 * KD)
            pe.wait_ge(pad_ready, 2)

            def xattn_tensor(b, prev, nxt, e):
                for s in range(H1 + 2):
                    if b is not None and s < H1:
                        if s == 0:
                            pe.wait_ge(qbx, b + 1)
                        pe.wait_ge(x_free, b * H1 + (s + 1))
                        rows = slice((s % 4) * DH, (s % 4 + 1) * DH)
                        for half in range(2):
                            last = pe.matmul(PS[0:L, 2 * (s % 2) + half, 0:SH], QBX[e][rows, s // 4, :],
                                             KX[e][rows, s // 4, half * SH:(half + 1) * SH], start=True, stop=True)
                        last.then_inc(x_full, 1)
                    if prev is not None and s == 2:
                        pe.wait_ge(ox_norm, prev + 1)
                        if nxt is not None:
                            pe.wait_ge(k_read, nxt * (2 * KD) + 2)
                        else:
                            pe.wait_ge(v_read, B * SJ)
                            pe.wait_ge(otx_free, prev)
                        for c in range(KD):
                            last = pe.transpose(PS[:, 7, c * L:(c + 1) * L], OX[1 - e][:, c * P:(c + 1) * P], ident[0:L, 0:L])
                        last.then_inc(otx_full, 1)
                    if nxt is not None and s in GROUP_AT:
                        if prev is not None and s == 2:
                            pe.wait_ge(otx_free, prev + 1)
                        kv_group(nxt, 1 - e, GROUP_AT[s], 7)
                    if b is not None and 1 <= s <= H1:
                        h = s - 1
                        pe.wait_ge(x_free, b * H1 + (h + 3))
                        for p in range(2):
                            pe.wait_ge(ptx_free, b * (2 * H1) + (2 * h + p + 1))
                            for j in range(3):
                                last = pe.transpose(PS[:, 4 + p, j * L:(j + 1) * L],
                                                    PX[h % 2][:, (3 * p + j) * P:(3 * p + j + 1) * P], ident[0:L, 0:L])
                            last.then_inc(ptx_full, 1)
                    if b is not None and s >= 2:
                        h = s - 2
                        if h == 0:
                            wait(pe, ox_norm, b)
                        pe.wait_ge(ptx_free, b * (2 * H1) + (2 * h + 4))
                        for j in range(SJ):
                            last = pe.matmul(PS[0:L, 6, h * DH:(h + 1) * DH], PTX[h % 2][0:width(j), j, :],
                                             VX[e][0:width(j), j, h * DH:(h + 1) * DH], start=(j == 0), stop=(j == SJ - 1))
                        if h == H1 - 1:
                            last.then_inc(ox_full, 1)

            xbatches(pe, xattn_tensor)
            pe.wait_ge(s_wm, 32)
            pe.wait_ge(otx_free, B)
            for h in range(2):
                for m in range(2 * KD):
                    g = h * 2 * KD + m
                    wait(pe, mx_free, max(0, g - 7))
                    for k in range(KD):
                        last = pe.matmul(PS[:, g % 8, 0:HALF], w1x[:, k, m * P:(m + 1) * P],
                                         AO2[:, k, h * HALF:(h + 1) * HALF], start=(k == 0), stop=(k == KD - 1))
                    last.then_inc(mx_full, 1)
            pe.wait_ge(mx_free, 4 * KD)
            for h in range(2):
                for m in range(KD):
                    for k in range(2 * KD):
                        last = pe.matmul(PS[:, 2 * m + h, 0:HALF], w2x[:, k, m * P:(m + 1) * P],
                                         HX[:, k, h * HALF:(h + 1) * HALF], start=(k == 0), stop=(k == 2 * KD - 1))
                    last.then_inc(o_full, 1)
            ln_tensor(pe, 4)
            pe.wait_ge(s_wt, 48)

            def ffn_tensor(a, g, d, l, piece, e):
                if a is not None:
                    pe.wait_ge(xb_ready, a + 1)
                    if g is not None:
                        pe.wait_ge(xq_read, g + 1)
                    pe.wait_ge(hq_read, piece_of_hq(a, g) + 1)
                    for k in range(KD):
                        last = pe.transpose(PS[:, 6, k * P:(k + 1) * P], XB[1 - e][:, k, :], ident[:, :])
                    last.then_inc(xk_full, 1)
                if g is not None:
                    pe.wait_ge(xq_read, g + 1)
                    for p, (c0, n) in enumerate(PARTS):
                        wait(pe, gu_free, g * 3 + p - 2 if not isinstance(g, int) or g else 0)
                        for w, view in enumerate((WGv, WUv)):
                            for k in range(KD):
                                last = pe.matmul(PS[:, 2 * p + w, 0:n], XQT[e][:, k, :], view[:, k, c0 // P:(c0 + n) // P, :],
                                                 start=(k == 0), stop=(k == KD - 1))
                        last.then_inc(gu_full, 1)
                if d is not None:
                    for p, (c0, n) in enumerate(PARTS):
                        pe.wait_ge(q_done, piece + (p + 1))
                        if p == 0:
                            if a is not None:
                                pe.wait_ge(xk_read, a + 1)
                        else:
                            pe.wait_ge(hq_read, d * 3 + p + 1)
                        for i in range(n // P):
                            last = pe.transpose(PS[:, 6, i * P:(i + 1) * P], HQ[:, c0 + i * P:c0 + (i + 1) * P], ident[:, :])
                        last.then_inc(hq_full, 1)
                    pe.wait_ge(hq_read, d * 3 + 4)
                    pe.wait_ge(f_sum, d + 1)
                    for m in range(I4M):
                        last = pe.matmul(PS[:, 7, :], HQT[:, m, :], WDv[:, m, :, :], start=(m == 0), stop=(m == I4M - 1))
                    last.then_inc(y_full, 1)
                if a is not None:
                    pe.wait_ge(q_done, piece + (1 if d is None else 4))
                    pe.wait_ge(xk_read, a + 1)
                    for k in range(KD):
                        last = pe.transpose(PS[:, 6, k * P:(k + 1) * P], XQ[:, k * P:(k + 1) * P], ident[:, :])
                    last.then_inc(xq_full, 1)

            def piece_of_hq(a, g):
                return 0 if g is None or isinstance(g, int) and g < 2 else g * 3 - 3

            tiles(pe, ffn_tensor)

        @block.scalar
        def _(act):
            act.wait_ge(s_wa, 96)
            act.wait_ge(gate_pe, 1)
            act.activation(TH, PS[0:N, 0, 0:B], ACT.Tanh, bias=sm[:, 0:1]).then_inc(gate_act, 1)
            act.wait_ge(gate_pe, 2)
            act.wait_ge(s_consts, 64)
            for c in range(KD):
                act.activation(SEL[:, c, :], PS[:, 1, c * B:(c + 1) * B], ACT.Sigmoid,
                               bias=col("sel_b", c)).then_inc(gate_act, 1)
            act.activation(AA, ALOG, ACT.Exp).then_inc(a_ready, 1)
            for h in range(2):
                act.wait_ge(proj, 1 + h)
                act.activation(BCS[:, h * HALF:(h + 1) * HALF], PS[0:2 * N, 2 + h, 0:HALF], ACT.Identity,
                               bias=bcbias).then_inc(proj_ev, 1)
            act.wait_ge(inv_ready, 1)

            def exp_of(m):
                act.wait_ge(sp_dve, max(1, 3 * m - 1))
                act.activation(SP1[:, m, :], SP1[:, m, :], ACT.Exp).then_inc(sp_act, 1)

            for g in range(2 * KD):
                m, h = g // 2, g % 2
                act.wait_ge(proj, 3 + g)
                act.activation(DL[:, m, h * HALF:(h + 1) * HALF], PS[:, (4 + g) % 8, 0:HALF], ACT.Identity,
                               bias=DB[:, m:m + 1]).then_inc(proj_ev, 1)
                if m and h == 0:
                    exp_of(m - 1)
            exp_of(KD - 1)
            act.wait_ge(sp_dve, 3 * KD - 1)
            act.activation(SP3, SP2, ACT.Ln).then_inc(sp_act, 1)
            act.wait_ge(sp_dve, 3 * KD)
            act.wait_ge(sp_act, KD + 1)
            act.activation(SP2, SP3, ACT.Exp, scale=-1.0).then_inc(sp_act, 1)
            act.wait_ge(sp_dve, 3 * KD + 3)
            with act.Fori(0, N // 2) as pair:
                n = pair * 2
                for e in range(2):
                    for c in range(KD):
                        act.wait_ge(ad_free, n * KD + (e * KD + c + 1))
                        act.nop()
                        act.activation(AD[:, c % 2, :], DL[:, c, :], ACT.Exp,
                                       scale=AA[:, c, bass.ds(n + e, 1)]).then_inc(ad_ready, 1)
            ln_scalar(act, 0)
            for h in range(2):
                for m in range(KD):
                    act.wait_ge(q_full, h * KD + m + 1)
                    act.activation(QT[:, m, h * HALF:(h + 1) * HALF], PS[:, 2 * m + h, 0:HALF], ACT.Copy,
                                   scale=float(D // H0) ** -0.5).then_inc(q0_read, 1)
            act.sem_inc(s_free, 2)
            act.sem_inc(tv_free, 2)

            def qk_scalar(b, prev, e):
                if b is not None:
                    act.wait_ge(s_full, b * 6 + 1)
                    act.activation(QP[e][:, 0:2, :], PS[:, 0:2, 0:H0 * L], ACT.Copy).then_inc(s_free, 1)
                    act.wait_ge(s_full, b * 6 + 2)
                    act.activation(QP[e][:, 2, :], PS[:, 2, 0:H0 * L], ACT.Copy).then_inc(s_free, 1)
                    for h in range(H0):
                        act.wait_ge(nm_ready, b * H0 + (h + 1))
                        act.activation(PR[e][:, h, :].rearrange("p (a s) -> p a s", a=2),
                                       PS[0:L, 2 * (h % 2):2 * (h % 2) + 2, 0:SH], ACT.Exp, bias=ST[e][:, 0, h:h + 1],
                                       accum_out=ST[e][:, 1, h:h + 1]).then_inc(s_free, 1)
                if prev is not None:
                    for m in range(KC):
                        act.wait_ge(tv_full, prev * 4 + (m + 1))
                        act.activation(TT[:, m, :], PS[:, 6 + m % 2, 0:H0 * L], ACT.Copy).then_inc(tv_free, 1)
                    act.wait_ge(tv_full, prev * 4 + (KC + 1))
                    act.activation(CO[:, :, bass.ds(prev * L, L)], PS[:, 7, 0:H0 * L].rearrange("p (h q) -> p h q", h=H0),
                                   ACT.Copy).then_inc(tv_free, 1)

            batches(act, qk_scalar)
            ln_scalar(act, 1)
            def chunk_high(e, c):
                act.wait_ge(s_ck[c % 3], chunk_loads(e, c))
                if c > 1 or not isinstance(e, int) or e:
                    wait_consumed(act, e, c - 2)
                act.activation(CH[c % 2], CR[c % 3].rearrange("p (j o) -> p j o", o=P), ACT.Copy).then_inc(ck_high, 1)

            for h in range(2):
                part = slice(h * HALF, (h + 1) * HALF)
                act.wait_ge(ln_out, 3 + h)
                act.activation(XH[:, :, part], XT[:, :, part], ACT.Copy).then_inc(x_high, 1)
            chunk_high(0, 0)

            act.wait_ge(rt_dve, 1)
            act.activation(SC, SC, ACT.Exp).then_inc(rt_exp, 1)

            def quant_scalar(piece, scaled, magnitude, sign):
                act.wait_ge(q_scaled, piece + 1)
                act.activation(magnitude, scaled, ACT.Abs).then_inc(q_abs, 1)
                act.activation(sign, scaled, ACT.Sign).then_inc(q_sign, 1)

            def hidden_high(e, s):
                act.wait_ge(up_free, e * 16 + (s + 3))
                act.activation(HHH[s % 2][:, s // 2, :], HT[:, s % 2, :], ACT.Copy).then_inc(hh_high, 1)

            def expert_scalar(e, slot):
                for m in range(FM):
                    for h in range(2):
                        s = 2 * m + h
                        if h == 0:
                            chunk_high(e, m + 1)
                        for i, u, us in units(e):
                            if s == 3 * i + 4:
                                act.wait_ge(wt_full, u + 1)
                                act.wait_ge(s_wst[us], ctx_loads(u, 16, us))
                                act.activation(WTS[us], PS[:, 4 + i, :], ACT.Copy).then_inc(wt_copied, 1)
                        if s:
                            hidden_high(e, s - 1)
                        act.wait_ge(up_full, e * 16 + (s + 1))
                        act.activation(SIL[:, h, :], PS[:, 2 * h, 0:HALF], ACT.Silu).then_inc(sil_ready, 1)
                        for i, u, us in units(e):
                            if s == 3 * i + 1:
                                quant_scalar(u, RAW[us], UA, US)
                    if isinstance(e, int) and e == 0 and m == FM // 2:
                        for half in range(2):
                            act.wait_ge(cm_full, half + 1)
                            act.activation(CBT[:, half * HALF:(half + 1) * HALF], PS[0:E, 5 + half, 0:HALF],
                                           ACT.Copy).then_inc(cm_read, 1)
                hidden_high(e, 2 * FM - 1)
                for m in range(KD):
                    if not (isinstance(e, int) and e == E and m == KD - 1):
                        chunk_high(e, FM + m + 1)

            experts(act, expert_scalar)
            ln_scalar(act, 2)
            for which, raw in enumerate((QS, R)):
                for h in range(2):
                    for m in range(KD):
                        act.wait_ge(q_full, 2 * KD + 8 * which + h * KD + m + 1)
                        act.activation(raw[:, m, h * HALF:(h + 1) * HALF], PS[:, 2 * m + h, 0:HALF],
                                       ACT.Copy).then_inc(qk_read, 1)
            for b in range(B):
                act.wait_ge(v1_full, b + 1)
                act.activation(VV[:, b, :], PS[0:L, b, :], ACT.Copy).then_inc(v1_read, 1)
            act.sem_inc(p1_free, 2)
            act.sem_inc(ot_free, 1)

            def attn1_scalar(b, prev, old, e):
                if old is not None:
                    act.wait_ge(ot_full, old + 1)
                    act.activation(AO[:, :, bass.ds(old * L, L)], PS[:, 7, 0:KD * L].rearrange("p (c q) -> p c q", c=KD),
                                   ACT.Copy).then_inc(ot_free, 1)
                if prev is not None:
                    for c in range(KD):
                        act.wait_ge(p1_full, prev * 4 + (c + 1))
                        act.activation(PT1[:, 4 * c:4 * c + 4, :], PS[0:L, 4 + c % 2, 0:4 * L].rearrange(
                            "p (r q) -> p r q", r=4), ACT.Copy).then_inc(p1_free, 1)
                if b is not None:
                    act.wait_ge(sc_dve, b * 2 + 2)
                    act.activation(SM[e], SM[e], ACT.Exp, scale=float(DH) ** -0.5).then_inc(sc_exp, 1)

            batches3(act, attn1_scalar)
            ln_scalar(act, 3)
            def keys_scalar(b, e, g, bank):
                if g < 2 * KD:
                    m, half = g // 2, g % 2
                    act.wait_ge(kv_full, b * NKV + (g + 1))
                    act.activation(KX[e][:, m, half * SH:(half + 1) * SH], PS[:, bank, 0:SH], ACT.Identity,
                                   bias=col("bk", m)).then_inc(k_read, 1)

            for g in range(NKV):
                keys_scalar(0, 0, g, g % 8)
            act.sem_inc(x_free, 2)

            def xattn_scalar(b, prev, nxt, e):
                for s in range(H1 + 2):
                    if b is not None and s < H1:
                        act.wait_ge(nmx, b * H1 + (s + 1))
                        wait(act, ptx_free, b * (2 * H1) + 2 * s)
                        act.activation(PX[s % 2][:, 0:S].rearrange("p (a s) -> p a s", a=2),
                                       PS[0:L, 2 * (s % 2):2 * (s % 2) + 2, 0:SH], ACT.Exp, bias=SX[e][:, 0, s:s + 1],
                                       accum_out=SX[e][:, 1, s:s + 1]).then_inc(x_free, 1)
                    if prev is not None and s == 2:
                        act.wait_ge(otx_full, prev + 1)
                        act.activation(AO2[:, :, bass.ds(prev * L, L)], PS[:, 7, 0:KD * L].rearrange(
                            "p (c q) -> p c q", c=KD), ACT.Copy).then_inc(otx_free, 1)
                    if nxt is not None and s in GROUP_AT:
                        keys_scalar(nxt, 1 - e, GROUP_AT[s], 7)

            xbatches(act, xattn_scalar)
            for h in range(2):
                for m in range(2 * KD):
                    g = h * 2 * KD + m
                    act.wait_ge(mx_full, g + 1)
                    act.activation(HX[:, m, h * HALF:(h + 1) * HALF], PS[:, g % 8, 0:HALF], ACT.Relu,
                                   bias=col("b1", m)).then_inc(mx_free, 1)
            ln_scalar(act, 4)
            act.sem_inc(hq_read, 1)

            def ffn_scalar(a, g, d, l, piece, e):
                if a is not None:
                    act.wait_ge(xk_full, a + 1)
                    act.activation(XK[:, bass.ds(a, 1), :], PS[:, 6:7, :], ACT.Copy).then_inc(xk_read, 1)

                def hidden(p):
                    if d is not None:
                        n = PARTS[p][1]
                        quant_scalar(piece + p, XN[p % 2][:, 0:n], AB[p % 2][:, 0:n], SG[p % 2][:, 0:n])

                def silu(p):
                    if g is not None:
                        n = PARTS[p][1]
                        act.wait_ge(gu_full, g * 3 + (p + 1))
                        wait(act, gu_free, g * 3 + p - 1 if not isinstance(g, int) or 3 * g + p > 1 else 0)
                        act.activation(SI[:, p % 2, 0:n], PS[:, 2 * p, 0:n], ACT.Silu).then_inc(si_ready, 1)

                def transposed(p):
                    if d is not None:
                        c0, n = PARTS[p]
                        act.wait_ge(hq_full, d * 3 + (p + 1))
                        act.activation(HQT[:, c0 // P:(c0 + n) // P, :], PS[:, 6, 0:n].rearrange("p (i q) -> p i q", q=P),
                                       ACT.Copy).then_inc(hq_read, 1)

                hidden(0)
                hidden(1)
                if l is not None:
                    act.wait_ge(f_dve, l * 5 + 3)
                    act.activation(YS, YR[e], ACT.Square, accum_out=LS[e][:, 2:3]).then_inc(f_var, 1)
                    act.wait_ge(f_var, l * 2 + 1)
                    act.activation(LS[e][:, 3:4], LS[e][:, 2:3], ACT.Sqrt, scale=1.0 / D,
                                   bias=eps_c[:, 0:1]).then_inc(f_var, 1)
                silu(0)
                hidden(2)
                silu(1)
                silu(2)
                transposed(0)
                transposed(1)
                transposed(2)
                if a is not None:
                    quant_scalar(piece + (0 if d is None else 3), XN[1], AB[1], SG[1])
                if a is not None:
                    act.wait_ge(xq_full, a + 1)
                    act.activation(XQT[1 - e], PS[:, 6, :].rearrange("p (k q) -> p k q", k=KD), ACT.Copy).then_inc(xq_read, 1)

            tiles(act, ffn_scalar)

        @block.gpsimd
        def _(pool):
            pool.memset(eps_c[:, :], LN_EPS)
            pool.memset(ZERO, 0.0).then_inc(zero_ready, 1)
            pool.wait_ge(sp_dve, 3 * KD + 3)
            with pool.Fori(0, N // 2) as pair:
                n = pair * 2
                for e in range(2):
                    pool.wait_ge(s_bc[e], n * 16 + 32)
                    for c in range(KD):
                        pool.wait_ge(w_done, n * KD + (e * KD + c + 1))
                        pool.tensor_tensor(U[:, c % 2, :], XS[:, c, :], BC[:, e, 0, :], ALU.mult).then_inc(u_ready, 1)
            pool.wait_ge(tv_free, B * 4 + 2)
            pool.wait_ge(ln_out, 4)
            pool.memset(ONE, 1.0).then_inc(one_ready, 1)
            pool.sem_inc(acc, 4)

            def quant_pool(piece, n, sign, scale, signed):
                pool.wait_ge(q_sign, piece + 1)
                pool.tensor_tensor(signed[:, 0:n].rearrange("p (b i) -> p b i", i=16), sign[:, 0:n].rearrange("p (b i) -> p b i", i=16),
                                   scale[:, 0:n // 16].unsqueeze(2).to_broadcast([P, n // 16, 16]), ALU.mult).then_inc(q_ss, 1)

            def chunk_low(e, c):
                pool.wait_ge(ck_high, e * CHUNKS + (c + 1))
                pool.tensor_tensor(CL[c % 2], CR[c % 3].rearrange("p (j o) -> p j o", o=P), CH[c % 2].bitcast(F32),
                                   ALU.subtract).then_inc(ck_low, 1)

            def hidden_low(e, s):
                pool.wait_ge(hh_high, e * 16 + (s + 1))
                pool.tensor_tensor(HHL[s % 2][:, s // 2, :], HT[:, s % 2, :], HHH[s % 2][:, s // 2, :].bitcast(F32),
                                   ALU.subtract).then_inc(hh_low, 1)

            def expert_pool(e, slot):
                for m in range(FM):
                    for h in range(2):
                        s = 2 * m + h
                        if h == 0:
                            chunk_low(e, m + 1)
                        if s:
                            hidden_low(e, s - 1)
                        for i, u, us in units(e):
                            if s == 3 * i + 2:
                                quant_pool(u, D, US, UC, US)
                hidden_low(e, 2 * FM - 1)
                for m in range(KD):
                    if not (isinstance(e, int) and e == E and m == KD - 1):
                        chunk_low(e, FM + m + 1)
                    for h in range(2):
                        t = 2 * m + h
                        rows = R[:, m, h * HALF:(h + 1) * HALF]
                        pool.wait_ge(dn_free, e * 8 + (t + 5))
                        pool.tensor_tensor(rows, rows, TMP[:, t % 4, :], ALU.add).then_inc(acc, 1)

            chunk_low(0, 0)
            pool.wait_ge(r_copied, 1)
            experts(pool, expert_pool)
            pool.wait_ge(acc, 8 * (E + 1) + 4)
            pool.sem_inc(ln_in, 2)
            pool.wait_ge(rot, 6)

            def attn1_pool(b, prev, old, e):
                if b is not None:
                    pool.wait_ge(sc_read, b + 1)
                    pool.tensor_copy(QB[e], QR[:, :, bass.ds(b * L, L)]).then_inc(qkb, 1)
                    pool.tensor_copy(KB[e], KR[:, :, bass.ds(b * L, L)]).then_inc(qkb, 1)

            batches3(pool, attn1_pool)
            pool.wait_ge(o_full, 2 * KD + 2 * KD)
            for e in range(2):
                pool.memset(PX[e][:, S:SJ * P], 0.0).then_inc(pad_ready, 1)
            pool.wait_ge(qx_read, 2 * KD)

            def xattn_pool(b, prev, nxt, e):
                if b is not None:
                    if not isinstance(b, int) or b:
                        pool.wait_ge(x_free, b * H1 - (H1 - 2))
                    pool.tensor_copy(QBX[e], QX[:, :, bass.ds(b * L, L)]).then_inc(qbx, 1)

            xbatches(pool, xattn_pool)
            pool.wait_ge(ln_out, 9)

            def ffn_pool(a, g, d, l, piece, e):
                if a is not None:
                    if isinstance(a, int) and a == 2:
                        pool.wait_ge(ln_out, 10)
                    if g is not None:
                        pool.wait_ge(xk_full, g + 1)
                    if isinstance(a, int) and a == NT - 1:
                        pool.memset(XB[1 - e][:, :, T - a * P:P], 0.0).then_inc(pad_ready, 1)
                        pool.wait_ge(pad_ready, 3)
                        pool.tensor_copy(XB[1 - e][:, :, 0:T - a * P], XT[:, :, a * P:T]).then_inc(xb_ready, 1)
                    else:
                        pool.tensor_copy(XB[1 - e], XT[:, :, bass.ds(a * P, P)]).then_inc(xb_ready, 1)
                if d is not None:
                    for p, (c0, n) in enumerate(PARTS):
                        quant_pool(piece + p, n, SG[p % 2], SCL[p % 2], SS[p % 2])
                if a is not None:
                    quant_pool(piece + (0 if d is None else 3), D, SG[1], SCL[1], SS[1])

            tiles(pool, ffn_pool)

        @block.vector
        def _(v):
            def link(ins):
                dve.inc(ins)
                v.wait_ge(dve.sem, dve.n)

            v.wait_ge(s_x, 16)
            v.wait_ge(s_wa, 96)
            link(v.reduce_sum(GC, XT[:, :, :].rearrange("p k (b t) -> p (k b) t", b=B), AX))
            link(v.tensor_copy(CUR8, sm[:, 2:3].to_broadcast([N, B])))
            v.tensor_scalar(GC, GC, 1.0 / L, None, ALU.mult).then_inc(gc_ready, 1)
            link(v.tensor_scalar(TAU[:, 0:1], sm[:, 1:2], 0.1, 10.0, ALU.max, ALU.min))
            link(v.reciprocal(TAU[:, 1:2], TAU[:, 0:1]))
            v.wait_ge(gate_act, 1)
            link(v.tensor_tensor(TH, TH, CUR8, ALU.subtract))
            link(v.tensor_scalar(TH, TH, TAU[:, 1:2], 0.1, ALU.mult, ALU.mult))
            v.tensor_tensor(H8, TH, CUR8, ALU.add).then_inc(newh_ready, 1)
            v.wait_ge(gate_act, 1 + KD)
            for c in range(KD):
                last = v.tensor_tensor(XS[:, c, :].rearrange("p (b t) -> p b t", b=B),
                                       XT[:, c, :].rearrange("p (b t) -> p b t", b=B),
                                       SEL[:, c, :].unsqueeze(2).to_broadcast([P, B, L]), ALU.mult)
            last.then_inc(xs_ready, 1)
            v.wait_ge(s_consts, 64)
            v.wait_ge(a_ready, 1)
            link(v.tensor_scalar(KEEP, AA, TINY_A, None, ALU.is_ge))
            link(v.tensor_scalar(TINY, KEEP, -1.0, 1.0, ALU.mult, ALU.add))
            link(v.tensor_scalar(AA, AA, -1.0, None, ALU.mult))
            link(v.tensor_tensor(INV, AA, KEEP, ALU.mult))
            link(v.tensor_tensor(INV, INV, TINY, ALU.add))
            link(v.reciprocal(INV, INV))
            link(v.tensor_tensor(DB, vec[:, VEC["delta_b"][0]:VEC["delta_b"][0] + KD],
                                 vec[:, VEC["dt_bias"][0]:VEC["dt_bias"][0] + KD], ALU.add))
            v.reduce_sum(CNT[:, 0:1], TINY.rearrange("p k n -> p (k n)"), AX).then_inc(inv_ready, 1)
            v.wait_ge(tiny_sum, 1)
            v.tensor_scalar(FLAG[:, :], PS[:, 1, 64:65], 0.0, None, ALU.is_gt).then_inc(flag_read, 1)
            v.wait_ge(flag_read, 1)
            any_tiny = v.value_load(FLAG[0:1, 0:1])
            def one_plus(m):
                v.wait_ge(sp_act, m + 1)
                v.tensor_scalar(SP2[:, m, :], SP1[:, m, :], 1.0, None, ALU.add).then_inc(sp_dve, 1)
                v.wait_ge(sp_dve, sp_step(m))
                v.scalar_tensor_tensor(SP1[:, m, :], SP2[:, m, :], -1.0, SP1[:, m, :], ALU.add, ALU.subtract).then_inc(sp_dve, 1)

            for m in range(KD):
                v.wait_ge(proj_ev, 2 * m + 4)
                v.scalar_tensor_tensor(SP1[:, m, :], DL[:, m, :], -1.0, DL[:, m, :], ALU.mult, ALU.min).then_inc(sp_dve, 1)
                if m:
                    one_plus(m - 1)
            one_plus(KD - 1)
            v.wait_ge(sp_dve, 3 * KD)
            v.wait_ge(sp_act, KD + 2)
            v.tensor_tensor(SP1, SP1, SP2, ALU.mult).then_inc(sp_dve, 1)
            v.wait_ge(sp_dve, 3 * KD + 1)
            v.scalar_tensor_tensor(DL, DL, 0.0, SP1, ALU.max, ALU.subtract).then_inc(sp_dve, 1)
            v.wait_ge(sp_dve, 3 * KD + 2)
            v.tensor_tensor(DL, DL, SP3, ALU.add).then_inc(sp_dve, 1)
            v.wait_ge(sp_dve, 3 * KD + 3)
            v.sem_inc(ad_free, 2)
            v.sem_inc(w_done, 2)

            def run_scan(t, r):
                v.wait_ge(w_done, t + 2)
                v.memset(AD[:, r, 0:T:L], 0.0).then_inc(rz, 1)
                v.wait_ge(v_used, t)
                v.wait_ge(rz, t)
                v.tensor_tensor_scan(HS[:, r, :], AD[:, r, :], W[:, r, :], 0.0, ALU.mult, ALU.add).then_inc(ad_free, 1)

            def output(t, r, state, c, e):
                v.wait_ge(ad_free, t + 2)
                v.scalar_tensor_tensor(V[:, r, :], HS[:, r, :], INV[:, c, bass.ds(state, 1)], BC[:, e, 1, :],
                                       ALU.mult, ALU.mult).then_inc(v_ready, 1)

            with v.If(any_tiny > 0):
                with v.Fori(0, N // 2) as pair:
                    for i in range(2 * KD):
                        t, r, c, state = pair * (2 * KD) + (i + 1), i % 2, i % KD, pair * 2 + i // KD
                        v.wait_ge(ad_ready, t)
                        v.nop()
                        v.wait_ge(u_ready, t)
                        v.nop()
                        v.wait_ge(v_used, t)
                        v.nop()
                        v.tensor_scalar(HS[:, r, :], AD[:, r, :], -1.0, KEEP[:, c, bass.ds(state, 1)],
                                        ALU.add, ALU.mult).then_inc(tiny_s, 1)
                        v.wait_ge(tiny_s, 2 * t - 1)
                        v.nop()
                        v.scalar_tensor_tensor(HS[:, r, :], DL[:, c, :], TINY[:, c, bass.ds(state, 1)],
                                               HS[:, r, :], ALU.mult, ALU.add).then_inc(tiny_s, 1)
                        v.wait_ge(tiny_s, 2 * t)
                        v.tensor_tensor(W[:, r, :], HS[:, r, :], U[:, r, :], ALU.mult).then_inc(w_done, 1)
                        run_scan(t, r)
                        output(t, r, state, c, i // KD)
            with v.Else():
                with v.Fori(0, N // 2) as pair:
                    def weighted_input(i):
                        t, r = pair * (2 * KD) + (i + 1), i % 2
                        v.wait_ge(ad_ready, t)
                        v.wait_ge(u_ready, t)
                        v.scalar_tensor_tensor(W[:, r, :], AD[:, r, :], -1.0, U[:, r, :], ALU.add, ALU.mult).then_inc(w_done, 1)

                    weighted_input(0)
                    for i in range(2 * KD):
                        t, r, c, state = pair * (2 * KD) + (i + 1), i % 2, i % KD, pair * 2 + i // KD
                        run_scan(t, r)
                        if i + 1 < 2 * KD:
                            weighted_input(i + 1)
                        output(t, r, state, c, i // KD)
            v.wait_ge(y_ready, 1)
            for h in range(2):
                part = slice(h * HALF, (h + 1) * HALF)
                v.tensor_tensor(R[:, :, part], XT[:, :, part], PS[:, h:8:2, 0:HALF], ALU.add).then_inc(ln_in, 1)
            ln_vector(v, 0)
            v.sem_inc(pt_free, 2)

            def qk_vector(b, prev, e):
                def norm(h):
                    v.wait_ge(s_free, b * 6 + (h + 5))
                    v.reciprocal(ST[e][:, 2, h:h + 1], ST[e][:, 1, h:h + 1]).then_inc(rs_ready, 1)
                    v.wait_ge(rs_ready, b * H0 + (h + 1))
                    v.tensor_scalar(PR[e][:, h, :], PR[e][:, h, :], ST[e][:, 2, h:h + 1], None, ALU.mult)\
                        .then_inc(pr_ready, 1)

                for h in range(H0):
                    if b is not None:
                        v.wait_ge(s_full, b * 6 + (h + 3))
                        v.tensor_reduce(ST[e][:, 0, h:h + 1], PS[0:L, 2 * (h % 2):2 * (h % 2) + 2, 0:SH],
                                        mybir.AxisListType.XY, ALU.max, negate=True).then_inc(nm_ready, 1)
                        if h:
                            norm(h - 1)
                    if prev is not None and h < 3:
                        for j in range(2 * h, 2 * h + 2):
                            v.wait_ge(pt_full, prev * SJ + (j + 1))
                            v.tensor_copy(PT[0:width(j), j, :], PS[0:width(j), 4 + j % 2, 0:H0 * L]).then_inc(pt_free, 1)
                if b is not None:
                    norm(H0 - 1)

            batches(v, qk_vector)
            for h in range(2):
                part = slice(h * HALF, (h + 1) * HALF)
                for m in range(KD):
                    v.wait_ge(o_full, h * KD + m + 1)
                    last = v.scalar_tensor_tensor(R[:, m, part], PS[:, 2 * m + h, 0:HALF], col("bo", m), XT[:, m, part],
                                                  ALU.add, ALU.add)
                last.then_inc(ln_in, 1)
            ln_vector(v, 1)
            def spread(x):
                return x.unsqueeze(2).to_broadcast([L, B, E])

            def biases(x):
                return x[0:L, :].unsqueeze(1).to_broadcast([L, B, E])

            for h in range(2):
                part = slice(h * HALF, (h + 1) * HALF)
                v.wait_ge(x_high, h + 1)
                v.tensor_tensor(XL[:, :, part], XT[:, :, part], XH[:, :, part].bitcast(F32), ALU.subtract).then_inc(x_low, 1)
            v.tensor_copy(R[:, :, :], XT[:, :, :]).then_inc(r_copied, 1)
            v.wait_ge(lg_full, 1)
            v.wait_ge(s_gw, 48)
            logits = PS[0:L, 4, 0:B * E].rearrange("p (b e) -> p b e", b=B)
            link(v.reduce_max(GS[:, 0, :], logits, AX))
            v.tensor_tensor(SC, logits, spread(GS[:, 0, :]), ALU.subtract).then_inc(rt_dve, 1)
            v.wait_ge(rt_exp, 1)
            link(v.reduce_sum(GS[:, 1, :], SC, AX))
            link(v.reciprocal(GS[:, 1, :], GS[:, 1, :]))
            link(v.tensor_tensor(SC, SC, spread(GS[:, 1, :]), ALU.mult))
            link(v.tensor_tensor(BI, SC, biases(gb), ALU.add))
            for best in range(2):
                link(v.reduce_max(GS[:, 2, :], BI, AX))
                link(v.tensor_tensor(KEY, BI, spread(GS[:, 2, :]), ALU.is_equal))
                link(v.tensor_tensor(KEY, KEY, biases(rank), ALU.mult))
                link(v.reduce_max(GS[:, 3, :], KEY, AX))
                link(v.tensor_tensor(OH, KEY, spread(GS[:, 3, :]), ALU.is_equal))
                if best == 0:
                    link(v.tensor_copy(CM, OH))
                    link(v.scalar_tensor_tensor(BI, OH, NEG, BI, ALU.mult, ALU.add))
            link(v.tensor_tensor(CM, CM, OH, ALU.add))
            v.tensor_tensor(CM, CM, SC, ALU.mult).then_inc(rt_dve, 1)
            v.sem_inc(up_free, 2)
            v.sem_inc(dn_free, 4)

            def quant_vector(piece, src, dst, n, places, part, behind=0):
                scaled, magnitude, signed, low, high, largest, scale, rscale = places

                def blocks(x):
                    return x.rearrange("p (b i) -> p b i", i=16)

                def step(j, ins):
                    ins.then_inc(q_scale if j < 3 else q_steps, 1)

                def after(j):
                    if j < 3:
                        v.wait_ge(q_scale, piece * 3 + (j + 1))
                    else:
                        v.wait_ge(q_steps, piece * 8 + (j - 2))

                nb, ab, qg, qh = n // 16, magnitude[:, 0:n], low[:, 0:n], high[:, 0:n]
                am, sc, ri = largest[:, 0:nb], scale[:, 0:nb], rscale[:, 0:nb]
                if part == 0:
                    if not isinstance(piece, int) or piece:
                        v.wait_ge(q_done, piece - behind)
                    step(0, v.tensor_reduce(am, blocks(src), AX, ALU.max, apply_absolute_value=True))
                    after(0)
                    step(1, v.tensor_scalar(sc, am, 1.0 / 6.0, 1e-12, ALU.mult, ALU.max))
                    after(1)
                    step(2, v.reciprocal(ri, sc))
                    after(2)
                    v.tensor_tensor(blocks(scaled[:, 0:n]), blocks(src), ri.unsqueeze(2).to_broadcast([P, nb, 16]), ALU.mult)\
                        .then_inc(q_scaled, 1)
                elif part == 1:
                    v.wait_ge(q_abs, piece + 1)
                    step(3, v.tensor_scalar(qg, ab, 0.25, None, ALU.is_gt))
                    step(4, v.tensor_scalar(qh, ab, 5.0, 2.0, ALU.is_gt, ALU.mult))
                    after(3)
                    step(5, v.scalar_tensor_tensor(qg, ab, 0.75, qg, ALU.is_gt, ALU.add))
                    after(4)
                    step(6, v.scalar_tensor_tensor(qh, ab, 2.5, qh, ALU.is_gt, ALU.add))
                else:
                    after(5)
                    step(7, v.scalar_tensor_tensor(qg, ab, 1.25, qg, ALU.is_gt, ALU.add))
                    after(6)
                    step(8, v.scalar_tensor_tensor(qh, ab, 3.5, qh, ALU.is_gt, ALU.add))
                    after(7)
                    step(9, v.scalar_tensor_tensor(qg, ab, 1.75, qg, ALU.is_gt, ALU.add))
                    after(9)
                    step(10, v.scalar_tensor_tensor(qg, qh, 2.0, qg, ALU.mult, ALU.add))
                    after(10)
                    v.wait_ge(q_ss, piece + 1)
                    v.scalar_tensor_tensor(dst, qg, 0.5, signed[:, 0:n], ALU.mult, ALU.mult).then_inc(q_done, 1)

            def expert_vector(e, slot):
                for m in range(FM):
                    for h in range(2):
                        s = 2 * m + h
                        v.wait_ge(sil_ready, e * 16 + (s + 1))
                        if not isinstance(e, int) or e or s >= 2:
                            v.wait_ge(hh_low, e * 16 + (s - 1))
                        v.tensor_tensor(HT[:, h, :], PS[:, 2 * h + 1, 0:HALF], SIL[:, h, :], ALU.mult).then_inc(up_free, 1)
                        for i, u, us in units(e):
                            if s // 3 == i:
                                if s % 3 == 0:
                                    v.wait_ge(s_raw[us], ctx_loads(u, 16, us))
                                quant_vector(u, RAW[us], RAW[us], D, (RAW[us], UA, US, UG, UH, UM, UC, UR), s % 3)
                v.wait_ge(s_cb[slot], ctx_loads(e, 16, slot))
                for m in range(KD):
                    for h in range(2):
                        t = 2 * m + h
                        v.wait_ge(dn_full, e * 8 + (t + 1))
                        v.wait_ge(acc, e * 8 + (t + 1))
                        v.tensor_tensor(TMP[:, t % 4, :], PS[:, 4 + t % 4, 0:HALF], CB[slot][:, h * HALF:(h + 1) * HALF], ALU.mult)\
                            .then_inc(dn_free, 1)

            experts(v, expert_vector)
            ln_vector(v, 2)
            v.wait_ge(s_wd, 64)
            for which, (raw, out) in enumerate(((QS, QR), (R[:, :, :], KR))):
                v.wait_ge(qk_read, 8 * which + 8)
                v.tensor_tensor(out.rearrange("p m (b t) -> p (m b) t", t=L), raw.rearrange("p m (b t) -> p (m b) t", t=L),
                                rope[:, 0:L].unsqueeze(1).to_broadcast([P, KD * B, L]), ALU.mult).then_inc(rot, 1)
                v.wait_ge(pm_full, which + 1)
                v.wait_ge(rot, 3 * which + 1)
                v.tensor_tensor(SQ[:, :, :].rearrange("p m (h b t) -> p (m h) b t", h=2, t=L),
                                PS[:, :, 0:HALF].rearrange("p g (b t) -> p g b t", t=L),
                                rope[:, L:2 * L].unsqueeze(1).unsqueeze(1).to_broadcast([P, 2 * KD, B // 2, L]),
                                ALU.mult).then_inc(rot, 1)
                v.wait_ge(rot, 3 * which + 2)
                v.tensor_tensor(out, out, SQ[:, :, :], ALU.add).then_inc(rot, 1)
            v.sem_inc(sc_read, 2)
            v.wait_ge(s_wd2, 48)

            def attn1_vector(b, prev, old, e):
                if b is not None:
                    v.wait_ge(sc_full, b + 1)
                    v.tensor_tensor(SM[e].rearrange("p (r c) k -> p r c k", r=4),
                                    PS[0:L, 0:4, 0:4 * L].rearrange("p r (c k) -> p r c k", c=4),
                                    causal.unsqueeze(1).unsqueeze(1).to_broadcast([L, 4, 4, L]), ALU.add)\
                        .then_inc(sc_read, 1)
                    v.wait_ge(sc_read, b + 3)
                    v.reduce_max(S1[e][:, 0, :], SM[e], AX).then_inc(sc_dve, 1)
                    v.wait_ge(sc_dve, b * 2 + 1)
                    v.tensor_tensor(SM[e], SM[e], S1[e][:, 0, :].unsqueeze(2).to_broadcast([L, H1, L]), ALU.subtract)\
                        .then_inc(sc_dve, 1)
                if prev is not None:
                    v.wait_ge(pv_full, prev + 1)
                    if not isinstance(prev, int) or prev:
                        v.wait_ge(ot_full, prev)
                    v.tensor_tensor(ON.rearrange("p (c r d) -> p c r d", c=4, r=4),
                                    PS[0:L, 6, :].rearrange("p (c r d) -> p c r d", c=4, r=4),
                                    S1[1 - e][:, 2, :].rearrange("p (r c) -> p c r", r=4).unsqueeze(3).to_broadcast([L, 4, 4, DH]),
                                    ALU.mult).then_inc(on_ready, 1)
                if b is not None:
                    v.wait_ge(sc_exp, b + 1)
                    v.reduce_sum(S1[e][:, 1, :], SM[e], AX).then_inc(ri_ready, 1)
                    v.wait_ge(ri_ready, b * 2 + 1)
                    v.reciprocal(S1[e][:, 2, :], S1[e][:, 1, :]).then_inc(ri_ready, 1)
                    v.wait_ge(ri_ready, b * 2 + 2)

            batches3(v, attn1_vector)
            for h in range(2):
                part = slice(h * HALF, (h + 1) * HALF)
                for m in range(KD):
                    v.wait_ge(o_full, 2 * KD + h * KD + m + 1)
                    last = v.tensor_tensor(R[:, m, part], XT[:, m, part], PS[:, 2 * m + h, 0:HALF], ALU.add)
                last.then_inc(ln_in, 1)
            ln_vector(v, 3)
            def values_vector(b, e, g, bank):
                if g >= 2 * KD:
                    j = g - 2 * KD
                    v.wait_ge(kv_full, b * NKV + (g + 1))
                    v.tensor_tensor(VX[e][0:width(j), j, :], PS[0:width(j), bank, :], bvr[0:width(j), :], ALU.add)\
                        .then_inc(v_read, 1)

            v.wait_ge(s_wx, 64)
            for g in range(NKV):
                values_vector(0, 0, g, g % 8)
            for h in range(2):
                for m in range(KD):
                    v.wait_ge(q_full, 6 * KD + h * KD + m + 1)
                    v.tensor_scalar(QX[:, m, h * HALF:(h + 1) * HALF], PS[:, 2 * m + h, 0:HALF], col("bq", m),
                                    float(DH) ** -0.5, ALU.add, ALU.mult).then_inc(qx_read, 1)
            v.sem_inc(ptx_free, 2)

            def xattn_vector(b, prev, nxt, e):
                for s in range(H1 + 2):
                    if b is not None and s < H1:
                        v.wait_ge(x_full, b * H1 + (s + 1))
                        v.tensor_reduce(SX[e][:, 0, s:s + 1], PS[0:L, 2 * (s % 2):2 * (s % 2) + 2, 0:SH],
                                        mybir.AxisListType.XY, ALU.max, negate=True).then_inc(nmx, 1)
                    if nxt is not None and s in GROUP_AT:
                        values_vector(nxt, 1 - e, GROUP_AT[s], 7)
                    if b is not None and 1 <= s <= H1:
                        h = s - 1
                        for p in range(2):
                            v.wait_ge(ptx_full, b * (2 * H1) + (2 * h + p + 1))
                            v.tensor_copy(PTX[h % 2][:, 3 * p:3 * p + 3, :], PS[:, 4 + p, 0:3 * L].rearrange(
                                "p (j q) -> p j q", j=3)).then_inc(ptx_free, 1)
                if b is not None:
                    v.wait_ge(x_free, b * H1 + (H1 + 2))
                    v.reciprocal(SX[e][:, 2, :], SX[e][:, 1, :]).then_inc(rix, 1)
                    v.wait_ge(rix, b + 1)
                    v.wait_ge(ox_full, b + 1)
                    v.tensor_tensor(OX[e].rearrange("p (h d) -> p h d", h=H1),
                                    PS[0:L, 6, :].rearrange("p (h d) -> p h d", h=H1),
                                    SX[e][:, 2, :].unsqueeze(2).to_broadcast([L, H1, DH]), ALU.mult).then_inc(ox_norm, 1)

            xbatches(v, xattn_vector)
            for h in range(2):
                part = slice(h * HALF, (h + 1) * HALF)
                for m in range(KD):
                    v.wait_ge(o_full, 4 * KD + h * KD + m + 1)
                    last = v.scalar_tensor_tensor(R[:, m, part], PS[:, 2 * m + h, 0:HALF], col("b2", m), XT[:, m, part],
                                                  ALU.add, ALU.add)
                last.then_inc(ln_in, 1)
            ln_vector(v, 4)
            places = [(XN[q], AB[q], SS[q], QG[q], QH[q], AM[q], SCL[q], RI[q]) for q in range(2)]

            def ffn_vector(a, g, d, l, piece, e):
                def hidden(p, parts):
                    if d is None:
                        return
                    c0, n = PARTS[p]
                    if p == 0 and 0 in parts:
                        v.wait_ge(gu_free, d * 3 + 3)
                        v.wait_ge(hq_read, d * 3 + 1)
                    for part in parts:
                        quant_vector(piece + p, HB[1 - e][:, c0:c0 + n], HQ[:, c0:c0 + n], n, places[p % 2], part, int(p > 0))

                def gated(p):
                    if g is not None:
                        c0, n = PARTS[p]
                        v.wait_ge(si_ready, g * 3 + (p + 1))
                        v.tensor_tensor(HB[e][:, c0:c0 + n], PS[:, 2 * p + 1, 0:n], SI[:, p % 2, 0:n], ALU.mult)\
                            .then_inc(gu_free, 1)

                def stream(parts):
                    if a is None:
                        return
                    if 0 in parts:
                        v.wait_ge(xk_read, a + 1)
                    elif g is not None:
                        v.wait_ge(xq_read, g + 1)
                    for part in parts:
                        quant_vector(piece + (0 if d is None else 3), XK[:, bass.ds(a, 1), :].rearrange("p a d -> p (a d)"),
                                     XQ, D, places[1], part, int(d is not None))

                hidden(0, [0])
                hidden(1, [0])
                hidden(0, [1, 2])
                if l is not None:
                    y, s = YR[e], LS[e]
                    v.wait_ge(y_full, l + 1)
                    v.wait_ge(s_tile[e], tile_stored(l, e))
                    v.tensor_tensor(y, PS[:, 7, :], XK[:, bass.ds(l, 1), :].rearrange("p a d -> p (a d)"), ALU.add).then_inc(f_sum, 1)
                    v.wait_ge(f_sum, l + 2)
                    v.reduce_sum(s[:, 0:1], y, AX).then_inc(f_dve, 1)
                    v.wait_ge(f_dve, l * 5 + 1)
                    v.tensor_scalar(s[:, 1:2], s[:, 0:1], 1.0 / D, None, ALU.mult).then_inc(f_dve, 1)
                    v.wait_ge(f_dve, l * 5 + 2)
                    v.tensor_scalar(y, y, s[:, 1:2], None, ALU.subtract).then_inc(f_dve, 1)
                hidden(2, [0])
                hidden(1, [1, 2])
                if l is not None:
                    v.wait_ge(f_var, l * 2 + 2)
                    v.reciprocal(s[:, 4:5], s[:, 3:4]).then_inc(f_dve, 1)
                    v.wait_ge(f_dve, l * 5 + 4)
                    v.tensor_scalar(y, y, s[:, 4:5], None, ALU.mult).then_inc(f_dve, 1)
                gated(0)
                hidden(2, [1, 2])
                gated(1)
                stream([0])
                gated(2)
                stream([1, 2])

            def tile_stored(d, e):
                return d * 8 - 8 * e + 16

            v.sem_inc(f_sum, 1)
            tiles(v, ffn_vector)


def columns(v):
    return np.asarray(v).reshape(-1, P).T


def expert_chunks(w1, w3, w2):
    up = np.stack([w1, w3], axis=1).reshape(E + 1, 2, FM, P, KD, P).transpose(0, 2, 5, 1, 4, 3)
    down = w2.reshape(E + 1, KD, P, FM, P).transpose(0, 1, 4, 3, 2)
    return np.concatenate([up.reshape(E + 1, FM, P, CHUNK), down.reshape(E + 1, KD, P, CHUNK)], axis=1)


def layouts(x, ctx_768, L0_attn_delta_W, L0_attn_delta_b, L0_attn_B_W, L0_attn_B_b, L0_attn_C_W, L0_attn_C_b,
            L0_attn_A_log, L0_attn_dt_bias, L0_attn_tau, L0_attn_Wi_W, L0_attn_Wi_b, L0_attn_Wr_W, L0_attn_sel_W,
            L0_attn_sel_b, L0_attn_h0, L0_xattn_Wq, L0_xattn_Wk, L0_xattn_Wv, L0_xattn_Wo, L0_xattn_bo,
            L0_ffn_gate_w, L0_ffn_gate_bias, L0_ffn_w1, L0_ffn_w2, L0_ffn_w3, L0_ffn_sw1, L0_ffn_sw2, L0_ffn_sw3,
            L1_attn_Wq, L1_attn_Wk, L1_attn_Wv, L1_attn_Wo, L1_xattn_Wq, L1_xattn_bq, L1_xattn_Wk, L1_xattn_bk,
            L1_xattn_Wv, L1_xattn_bv, L1_xattn_W1, L1_xattn_b1, L1_xattn_W2, L1_xattn_b2, L1_ffn_w_gate,
            L1_ffn_w_up, L1_ffn_w_down):
    inv = (np.float32(1.0) / np.float32(10000.0) ** (np.arange(0, DH, 2, dtype=np.float32) / np.float32(DH))).astype(np.float32)
    freqs = np.arange(L, dtype=np.float32)[:, None] * inv[None, :]
    pair = (np.arange(P) % DH) // 2
    rope = np.concatenate([np.cos(freqs).astype(np.float32).T[pair], np.sin(freqs).astype(np.float32).T[pair]], axis=1)
    perm = np.zeros((P, P), np.float32)
    perm[np.arange(1, P, 2), np.arange(0, P, 2)] = -1.0
    perm[np.arange(0, P, 2), np.arange(1, P, 2)] = 1.0
    mask = np.triu(np.full((L, L), NEG, np.float32), k=1)
    return [
        ("xT", x.reshape(T, D).T),
        ("vecs", np.concatenate([columns(v) for v in (L0_attn_delta_b, L0_attn_dt_bias, L0_attn_sel_b, L0_xattn_bo,
                                                      L1_xattn_bq, L1_xattn_bk, L1_xattn_b1, L1_xattn_b2)], axis=1)),
        ("small16", np.stack([L0_attn_Wi_b, L0_attn_tau, L0_attn_h0[0]], axis=1)),
        ("bcb", np.concatenate([L0_attn_B_b, L0_attn_C_b])[:, None]),
        ("alog", L0_attn_A_log),
        ("ident", np.eye(P, dtype=np.float32)),
        ("mean_w", np.full((P, P), 1.0 / D, np.float32)),
        ("rope", rope), ("perm", perm), ("causal", mask),
        ("wiT", L0_attn_Wi_W.T), ("wrT", L0_attn_Wr_W.T), ("selT", L0_attn_sel_W.T),
        ("bcT", np.concatenate([L0_attn_B_W, L0_attn_C_W]).T), ("dwT", L0_attn_delta_W.T),
        ("ctxT", ctx_768.transpose(0, 2, 1)), ("ctxN", ctx_768),
        ("wq0T", L0_xattn_Wq.T), ("wk0", L0_xattn_Wk), ("wv0T", L0_xattn_Wv.T), ("wo0T", L0_xattn_Wo.T),
        ("gateT", L0_ffn_gate_w.T), ("gate_bias", np.concatenate([L0_ffn_gate_bias, np.arange(E, 0, -1, dtype=np.float32)])[None, :]),
        ("wc", expert_chunks(np.concatenate([L0_ffn_w1, L0_ffn_sw1[None]]), np.concatenate([L0_ffn_w3, L0_ffn_sw3[None]]),
                             np.concatenate([L0_ffn_w2, L0_ffn_sw2[None]]))),
        ("wq1T", L1_attn_Wq.T), ("wk1T", L1_attn_Wk.T), ("wv1T", L1_attn_Wv.T), ("wo1T", L1_attn_Wo.T),
        ("xq1", L1_xattn_Wq), ("xk1", L1_xattn_Wk), ("xv1", L1_xattn_Wv), ("bv1", L1_xattn_bv[None, :]),
        ("xw1", L1_xattn_W1), ("xw2", L1_xattn_W2),
        ("wf", np.concatenate([w.reshape(-1, P, w.shape[1]).transpose(1, 0, 2).reshape(P, -1)
                               for w in (L1_ffn_w_gate, L1_ffn_w_up, L1_ffn_w_down)], axis=1)),
    ]


def kernel(**inputs):
    import concourse.bacc as bacc
    from concourse.bass_utils import run_bass_kernel_spmd

    nc = bacc.Bacc("TRN2", target_bir_lowering=False, num_devices=1)
    arrays, args = {}, []
    for name, a in layouts(**{k: np.asarray(v) for k, v in inputs.items()}):
        name = "in_" + name
        arrays[name] = np.ascontiguousarray(a)
        args.append(nc.dram_tensor(name, arrays[name].shape, mybir.dt.from_np(arrays[name].dtype),
                                   kind="ExternalInput").ap())
    args.append(nc.dram_tensor("out", (T, D), F32, kind="ExternalOutput").ap())
    program(nc, *args)
    got = run_bass_kernel_spmd(nc, [arrays], core_ids=[0]).results[0]["out"]
    return np.ascontiguousarray(got).reshape(B, L, D)
```
